# Optimizing a Trainium2 kernel written in Bass

```python
import numpy as np
import jax
import jax.numpy as jnp

def _softmax(x, axis=-1):
    return jax.nn.softmax(x, axis=axis)

def _gelu(x):
    return jax.nn.gelu(x, approximate=True)

def _silu(x):
    return jax.nn.silu(x)

def _sigmoid(x):
    return jax.nn.sigmoid(x)

def _layernorm(x, axis=-1, eps=1e-05):
    m = jnp.mean(x, axis=axis, keepdims=True)
    v = jnp.var(x, axis=axis, keepdims=True)
    return (x - m) / jnp.sqrt(v + eps)

def _scatter_add(tgt, idx, src, axis=0):
    return tgt.at[idx].add(src)

def _segment_sum(src, seg, n):
    return jax.ops.segment_sum(src, seg, n)
kernel_name = 'mk_vit_tower_d2_tok_img1024_r4_d17c4e'

def setup_inputs(seed: int=0):
    np.random.seed(seed)
    _w = jnp.asarray

    def _rec_inputs():
        import jax
        import jax.numpy as jnp
        _rk = jax.random.key(seed)
        x = -0.00016672 + 0.999947 * jax.random.normal(jax.random.fold_in(_rk, 1), (16, 3, 96, 96), jnp.float32)
        return x
    x = _rec_inputs()

    def _L0_tok_setup():
        import jax, jax.numpy as jnp
        import numpy as np
        IMG = 96
        PATCH = 16
        C_IN = 3
        EMBED = 256
        NPH = IMG // PATCH
        NUM_PATCHES = NPH * NPH
        PATCH_DIM = PATCH * PATCH * C_IN
        key = jax.random.key(seed)
        k_x, k_w, k_b, k_cls, k_pos = jax.random.split(key, 5)
        x = jax.random.normal(k_x, (64, C_IN, IMG, IMG), dtype=jnp.float32)
        W = jax.random.normal(k_w, (EMBED, PATCH_DIM), dtype=jnp.float32) * (1.0 / np.sqrt(PATCH_DIM))
        b = jax.random.normal(k_b, (EMBED,), dtype=jnp.float32) * 0.01
        cls_token = jax.random.normal(k_cls, (1, 1, EMBED), dtype=jnp.float32) * 0.02
        pos_embed = jax.random.normal(k_pos, (1, NUM_PATCHES + 1, EMBED), dtype=jnp.float32) * 0.02
        return {'x': x, 'W': W, 'b': b, 'cls_token': cls_token, 'pos_embed': pos_embed}
    _L0_tok_all = _L0_tok_setup()
    _L0_tok_in = {k: v for k, v in _L0_tok_all.items() if k in ('W', 'b', 'cls_token', 'pos_embed')}
    del _L0_tok_all

    def _L0_attn_setup():
        import jax, jax.numpy as jnp
        import numpy as np
        N_EMBD = 256
        N_HEAD = 16
        HEAD_DIM = N_EMBD // N_HEAD
        KV_RANK = 64
        Q_RANK = 128
        ROPE_DIM = 32
        B, T = (2, 512)
        EPS = 1e-06

        def _rope_tables(T, dim):
            inv_freq = 1.0 / 10000.0 ** (np.arange(0, dim, 2, dtype=np.float32) / dim)
            t = np.arange(T, dtype=np.float32)
            freqs = np.outer(t, inv_freq)
            emb = np.concatenate([freqs, freqs], -1)
            return (jnp.asarray(np.cos(emb)), jnp.asarray(np.sin(emb)))

        def _apply_rope(x, cos, sin):
            d2 = x.shape[-1] // 2
            x1, x2 = (x[..., :d2], x[..., d2:])
            rot = jnp.concatenate([-x2, x1], axis=-1)
            return x * cos[None, None, :, :] + rot * sin[None, None, :, :]
        key = jax.random.key(seed)
        ks = jax.random.split(key, 10)

        def w(k, fan_in, fan_out):
            return jax.random.normal(k, (fan_in, fan_out), dtype=jnp.float32) * fan_in ** (-0.5)
        return {'x': jax.random.normal(ks[0], (B, T, N_EMBD), dtype=jnp.float32), 'W_kv': w(ks[1], N_EMBD, KV_RANK), 'g_kv': jnp.ones((KV_RANK,), dtype=jnp.float32), 'W_kdec': w(ks[2], KV_RANK, N_HEAD * HEAD_DIM), 'W_vdec': w(ks[3], KV_RANK, N_HEAD * HEAD_DIM), 'W_q': w(ks[4], N_EMBD, Q_RANK), 'W_qdec': w(ks[5], Q_RANK, N_HEAD * HEAD_DIM), 'W_krope': w(ks[6], N_EMBD, N_HEAD * ROPE_DIM), 'W_qrope': w(ks[7], Q_RANK, N_HEAD * ROPE_DIM), 'W_o': w(ks[8], N_HEAD * HEAD_DIM, N_EMBD)}
    _L0_attn_all = _L0_attn_setup()
    _L0_attn_in = {k: v for k, v in _L0_attn_all.items() if k in ('W_kv', 'g_kv', 'W_kdec', 'W_vdec', 'W_q', 'W_qdec', 'W_krope', 'W_qrope', 'W_o')}
    del _L0_attn_all

    def _L0_ffn_setup():
        import jax, jax.numpy as jnp
        import numpy as np
        H, F, E_SHARED, E_ROUTED, K = (256, 1024, 1, 8, 2)

        def _expert(x, w_up, w_down):
            h = jax.nn.gelu(jnp.einsum('bsh,hf->bsf', x, w_up), approximate=False)
            return jnp.einsum('bsf,fh->bsh', h, w_down)
        key = jax.random.key(seed)
        ks = jax.random.split(key, 6)
        x = jax.random.normal(ks[0], (4, 512, H), dtype=jnp.float32)
        s = 0.02
        shared_up = jax.random.normal(ks[1], (E_SHARED, H, F), dtype=jnp.float32) * s
        shared_down = jax.random.normal(ks[2], (E_SHARED, F, H), dtype=jnp.float32) * s
        routed_up = jax.random.normal(ks[3], (E_ROUTED, H, F), dtype=jnp.float32) * s
        routed_down = jax.random.normal(ks[4], (E_ROUTED, F, H), dtype=jnp.float32) * s
        router_w = jax.random.normal(ks[5], (H, E_ROUTED), dtype=jnp.float32) * s
        return {'x': x, 'shared_up': shared_up, 'shared_down': shared_down, 'routed_up': routed_up, 'routed_down': routed_down, 'router_w': router_w}
    _L0_ffn_all = _L0_ffn_setup()
    _L0_ffn_in = {k: v for k, v in _L0_ffn_all.items() if k in ('shared_up', 'shared_down', 'routed_up', 'routed_down', 'router_w')}
    del _L0_ffn_all

    def _L1_attn_setup():
        import jax, jax.numpy as jnp
        import numpy as np
        D_MODEL = 256
        D_STATE = 16
        DT_RANK = 64
        DT_MIN = 0.001
        DT_MAX = 0.1
        key = jax.random.key(seed)
        ks = jax.random.split(key, 7)
        B, S = (2, 512)
        return {'x': jax.random.normal(ks[0], (B, S, D_MODEL), jnp.float32), 'w_in': jax.random.normal(ks[1], (D_MODEL, D_MODEL), jnp.float32) / np.sqrt(D_MODEL).astype(np.float32), 'w_x': jax.random.normal(ks[2], (D_MODEL, DT_RANK + 2 * D_STATE), jnp.float32) / np.sqrt(D_MODEL).astype(np.float32), 'w_dt': jax.random.normal(ks[3], (DT_RANK, D_MODEL), jnp.float32) / np.sqrt(DT_RANK).astype(np.float32), 'b_dt': jnp.zeros((D_MODEL,), jnp.float32), 'A_log': jax.random.normal(ks[5], (D_MODEL, D_STATE), jnp.float32) * 0.5, 'Dp': jax.random.normal(ks[6], (D_MODEL,), jnp.float32)}
    _L1_attn_all = _L1_attn_setup()
    _L1_attn_in = {k: v for k, v in _L1_attn_all.items() if k in ('w_in', 'w_x', 'w_dt', 'b_dt', 'A_log', 'Dp')}
    del _L1_attn_all

    def _L1_ffn_setup():
        import jax, jax.numpy as jnp
        import numpy as np
        E, K, NG, TG = (64, 8, 8, 4)
        CAP = 256
        SCALE = 2.5

        def _route(x_flat, gate_weight, e_bias):
            T = x_flat.shape[0]
            logits = x_flat.astype(jnp.float32) @ gate_weight.astype(jnp.float32).T
            scores = jax.nn.sigmoid(logits)
            sfc = scores + e_bias[None, :]
            group_scores = jax.lax.top_k(sfc.reshape(T, NG, E // NG), 2)[0].sum(-1)
            _, gidx = jax.lax.top_k(group_scores, TG)
            gmask = jnp.zeros((T, NG), jnp.float32).at[jnp.arange(T)[:, None], gidx].set(1.0)
            smask = jnp.repeat(gmask, E // NG, axis=1)
            tmp = jnp.where(smask > 0, sfc, 0.0)
            _, topk_idx = jax.lax.top_k(tmp, K)
            topk_w = jnp.take_along_axis(scores, topk_idx, axis=1)
            topk_w = topk_w / (topk_w.sum(-1, keepdims=True) + 1e-20)
            return (topk_idx, topk_w * SCALE)

        def _moe_forward(hidden_states, gate_weight, e_bias, w1, w2, w3, shared_gate, shared_up, shared_down):
            B, S, H = hidden_states.shape
            T = B * S
            x = hidden_states.reshape(T, H)
            topk_idx, topk_w = _route(x, gate_weight, e_bias)
            Sk = T * K
            flat_e = topk_idx.reshape(-1)
            order = jnp.argsort(flat_e)
            sorted_e = flat_e[order]
            counts = jax.ops.segment_sum(jnp.ones((Sk,), jnp.int32), flat_e, num_segments=E)
            offsets = jnp.cumsum(counts) - counts
            pos = jnp.arange(Sk) - offsets[sorted_e]
            tok_sorted = x[order // K]
            xe = jnp.zeros((E, CAP, H), x.dtype).at[sorted_e, pos].set(tok_sorted, mode='drop')
            h = jax.nn.silu(jnp.einsum('ech,efh->ecf', xe, w1)) * jnp.einsum('ech,efh->ecf', xe, w3)
            ye = jnp.einsum('ecf,ehf->ech', h, w2)
            pos_c = jnp.minimum(pos, CAP - 1)
            vals = ye[sorted_e, pos_c]
            vals = jnp.where((pos < CAP)[:, None], vals, 0.0)
            flat_w = topk_w.reshape(-1)[order].astype(vals.dtype)
            flat_t = (jnp.arange(Sk) // K)[order]
            out = jax.ops.segment_sum(vals * flat_w[:, None], flat_t, num_segments=T)
            shared = jax.nn.silu(x @ shared_gate.T) * (x @ shared_up.T) @ shared_down.T
            return (out + shared).reshape(B, S, H)
        key = jax.random.key(seed)
        ks = jax.random.split(key, 9)
        B, S, H, F = (1, 512, 256, 128)
        bound = 1.0 / 32.0
        return {'hidden_states': jax.random.normal(ks[0], (B, S, H), jnp.float32), 'gate_weight': jax.random.uniform(ks[1], (E, H), jnp.float32, -bound, bound), 'e_bias': jnp.zeros((E,), jnp.float32), 'w1': jax.random.normal(ks[2], (E, F, H), jnp.float32) * 0.02, 'w2': jax.random.normal(ks[3], (E, H, F), jnp.float32) * 0.02, 'w3': jax.random.normal(ks[4], (E, F, H), jnp.float32) * 0.02, 'shared_gate': jax.random.normal(ks[5], (2 * F, H), jnp.float32) * 0.02, 'shared_up': jax.random.normal(ks[6], (2 * F, H), jnp.float32) * 0.02, 'shared_down': jax.random.normal(ks[7], (H, 2 * F), jnp.float32) * 0.02}
    _L1_ffn_all = _L1_ffn_setup()
    _L1_ffn_in = {k: v for k, v in _L1_ffn_all.items() if k in ('gate_weight', 'e_bias', 'w1', 'w2', 'w3', 'shared_gate', 'shared_up', 'shared_down')}
    del _L1_ffn_all
    return {'x': x, 'L0_tok_W': _L0_tok_in['W'], 'L0_tok_b': _L0_tok_in['b'], 'L0_tok_cls_token': _L0_tok_in['cls_token'], 'L0_tok_pos_embed': _L0_tok_in['pos_embed'], 'L0_attn_W_kv': _L0_attn_in['W_kv'], 'L0_attn_g_kv': _L0_attn_in['g_kv'], 'L0_attn_W_kdec': _L0_attn_in['W_kdec'], 'L0_attn_W_vdec': _L0_attn_in['W_vdec'], 'L0_attn_W_q': _L0_attn_in['W_q'], 'L0_attn_W_qdec': _L0_attn_in['W_qdec'], 'L0_attn_W_krope': _L0_attn_in['W_krope'], 'L0_attn_W_qrope': _L0_attn_in['W_qrope'], 'L0_attn_W_o': _L0_attn_in['W_o'], 'L0_ffn_shared_up': _L0_ffn_in['shared_up'], 'L0_ffn_shared_down': _L0_ffn_in['shared_down'], 'L0_ffn_routed_up': _L0_ffn_in['routed_up'], 'L0_ffn_routed_down': _L0_ffn_in['routed_down'], 'L0_ffn_router_w': _L0_ffn_in['router_w'], 'L1_attn_w_in': _L1_attn_in['w_in'], 'L1_attn_w_x': _L1_attn_in['w_x'], 'L1_attn_w_dt': _L1_attn_in['w_dt'], 'L1_attn_b_dt': _L1_attn_in['b_dt'], 'L1_attn_A_log': _L1_attn_in['A_log'], 'L1_attn_Dp': _L1_attn_in['Dp'], 'L1_ffn_gate_weight': _L1_ffn_in['gate_weight'], 'L1_ffn_e_bias': _L1_ffn_in['e_bias'], 'L1_ffn_w1': _L1_ffn_in['w1'], 'L1_ffn_w2': _L1_ffn_in['w2'], 'L1_ffn_w3': _L1_ffn_in['w3'], 'L1_ffn_shared_gate': _L1_ffn_in['shared_gate'], 'L1_ffn_shared_up': _L1_ffn_in['shared_up'], 'L1_ffn_shared_down': _L1_ffn_in['shared_down']}

def reference(x, L0_tok_W, L0_tok_b, L0_tok_cls_token, L0_tok_pos_embed, L0_attn_W_kv, L0_attn_g_kv, L0_attn_W_kdec, L0_attn_W_vdec, L0_attn_W_q, L0_attn_W_qdec, L0_attn_W_krope, L0_attn_W_qrope, L0_attn_W_o, L0_ffn_shared_up, L0_ffn_shared_down, L0_ffn_routed_up, L0_ffn_routed_down, L0_ffn_router_w, L1_attn_w_in, L1_attn_w_x, L1_attn_w_dt, L1_attn_b_dt, L1_attn_A_log, L1_attn_Dp, L1_ffn_gate_weight, L1_ffn_e_bias, L1_ffn_w1, L1_ffn_w2, L1_ffn_w3, L1_ffn_shared_gate, L1_ffn_shared_up, L1_ffn_shared_down):
    import jax
    import jax.numpy as jnp

    def _L0_tok_ref(x, W, b, cls_token, pos_embed):
        import jax, jax.numpy as jnp
        import numpy as np
        IMG = 96
        PATCH = 16
        C_IN = 3
        EMBED = 256
        NPH = IMG // PATCH
        NUM_PATCHES = NPH * NPH
        PATCH_DIM = PATCH * PATCH * C_IN
        B, C, H, Wd = x.shape
        nph, npw = (H // PATCH, Wd // PATCH)
        patches = x.reshape(B, C, nph, PATCH, npw, PATCH)
        patches = patches.transpose(0, 2, 4, 1, 3, 5)
        patches = patches.reshape(B, nph * npw, C * PATCH * PATCH)
        proj = jnp.einsum('bnd,ed->bne', patches, W) + b
        cls = jnp.broadcast_to(cls_token, (B, 1, cls_token.shape[-1]))
        out = jnp.concatenate([cls, proj], axis=1) + pos_embed
        return out

    def _L0_attn_ref(x, W_kv, g_kv, W_kdec, W_vdec, W_q, W_qdec, W_krope, W_qrope, W_o):
        import jax, jax.numpy as jnp
        import numpy as np
        N_EMBD = 256
        N_HEAD = 16
        HEAD_DIM = N_EMBD // N_HEAD
        KV_RANK = 64
        Q_RANK = 128
        ROPE_DIM = 32
        B, T = (2, 512)
        EPS = 1e-06

        def _rope_tables(T, dim):
            inv_freq = 1.0 / 10000.0 ** (np.arange(0, dim, 2, dtype=np.float32) / dim)
            t = np.arange(T, dtype=np.float32)
            freqs = np.outer(t, inv_freq)
            emb = np.concatenate([freqs, freqs], -1)
            return (jnp.asarray(np.cos(emb)), jnp.asarray(np.sin(emb)))

        def _apply_rope(x, cos, sin):
            d2 = x.shape[-1] // 2
            x1, x2 = (x[..., :d2], x[..., d2:])
            rot = jnp.concatenate([-x2, x1], axis=-1)
            return x * cos[None, None, :, :] + rot * sin[None, None, :, :]
        Bx, Tx, C = x.shape
        kv_c = x @ W_kv
        kv_c = kv_c * jax.lax.rsqrt(jnp.mean(kv_c * kv_c, axis=-1, keepdims=True) + EPS) * g_kv
        q_c = x @ W_q

        def heads(y, d):
            return y.reshape(Bx, Tx, N_HEAD, d).transpose(0, 2, 1, 3)
        k_content = heads(kv_c @ W_kdec, HEAD_DIM)
        v = heads(kv_c @ W_vdec, HEAD_DIM)
        q_content = heads(q_c @ W_qdec, HEAD_DIM)
        k_rope = heads(x @ W_krope, ROPE_DIM)
        q_rope = heads(q_c @ W_qrope, ROPE_DIM)
        cos, sin = _rope_tables(Tx, ROPE_DIM)
        q_rope = _apply_rope(q_rope, cos, sin)
        k_rope = _apply_rope(k_rope, cos, sin)
        q = jnp.concatenate([q_content, q_rope], axis=-1)
        k = jnp.concatenate([k_content, k_rope], axis=-1)
        scale = 1.0 / jnp.sqrt(jnp.float32(q.shape[-1]))
        scores = jnp.einsum('bhqd,bhkd->bhqk', q, k) * scale
        causal = jnp.tril(jnp.ones((Tx, Tx), dtype=bool))
        scores = jnp.where(causal[None, None], scores, jnp.float32(-jnp.inf))
        attn = jax.nn.softmax(scores, axis=-1)
        out = jnp.einsum('bhqk,bhkd->bhqd', attn, v)
        out = out.transpose(0, 2, 1, 3).reshape(Bx, Tx, N_HEAD * HEAD_DIM)
        return out @ W_o

    def _L0_ffn_ref(x, shared_up, shared_down, routed_up, routed_down, router_w):
        import jax, jax.numpy as jnp
        import numpy as np
        H, F, E_SHARED, E_ROUTED, K = (256, 1024, 1, 8, 2)

        def _expert(x, w_up, w_down):
            h = jax.nn.gelu(jnp.einsum('bsh,hf->bsf', x, w_up), approximate=False)
            return jnp.einsum('bsf,fh->bsh', h, w_down)
        shared_out = jnp.zeros_like(x)
        for i in range(E_SHARED):
            shared_out = shared_out + _expert(x, shared_up[i], shared_down[i])
        probs = jax.nn.softmax(jnp.einsum('bsh,he->bse', x, router_w), axis=-1)
        top_k_prob, top_k_idx = jax.lax.top_k(probs, K)
        onehot = jax.nn.one_hot(top_k_idx, E_ROUTED, dtype=x.dtype)
        gates = jnp.einsum('bsk,bske->bse', top_k_prob, onehot)
        routed_out = jnp.zeros_like(x)
        for e in range(E_ROUTED):
            y = _expert(x, routed_up[e], routed_down[e])
            routed_out = routed_out + gates[..., e:e + 1] * y
        return shared_out + routed_out + x

    def _L1_attn_ref(x, w_in, w_x, w_dt, b_dt, A_log, Dp):
        import jax, jax.numpy as jnp
        import numpy as np
        D_MODEL = 256
        D_STATE = 16
        DT_RANK = 64
        DT_MIN = 0.001
        DT_MAX = 0.1
        x_in = jnp.einsum('bsd,de->bse', x, w_in)
        proj = jnp.einsum('bsd,dp->bsp', x_in, w_x)
        dt_low, Bm, Cm = jnp.split(proj, [DT_RANK, DT_RANK + D_STATE], axis=-1)
        dt = jax.nn.softplus(jnp.einsum('bsr,rd->bsd', dt_low, w_dt) + b_dt) * (DT_MAX - DT_MIN) + DT_MIN
        A = -jnp.exp(A_log)
        b, s, d = x.shape
        h0 = jnp.zeros((b, d, D_STATE), x.dtype)
        dt_tm = jnp.swapaxes(dt, 0, 1)
        u_tm = jnp.swapaxes(x_in, 0, 1)
        B_tm = jnp.swapaxes(Bm, 0, 1)
        C_tm = jnp.swapaxes(Cm, 0, 1)

        def step(h, inp):
            dtt, ut, bt, ct = inp
            dA = dtt[:, :, None] * A
            barA = jnp.exp(dA)
            inp_term = jnp.einsum('bdn,bn,bd->bn', dA, bt, ut)
            h = barA * h + inp_term[:, None, :]
            y = jnp.einsum('bdn,bn->bd', h, ct) + Dp * ut
            return (h, y)
        _, ys = jax.lax.scan(step, h0, (dt_tm, u_tm, B_tm, C_tm))
        return jnp.swapaxes(ys, 0, 1)

    def _L1_ffn_ref(hidden_states, gate_weight, e_bias, w1, w2, w3, shared_gate, shared_up, shared_down):
        import jax, jax.numpy as jnp
        import numpy as np
        E, K, NG, TG = (64, 8, 8, 4)
        CAP = 256
        SCALE = 2.5

        def _route(x_flat, gate_weight, e_bias):
            T = x_flat.shape[0]
            logits = x_flat.astype(jnp.float32) @ gate_weight.astype(jnp.float32).T
            scores = jax.nn.sigmoid(logits)
            sfc = scores + e_bias[None, :]
            group_scores = jax.lax.top_k(sfc.reshape(T, NG, E // NG), 2)[0].sum(-1)
            _, gidx = jax.lax.top_k(group_scores, TG)
            gmask = jnp.zeros((T, NG), jnp.float32).at[jnp.arange(T)[:, None], gidx].set(1.0)
            smask = jnp.repeat(gmask, E // NG, axis=1)
            tmp = jnp.where(smask > 0, sfc, 0.0)
            _, topk_idx = jax.lax.top_k(tmp, K)
            topk_w = jnp.take_along_axis(scores, topk_idx, axis=1)
            topk_w = topk_w / (topk_w.sum(-1, keepdims=True) + 1e-20)
            return (topk_idx, topk_w * SCALE)

        def _moe_forward(hidden_states, gate_weight, e_bias, w1, w2, w3, shared_gate, shared_up, shared_down):
            B, S, H = hidden_states.shape
            T = B * S
            x = hidden_states.reshape(T, H)
            topk_idx, topk_w = _route(x, gate_weight, e_bias)
            Sk = T * K
            flat_e = topk_idx.reshape(-1)
            order = jnp.argsort(flat_e)
            sorted_e = flat_e[order]
            counts = jax.ops.segment_sum(jnp.ones((Sk,), jnp.int32), flat_e, num_segments=E)
            offsets = jnp.cumsum(counts) - counts
            pos = jnp.arange(Sk) - offsets[sorted_e]
            tok_sorted = x[order // K]
            xe = jnp.zeros((E, CAP, H), x.dtype).at[sorted_e, pos].set(tok_sorted, mode='drop')
            h = jax.nn.silu(jnp.einsum('ech,efh->ecf', xe, w1)) * jnp.einsum('ech,efh->ecf', xe, w3)
            ye = jnp.einsum('ecf,ehf->ech', h, w2)
            pos_c = jnp.minimum(pos, CAP - 1)
            vals = ye[sorted_e, pos_c]
            vals = jnp.where((pos < CAP)[:, None], vals, 0.0)
            flat_w = topk_w.reshape(-1)[order].astype(vals.dtype)
            flat_t = (jnp.arange(Sk) // K)[order]
            out = jax.ops.segment_sum(vals * flat_w[:, None], flat_t, num_segments=T)
            shared = jax.nn.silu(x @ shared_gate.T) * (x @ shared_up.T) @ shared_down.T
            return (out + shared).reshape(B, S, H)
        return _moe_forward(hidden_states, gate_weight, e_bias, w1, w2, w3, shared_gate, shared_up, shared_down)
    h = _L0_tok_ref(x, L0_tok_W, L0_tok_b, L0_tok_cls_token, L0_tok_pos_embed)
    h = h + _L0_attn_ref(_layernorm(h, axis=-1), L0_attn_W_kv, L0_attn_g_kv, L0_attn_W_kdec, L0_attn_W_vdec, L0_attn_W_q, L0_attn_W_qdec, L0_attn_W_krope, L0_attn_W_qrope, L0_attn_W_o)
    h = h + _L0_ffn_ref(_layernorm(h, axis=-1), L0_ffn_shared_up, L0_ffn_shared_down, L0_ffn_routed_up, L0_ffn_routed_down, L0_ffn_router_w)
    h = h + _L1_attn_ref(_layernorm(h, axis=-1), L1_attn_w_in, L1_attn_w_x, L1_attn_w_dt, L1_attn_b_dt, L1_attn_A_log, L1_attn_Dp)
    h = h + _L1_ffn_ref(_layernorm(h, axis=-1), L1_ffn_gate_weight, L1_ffn_e_bias, L1_ffn_w1, L1_ffn_w2, L1_ffn_w3, L1_ffn_shared_gate, L1_ffn_shared_up, L1_ffn_shared_down)
    return h

_drawn_inputs = setup_inputs


def setup_inputs(seed=0):
    import zlib

    import numpy as np

    out = dict(_drawn_inputs(seed))
    spreads = {'L0_attn_g_kv': (1.0, 0.2), 'L1_attn_b_dt': (0.0, 0.1), 'L1_ffn_e_bias': (0.0, 0.8)}
    factors = {'L0_ffn_router_w': 2.966,
     'L1_ffn_gate_weight': 8.0,
     'L1_ffn_w1': 8.0,
     'L1_ffn_w2': 8.0,
     'L1_ffn_w3': 8.0,
     'L1_ffn_shared_gate': 8.0,
     'L1_ffn_shared_up': 8.0,
     'L1_ffn_shared_down': 8.0}
    for name, (base, spread) in spreads.items():
        noise = np.random.default_rng([zlib.crc32(name.encode()), seed]).standard_normal(out[name].shape)
        drawn = base * np.exp(spread * noise) if base else spread * noise
        out[name] = jnp.asarray(drawn.astype(out[name].dtype))
    for name, factor in factors.items():
        out[name] = (out[name] * factor).astype(out[name].dtype)
    return out
```

```python
from contextlib import ExitStack

import numpy as np
import concourse.bass as bass
from concourse import mybir

F32 = mybir.dt.float32
BF16 = mybir.dt.bfloat16
ALU = mybir.AluOpType
ACT = mybir.ActivationFunctionType
AX = mybir.AxisListType

P = 128
B = 16
T = 37
NT = B * T
NTILE = -(-NT // P)
ROWS = [min(P, NT - P * t) for t in range(NTILE)]
NPAD = NTILE * P
HALF = NT // 2
D = 256
KP = 768 // P
LN_EPS = 1e-5
RMS_EPS = 1e-6

NH, HD, RD = 16, 16, 32
R_KV, R_Q = 64, 128
SCALE = float(HD + RD) ** -0.5
IMGS = 3
GR = IMGS * T
GROUPS = [(g * GR, min(GR, NT - g * GR)) for g in range(-(-NT // GR))]
NG = len(GROUPS)
MASKED = -1e30

E0, F0 = 9, 1024
FT0 = F0 // P
K0 = 2
SLOTS0 = 3

NS = 16
R_DT = 64
DT_MIN, DT_MAX = 0.001, 0.1

E1, F1 = 66, 128
NR1, NGRP, TOPG, TOPK = 64, 8, 4, 8
CAP = 256
SCALE1 = 2.5
SLOTS1 = 3
NI = 72
W1C = 2 * 2 * F1 + D
REMOVED = -3e38


def vit_tower(nc, A, out):
    ctx = ExitStack()
    with ctx:
        def sb(name, shape, dt=F32):
            return ctx.enter_context(nc.sbuf_tensor(name, shape, dt))

        def sem(name):
            return ctx.enter_context(nc.semaphore(name))

        PS = ctx.enter_context(nc.psum_tensor("PS", [P, 8, 512], F32))

        h = sb("h", [P, NTILE, D])
        xn = sb("xn", [P, NTILE, D])
        xT = sb("xT", [P, 2, NPAD])
        stats = sb("stats", [P, NTILE, 6])
        mv = sb("mv", [P, NTILE, 2])
        std = sb("std", [P, NTILE])
        rstd = sb("rstd", [P, NTILE])
        ident = sb("ident", [P, P])
        identb = sb("identb", [P, P], BF16)
        onesb = sb("onesb", [P, P], BF16)
        upperb = sb("upperb", [P, P], BF16)
        maskb = sb("maskb", [GR, 4, GR], BF16)
        ones64 = sb("ones64", [R_KV, R_KV])
        before = sb("before", [P, 8, 8])
        cosT = sb("cosT", [P, T])
        sinT = sb("sinT", [P, T])
        sel = sb("sel", [NS, NS, P])

        wkv = sb("wkv", [P, 2, R_KV])
        wq = sb("wq", [P, 2, R_Q])
        g_kv = sb("g_kv", [R_KV, 1])
        wo = sb("wo", [P, 2, D])
        wvdec = sb("wvdec", [R_KV, D])
        w_in = sb("w_in", [P, 2, D])
        w_x = sb("w_x", [P, 2, R_DT + 2 * NS])
        w_dt = sb("w_dt", [R_DT, D])
        b_dt = sb("b_dt", [P, 2])
        a_log = sb("a_log", [P, 2, NS])
        d_p = sb("d_p", [P, 2])
        rw0 = sb("rw0", [P, 2, 8])
        gw1 = sb("gw1", [P, 2, NR1])
        e_bias = sb("e_bias", [P, NR1])

        SCR = 20400
        scratch = sb("scratch", [P, SCR])

        def views(*shapes):
            at, out_ = 0, []
            for rows, shape in shapes:
                n = int(np.prod(shape))
                v = scratch[0:rows, at:at + n]
                if len(shape) > 1:
                    names = "abcd"[:len(shape)]
                    v = v.rearrange(f"p ({' '.join(names)}) -> p {' '.join(names)}",
                                    **{c: s for c, s in zip(names[1:], shape[1:])})
                out_.append(v)
                at += n
            assert at <= SCR, at
            return out_

        w0up = sb("w0up", [P, SLOTS0, 2, F0])
        w0dn = sb("w0dn", [P, SLOTS0, FT0, D])
        w0flat = w0up[:, :, :, :].rearrange("p s c f -> p (s c f)")
        patches = w0flat[:, 0:KP * NT].rearrange("p (k n) -> p k n", k=KP)
        wtok = w0dn[:, 0, 0:KP, :]
        rowsel = w0dn[0:T + 2, 1, 0:3, :].rearrange("p a b -> p (a b)")[:, 0:NT]
        posb = w0dn[0:T + 2, 2, 0, :]
        (qk, prob, probT, vext, OT, rt, kvn, qc, wkac) = views(
            (P, (2, 4, 2, NT)), (GR, (NH, GR)), (GR, (NH, GR)), (GR, (NG, NH, HD + 1)),
            (P, (2, NT)), (P, (4, NT)), (R_KV, (NT,)), (P, (NT,)), (R_KV, (4, P)))
        kv_sb, sq, rms, rrms = (w0flat[0:R_KV, 3072 + k * NT:3072 + (k + 1) * NT] for k in range(4))
        wkar = w0flat[:, 0:1024].rearrange("p (c m n) -> p c m n", c=2, m=4)
        wkbr = w0flat[:, 1024:2048].rearrange("p (c m n) -> p c m n", c=2, m=4)
        wqa = w0flat[:, 2048:2560].rearrange("p (m n) -> p m n", m=4)
        wqb = w0flat[:, 2560:3072].rearrange("p (m n) -> p m n", m=4)
        mx = sb("mx", [GR, NH])
        rsum = sb("rsum", [GR, NH])
        obuf = sb("obuf", [GR, D])
        (hT0,) = views((P, (FT0, NT)))
        lg0 = sb("lg0", [P, NTILE, 8])
        p0 = sb("p0", [P, NTILE, 8])
        r5 = sb("r5", [P, NTILE])
        cmp_gt = sb("cmp_gt", [P, NTILE, 8, 8])
        cmp_eq = sb("cmp_eq", [P, NTILE, 8, 8])
        rank = sb("rank", [P, NTILE, 8])
        gates0 = sb("gates0", [P, NTILE, E0])
        BA = 4
        (u, dt, dtu, spa, spb, bT, cT, dtl, inpT, barA, hs, hc, du) = views(
            (P, (2, NT)), (P, (2, NT)), (P, (2, NT)), (P, (2, NT)), (P, (2, NT)),
            (NS, (NT,)), (NS, (NT,)), (R_DT, (NT,)), (NS, (NT,)),
            (P, (BA, NT)), (P, (2, NT)), (P, (4, NT)), (P, (2, NT)))
        a_neg = sb("a_neg", [P, 2, NS])
        zerosb = sb("zerosb", [P, 512], BF16)
        w1s = sb("w1s", [P, SLOTS1, W1C])
        (silu_g, hT1) = views((P, (2, HALF)), (P, (NT,)))
        scores = sb("scores", [P, NTILE, NR1])
        sfc = sb("sfc", [P, NTILE, NR1])
        top8g = sb("top8g", [P, NTILE * NGRP, 8])
        gscore = sb("gscore", [P, NTILE, NGRP])
        tmp = sb("tmp", [P, NTILE, NR1])
        top8 = sb("top8", [P, NTILE, 8])
        chosen = sb("chosen", [P, NTILE, NR1])
        chosenb = sb("chosenb", [P, NTILE, NR1], BF16)
        gates1 = sb("gates1", [P, NTILE, NR1 + 1])
        validb = sb("validb", [P, NTILE], BF16)
        upto = sb("upto", [NR1, NR1], BF16)
        place = sb("place", [NR1, NI])
        numbers = sb("numbers", [NR1, 3])
        active = sb("active", [NR1, 1])
        activeb = sb("activeb", [NR1, 1], BF16)
        upto_n = sb("upto_n", [NR1, 1])
        onehot = sb("onehot", [NR1, NI])
        counts = sb("counts", [1, 1])
        lists = sb("lists", [1, 2 * NI + 1], mybir.dt.int32)

        patch_in = [sem(f"patch_in{k}") for k in range(KP)]
        pos_in = sem("pos_in")
        ident_in = sem("ident_in")
        attn_in = sem("attn_in")
        attn2_in = sem("attn2_in")
        route_in = sem("route_in")
        scan_in = sem("scan_in")
        embed_mm = sem("embed_mm")
        dve_step = sem("dve_step")
        act_step = sem("act_step")
        var_ready = sem("var_ready")
        std_ready = sem("std_ready")
        xn_ready = sem("xn_ready")
        xT_mm = sem("xT_mm")
        xT_lo = sem("xT_lo")
        xT_hi = sem("xT_hi")
        kv_mm, kv_ready, sq_ready, ms_mm, rms_ready, kvn_ready = (
            sem(n) for n in ("kv_mm", "kv_ready", "sq_ready", "ms_mm", "rms_ready", "kvn_ready"))
        qc_mm, qc_ready = sem("qc_mm"), sem("qc_ready")
        rope_mm, rope_read, rope_done = sem("rope_mm"), sem("rope_read"), sem("rope_done")
        v_mm, v_ready, v_ones = sem("v_mm"), sem("v_ready"), sem("v_ones")
        s_mm, s_shift, p_ready = sem("s_mm"), sem("s_shift"), sem("p_ready")
        pt_mm, pt_ready = sem("pt_mm"), sem("pt_ready")
        pv_mm, o_ready, wo_mm = sem("pv_mm"), sem("o_ready"), sem("wo_mm")
        h_attn = sem("h_attn")
        r0_mm, r0_shift, r0_exp = sem("r0_mm"), sem("r0_shift"), sem("r0_exp")
        up_in = [sem(f"up_in{s}") for s in range(SLOTS0)]
        dn_in = [sem(f"dn_in{s}") for s in range(SLOTS0)]
        up_mm, gelu_done, y_mm, y_taken = sem("up_mm"), sem("gelu_done"), sem("y_mm"), sem("y_taken")
        u_mm, u_ready, dtl_mm, dtl_ready = sem("u_mm"), sem("u_ready"), sem("dtl_mm"), sem("dtl_ready")
        b_mm, b_ready, c_mm, c_ready = sem("b_mm"), sem("b_ready"), sem("c_mm"), sem("c_ready")
        dt_mm, sp_abs, sp_ln, sp_max = sem("dt_mm"), sem("sp_abs"), sem("sp_ln"), sem("sp_max")
        dt_ready, dtu_ready, a_exp, a_ready = sem("dt_ready"), sem("dtu_ready"), sem("a_exp"), sem("a_ready")
        g_mm, inp_ready, ring_ready, du_ready = sem("g_mm"), sem("inp_ready"), sem("ring_ready"), sem("du_ready")
        barA_ready, ib_mm, cb_mm, scanned = sem("barA_ready"), sem("ib_mm"), sem("cb_mm"), sem("scanned")
        hc_ready, hc_used, yscan_mm = sem("hc_ready"), sem("hc_used"), sem("yscan_mm")
        r1_mm, sig_ready, chosen_ready, pos_mm = sem("r1_mm"), sem("sig_ready"), sem("chosen_ready"), sem("pos_mm")
        w1_in = [sem(f"w1_in{s}") for s in range(SLOTS1)]
        count_mm, active_ready, place_mm, onehot_ready, lists_mm, lists_ready = (
            sem(n) for n in ("count_mm", "active_ready", "place_mm", "onehot_ready", "lists_mm", "lists_ready"))
        gu_mm, silu_ready, hT_ready = sem("gu_mm"), sem("silu_ready"), sem("hT_ready")
        y1_mm, y1_taken, out_done = sem("y1_mm"), sem("y1_taken"), sem("out_done")

        block = ctx.enter_context(nc.Block())

        YG = [(0, 1), (2, 3), (4,)]

        @block.sync
        def _(sp):
            for k in range(KP):
                sp.dma_start(patches[:, k, :], A["patchesT"][k]).then_inc(patch_in[k], 16)
                sp.dma_start(wtok[:, k, :], A["W_tok"][k]).then_inc(patch_in[k], 16)
            sp.dma_start(rowsel, A["rowsel"]).then_inc(pos_in, 16)
            sp.dma_start(posb, A["posb"]).then_inc(pos_in, 16)
            sp.dma_start(ident[:, :], A["ident"]).then_inc(ident_in, 16)
            for dst, name in ((wkv[:, :, :], "wkv"), (wq[:, :, :], "wq"), (g_kv[:, :], "g_kv"),
                              (ones64[:, :], "ones64"), (wkac, "wkac"), (cosT[:, :], "cosT"),
                              (sinT[:, :], "sinT"), (wvdec[:, :], "wvdec"), (wo[:, :, :], "wo"),
                              (maskb[:, :, :], "maskb"), (identb[:, :], "identb")):
                sp.dma_start(dst, A[name]).then_inc(attn_in, 16)
            sp.wait_ge(embed_mm, NTILE)
            for dst, name in ((wqa, "wqa"), (wqb, "wqb"), (wkar, "wkar"), (wkbr, "wkbr")):
                sp.dma_start(dst, A[name]).then_inc(attn2_in, 16)
            for dst, name in ((rw0[:, :, :], "rw0"), (gw1[:, :, :], "gw1"), (e_bias[:, :], "e_bias"),
                              (before[:, :, :], "before"), (onesb[:, :], "onesb"), (upperb[:, :], "upperb"),
                              (validb[:, :], "validb"), (upto[:, :], "upto"), (place[:, :], "place"),
                              (numbers[:, :], "numbers")):
                sp.dma_start(dst, A[name]).then_inc(route_in, 16)
            for dst, name in ((w_in[:, :, :], "w_in"), (w_x[:, :, :], "w_x"), (w_dt[:, :], "w_dt"),
                              (b_dt[:, :], "b_dt"), (a_log[:, :, :], "a_log"), (d_p[:, :], "d_p"),
                              (sel[:, :, :], "sel")):
                sp.dma_start(dst, A[name]).then_inc(scan_in, 16)
            for s in range(SLOTS0):
                sp.dma_start(w0dn[:, s], A["w0dn"][s]).then_inc(dn_in[s], 16)
            sp.wait_ge(rope_mm, 8)
            for s in range(SLOTS0):
                sp.dma_start(w0up[:, s], A["w0up"][s]).then_inc(up_in[s], 16)
            for s in range(2):
                sp.dma_start(w1s[:, s, :], A["w1"][NR1 + s]).then_inc(w1_in[s], 16)
            with sp.Fori(0, E0 // SLOTS0 - 1) as i:
                for s in range(SLOTS0):
                    sp.wait_ge(up_mm, i * (SLOTS0 * FT0) + (s + 1) * FT0)
                    sp.dma_start(w0up[:, s], A["w0up"][i * SLOTS0 + (SLOTS0 + s)]).then_inc(up_in[s], 16)
                    sp.wait_ge(y_mm, i * (SLOTS0 * 3) + (s + 1) * 3)
                    sp.dma_start(w0dn[:, s], A["w0dn"][i * SLOTS0 + (SLOTS0 + s)]).then_inc(dn_in[s], 16)
            sp.wait_ge(lists_ready, 1)
            iters = sp.value_load(lists[0:1, 2 * NI:2 * NI + 1], min_val=2, max_val=-(-NR1 // SLOTS1))
            for s in range(SLOTS1):
                if s < 2:
                    sp.wait_ge(y1_mm, 3 * (s + 1))
                e = sp.value_load(lists[0:1, s:s + 1], min_val=0, max_val=NR1 - 1)
                sp.dma_start(w1s[:, s, :], A["w1"][e]).then_inc(w1_in[s], 16)
            with sp.Fori(0, iters - 1) as i:
                for s in range(SLOTS1):
                    e = sp.value_load(lists[0:1, bass.ds(i * SLOTS1 + (SLOTS1 + s), 1)], min_val=0, max_val=NR1 - 1)
                    sp.wait_ge(y1_mm, i * (SLOTS1 * 3) + (6 + (s + 1) * 3))
                    sp.dma_start(w1s[:, s, :], A["w1"][e]).then_inc(w1_in[s], 16)
            for t in range(NTILE):
                sp.wait_ge(y1_taken, iters * (3 * SLOTS1) + (6 + t // 2 + 1))
                sp.dma_start(out[t * P:t * P + ROWS[t], :], h[0:ROWS[t], t, :]).then_inc(out_done, 16)
            sp.wait_ge(out_done, 16 * NTILE)

        @block.gpsimd
        def _(pool):
            nc.gpsimd.memset(vext[:, :, :, HD:HD + 1], 1.0).then_inc(v_ones, 1)
            for idx in range(8):
                which, m = idx // 4, idx % 4
                pool.wait_ge(rope_read, idx + 1)
                nc.gpsimd.tensor_tensor(qk[:, which, m, 0, :], rt[:, 0, :], rt[:, 1, :], ALU.subtract)
                nc.gpsimd.tensor_tensor(qk[:, which, m, 1, :], rt[:, 2, :], rt[:, 3, :], ALU.add).then_inc(rope_done, 1)

        @block.scalar
        def _(act):
            steps = [0]

            def link(ins):
                steps[0] += 1
                ins.then_inc(act_step, 1)
                act.wait_ge(act_step, steps[0])

            def layernorm(l):
                act.wait_ge(var_ready, l + 1)
                nc.scalar.activation(std[:, :], mv[:, :, 1], ACT.Sqrt, bias=LN_EPS).then_inc(std_ready, 1)
                act.wait_ge(xT_mm, l + 1)
                nc.scalar.copy(xT[:, 1, :], PS[:, 2:4, :].rearrange("p b n -> p (b n)")[:, 0:NPAD]).then_inc(xT_hi, 1)

            layernorm(0)
            act.wait_ge(qc_mm, 1)
            nc.scalar.copy(qc.rearrange("p (b n) -> p b n", b=2), PS[:, 2:4, 0:HALF]).then_inc(qc_ready, 1)
            act.wait_ge(kv_ready, 1)
            nc.scalar.activation(sq, kv_sb, ACT.Square).then_inc(sq_ready, 1)
            act.wait_ge(ms_mm, 1)
            nc.scalar.activation(rms.rearrange("p (b n) -> p b n", b=2), PS[0:R_KV, 4:6, 0:HALF], ACT.Sqrt,
                                 bias=RMS_EPS).then_inc(rms_ready, 1)
            act.wait_ge(v_ones, 1)
            for i in range(NG // 2):
                act.wait_ge(v_mm, i + 1)
                rows = GR if i < NG // 2 - 1 else None
                if rows:
                    nc.scalar.copy(vext[:, 2 * i:2 * i + 2, :, 0:HD],
                                   PS[0:GR, 4 + i, :].rearrange("p (g h d) -> p g h d", g=2, h=NH)).then_inc(v_ready, 1)
                else:
                    last = GROUPS[-1][1]
                    nc.scalar.copy(vext[:, 2 * i, :, 0:HD],
                                   PS[0:GR, 4 + i, 0:D].rearrange("p (h d) -> p h d", h=NH))
                    nc.scalar.copy(vext[0:last, 2 * i + 1, :, 0:HD],
                                   PS[0:last, 4 + i, D:2 * D].rearrange("p (h d) -> p h d", h=NH)).then_inc(v_ready, 1)

            def exps(g):
                rows = GROUPS[g][1]
                act.wait_ge(s_shift, g + 1)
                nc.scalar.activation(prob[0:rows, :, 0:rows], prob[0:rows, :, 0:rows], ACT.Exp,
                                     scale=SCALE).then_inc(p_ready, 1)

            def o_transposed(g):
                c0, rows = GROUPS[g]
                k = ticket[("O", g)]
                act.wait_ge(pt_mm, k + 1)
                nc.scalar.copy(OT[:, :, c0:c0 + rows],
                               PS[:, 4 + k % 3, 0:2 * GR].rearrange("p (c n) -> p c n", c=2)[:, :, 0:rows]).then_inc(pt_ready, 1)

            exps(0)
            for g in range(NG):
                rows = GROUPS[g][1]
                if g:
                    o_transposed(g - 1)
                for q in range(4):
                    k = ticket[("P", g, q)]
                    act.wait_ge(pt_mm, k + 1)
                    if g and q == 0:
                        act.wait_ge(pv_mm, g)
                    nc.scalar.copy(probT[0:rows, 4 * q:4 * q + 4, 0:rows],
                                   PS[0:rows, 4 + k % 3, 0:4 * GR].rearrange("p (c n) -> p c n", c=4)[:, :, 0:rows]).then_inc(pt_ready, 1)
                if g + 1 < NG:
                    exps(g + 1)
            o_transposed(NG - 1)

            layernorm(1)
            act.wait_ge(r0_shift, 1)
            nc.scalar.activation(lg0[:, :, :], lg0[:, :, :], ACT.Exp).then_inc(r0_exp, 1)
            with act.Fori(0, E0 // SLOTS0) as i:
                for s in range(SLOTS0):
                    for f in range(FT0):
                        z = f % 2
                        act.wait_ge(up_mm, i * (SLOTS0 * FT0) + (s * FT0 + f + 1))
                        nc.scalar.activation(hT0[:, f, :].rearrange("p (b n) -> p b n", b=2),
                                             PS[:, 2 * z:2 * z + 2, 0:HALF], ACT.Gelu).then_inc(gelu_done, 1)

            layernorm(2)
            act.wait_ge(scan_in, 7 * 16)
            nc.scalar.activation(a_neg[:, :, :], a_log[:, :, :], ACT.Exp).then_inc(a_exp, 1)
            act.wait_ge(u_mm, 1)
            for c in range(2):
                last = nc.scalar.copy(u[:, c, :].rearrange("p (b n) -> p b n", b=2), PS[:, 2 * c:2 * c + 2, 0:HALF])
            last.then_inc(u_ready, 1)
            act.wait_ge(dtl_mm, 1)
            nc.scalar.copy(dtl.rearrange("p (b n) -> p b n", b=2), PS[0:R_DT, 4:6, 0:HALF]).then_inc(dtl_ready, 1)
            act.wait_ge(b_mm, 1)
            nc.scalar.copy(bT.rearrange("p (b n) -> p b n", b=2), PS[0:NS, 6:8, 0:HALF]).then_inc(b_ready, 1)
            act.wait_ge(c_mm, 1)
            nc.scalar.copy(cT.rearrange("p (b n) -> p b n", b=2), PS[0:NS, 4:6, 0:HALF]).then_inc(c_ready, 1)
            act.wait_ge(sp_max, 1)
            link(nc.scalar.activation(spa, spb, ACT.Abs))
            link(nc.scalar.activation(spa, spa, ACT.Exp, scale=-1.0))
            nc.scalar.activation(spa, spa, ACT.Ln, bias=1.0).then_inc(sp_ln, 1)
            act.wait_ge(dt_ready, 1)
            act.wait_ge(a_ready, 1)
            act.wait_ge(ring_ready, 1)
            for n in range(NS):
                for c in range(2):
                    k = 2 * n + c
                    if k >= BA:
                        act.wait_ge(scanned, k - BA + 1)
                    nc.scalar.activation(barA[:, k % BA, :].rearrange("p (b t) -> p b t", b=B)[:, :, 1:T],
                                         dt[:, c, :].rearrange("p (b t) -> p b t", b=B)[:, :, 1:T], ACT.Exp,
                                         scale=a_neg[:, c, n:n + 1]).then_inc(barA_ready, 1)

            layernorm(3)
            act.wait_ge(r1_mm, 1)
            nc.scalar.activation(scores[:, :, :].rearrange("p t e -> p (t e)"), PS[:, 7, 0:NTILE * NR1],
                                 ACT.Sigmoid).then_inc(sig_ready, 1)
            def silu_of(x):
                for n in range(2):
                    act.wait_ge(gu_mm, x * 2 + (n + 1))
                    nc.scalar.activation(silu_g[:, n, :], PS[:, 2 * n, 0:HALF], ACT.Silu).then_inc(silu_ready, 1)

            for x in range(2):
                silu_of(x)
            act.wait_ge(lists_ready, 1)
            iters = act.value_load(lists[0:1, 2 * NI:2 * NI + 1], min_val=2, max_val=-(-NR1 // SLOTS1))
            with act.Fori(0, iters) as i:
                for s in range(SLOTS1):
                    silu_of(i * SLOTS1 + (2 + s))

        @block.vector
        def _(dve):
            steps = [0]

            def step(ins):
                steps[0] += 1
                ins.then_inc(dve_step, 1)

            def settle():
                dve.wait_ge(dve_step, steps[0])

            def link(ins):
                step(ins)
                settle()

            def layernorm(l):
                for t in range(NTILE):
                    step(nc.vector.bn_stats(stats[:, t, :], h[:, t, :]))
                settle()
                for t in range(NTILE):
                    last = nc.vector.bn_aggr(mv[:, t, :], stats[:, t, :])
                last.then_inc(var_ready, 1)
                dve.wait_ge(std_ready, l + 1)
                link(nc.vector.reciprocal(rstd[:, :], std[:, :]))
                for t in range(NTILE):
                    nc.vector.tensor_scalar(xn[:, t, :], h[:, t, :], mv[:, t, 0:1], rstd[:, t:t + 1],
                                            ALU.subtract, ALU.mult).then_inc(xn_ready, 1)
                dve.wait_ge(xT_mm, l + 1)
                nc.vector.tensor_copy(xT[:, 0, :], PS[:, 0:2, :].rearrange("p b n -> p (b n)")[:, 0:NPAD]).then_inc(xT_lo, 1)

            def rank_of(score):
                sj = score.unsqueeze(2).broadcast_to([P, NTILE, 8, 8])
                se = score.unsqueeze(3).broadcast_to([P, NTILE, 8, 8])
                step(nc.vector.tensor_tensor(cmp_gt[:, :, :, :], sj, se, ALU.is_gt))
                link(nc.vector.tensor_tensor(cmp_eq[:, :, :, :], sj, se, ALU.is_equal))
                link(nc.vector.tensor_tensor(cmp_eq[:, :, :, :].rearrange("p t e j -> p t (e j)"),
                                             cmp_eq[:, :, :, :].rearrange("p t e j -> p t (e j)"),
                                             before[:, :, :].rearrange("p e j -> p (e j)").unsqueeze(1).broadcast_to([P, NTILE, 64]),
                                             ALU.mult))
                link(nc.vector.tensor_tensor(cmp_gt[:, :, :, :], cmp_gt[:, :, :, :], cmp_eq[:, :, :, :], ALU.add))
                link(nc.vector.tensor_reduce(rank[:, :, :], cmp_gt[:, :, :, :], AX.X, ALU.add))

            link(nc.vector.memset(h[:, NTILE - 1, :], 0.0))
            step(nc.vector.memset(zerosb[:, :], 0.0))
            for t in range(NTILE):
                dve.wait_ge(embed_mm, t + 1)
                step(nc.vector.tensor_copy(h[0:ROWS[t], t, :], PS[0:ROWS[t], t, 0:D]))
            settle()

            layernorm(0)
            dve.wait_ge(kv_mm, 1)
            link(nc.vector.tensor_copy(kv_sb.rearrange("p (b n) -> p b n", b=2), PS[0:R_KV, 0:2, 0:HALF]))
            step(nc.vector.memset(mx[:, :], 0.0))
            nc.vector.memset(rsum[:, :], 0.0).then_inc(kv_ready, 1)
            dve.wait_ge(rms_ready, 1)
            link(nc.vector.reciprocal(rrms, rms))
            dve.wait_ge(attn_in, 11 * 16)
            nc.vector.scalar_tensor_tensor(kvn, kv_sb, g_kv[:, 0:1], rrms, ALU.mult, ALU.mult).then_inc(kvn_ready, 1)

            def table(tab):
                return tab[:, :].unsqueeze(1).broadcast_to([P, 8, T])

            for idx in range(8):
                b0 = 4 * (idx % 2)
                dve.wait_ge(rope_mm, idx + 1)
                if idx:
                    dve.wait_ge(rope_done, idx)
                for j, (src, tab) in enumerate(((0, cosT), (2, sinT), (2, cosT), (0, sinT))):
                    for n in range(2):
                        last = nc.vector.tensor_tensor(
                            rt[:, j, n * HALF:(n + 1) * HALF].rearrange("p (b t) -> p b t", t=T),
                            PS[:, b0 + src + n, 0:HALF].rearrange("p (b t) -> p b t", t=T), table(tab), ALU.mult)
                last.then_inc(rope_read, 1)

            def shift_scores(g):
                rows = GROUPS[g][1]
                S = PS[0:rows, 0:4, 0:4 * GR].rearrange("p j (m n) -> p j m n", m=4)[:, :, :, 0:rows]
                dve.wait_ge(s_mm, g + 1)
                link(nc.vector.tensor_reduce(mx[0:rows, :].rearrange("p (j m) -> p j m", j=4), S, AX.X, ALU.max))
                if g:
                    dve.wait_ge(pt_mm, ticket[("P", g - 1, 3)] + 1)
                nc.vector.tensor_tensor(prob[0:rows, :, 0:rows].rearrange("p (j m) n -> p j m n", j=4), S,
                                        mx[0:rows, :].rearrange("p (j m) -> p j m", j=4).unsqueeze(3).broadcast_to([rows, 4, 4, rows]),
                                        ALU.subtract).then_inc(s_shift, 1)

            shift_scores(0)
            for g in range(NG):
                rows = GROUPS[g][1]
                if g + 1 < NG:
                    shift_scores(g + 1)
                dve.wait_ge(pv_mm, g + 1)
                O = PS[0:rows, 7, 0:NH * (HD + 1)].rearrange("p (h d) -> p h d", h=NH)
                link(nc.vector.reciprocal(rsum[0:rows, :], O[:, :, HD]))
                if g:
                    dve.wait_ge(pt_mm, ticket[("O", g - 1)] + 1)
                nc.vector.tensor_tensor(obuf[0:rows, :].rearrange("p (m j d) -> p j m d", m=4, j=4),
                                        O[:, :, 0:HD].rearrange("p (j m) d -> p j m d", j=4),
                                        rsum[0:rows, :].rearrange("p (j m) -> p j m", j=4).unsqueeze(3).broadcast_to([rows, 4, 4, HD]),
                                        ALU.mult).then_inc(o_ready, 1)
            for t in range(NTILE):
                dve.wait_ge(wo_mm, t + 1)
                step(nc.vector.tensor_tensor(h[0:ROWS[t], t, :], PS[0:ROWS[t], t, 0:D], h[0:ROWS[t], t, :], ALU.add))
            settle()

            layernorm(1)
            dve.wait_ge(r0_mm, 1)
            logits = PS[:, 7, 0:NTILE * 8].rearrange("p (t e) -> p t e", t=NTILE)

            def over_e(v, n=8):
                return v[:, :].unsqueeze(2).broadcast_to([P, NTILE, n])

            link(nc.vector.tensor_reduce(r5[:, :], logits, AX.X, ALU.max))
            nc.vector.tensor_tensor(lg0[:, :, :], logits, over_e(r5), ALU.subtract).then_inc(r0_shift, 1)
            dve.wait_ge(r0_exp, 1)
            link(nc.vector.tensor_reduce(r5[:, :], lg0[:, :, :], AX.X, ALU.add))
            link(nc.vector.reciprocal(r5[:, :], r5[:, :]))
            link(nc.vector.tensor_tensor(p0[:, :, :], lg0[:, :, :], over_e(r5), ALU.mult))
            dve.wait_ge(route_in, 10 * 16)
            rank_of(p0[:, :, :])
            step(nc.vector.memset(gates0[:, :, 0:1], 1.0))
            link(nc.vector.scalar_tensor_tensor(gates0[:, :, 1:E0], rank[:, :, :], float(K0), p0[:, :, :],
                                                ALU.is_lt, ALU.mult))
            for tiles in YG:
                a, b = tiles[0], tiles[-1] + 1
                nc.vector.tensor_tensor(h[:, a:b, :], h[:, a:b, :], xn[:, a:b, :], ALU.add).then_inc(y_taken, 1)
            with dve.Fori(0, E0 // SLOTS0) as i:
                for s in range(SLOTS0):
                    for grp, tiles in enumerate(YG):
                        dve.wait_ge(y_mm, i * (3 * SLOTS0) + (3 * s + grp + 1))
                        dve.wait_ge(y_taken, i * (3 * SLOTS0) + (3 * s + grp + 1))
                        for t in tiles:
                            g_col = gates0[0:ROWS[t], t, :][:, bass.ds(i * SLOTS0 + s, 1)]
                            last = nc.vector.scalar_tensor_tensor(
                                h[0:ROWS[t], t, :], PS[0:ROWS[t], 4 + grp, (t % 2) * D:(t % 2 + 1) * D], g_col,
                                h[0:ROWS[t], t, :], ALU.mult, ALU.add)
                        last.then_inc(y_taken, 1)
            dve.wait_ge(y_taken, 3 * E0 + 3)

            layernorm(2)
            dve.wait_ge(a_exp, 1)
            nc.vector.tensor_scalar(a_neg[:, :, :], a_neg[:, :, :], -1.0, None, ALU.mult).then_inc(a_ready, 1)
            nc.vector.memset(barA.rearrange("p r (b t) -> p r b t", b=B)[:, :, :, 0:1], 0.0).then_inc(ring_ready, 1)
            dve.wait_ge(dt_mm, 1)
            for c in range(2):
                for n, bank in enumerate((2 * c, 2 * c + 1)):
                    last = nc.vector.tensor_scalar(spb[:, c, n * HALF:(n + 1) * HALF], PS[:, bank, 0:HALF],
                                                   b_dt[:, c:c + 1], None, ALU.add)
            last.then_inc(sp_max, 1)
            dve.wait_ge(sp_max, 1)
            dve.wait_ge(sp_ln, 1)
            link(nc.vector.tensor_scalar(spb, spb, 0.0, None, ALU.max))
            link(nc.vector.tensor_tensor(spa, spa, spb, ALU.add))
            nc.vector.tensor_scalar(dt, spa, DT_MAX - DT_MIN, DT_MIN, ALU.mult, ALU.add).then_inc(dt_ready, 1)
            dve.wait_ge(dt_ready, 1)
            dve.wait_ge(u_ready, 1)
            nc.vector.tensor_tensor(dtu, dt, u, ALU.mult).then_inc(dtu_ready, 1)
            for c in range(2):
                last = nc.vector.tensor_scalar(du[:, c, :], u[:, c, :], d_p[:, c:c + 1], None, ALU.mult)
            last.then_inc(du_ready, 1)
            dve.wait_ge(g_mm, 1)
            dve.wait_ge(b_ready, 1)
            nc.vector.tensor_tensor(inpT.rearrange("p (b n) -> p b n", b=2), PS[0:NS, 6:8, 0:HALF],
                                    bT.rearrange("p (b n) -> p b n", b=2), ALU.mult).then_inc(inp_ready, 1)
            IB = PS[:, 3:5, :].rearrange("p b n -> p (b n)")[:, 0:NT]
            CB = PS[:, 5:7, :].rearrange("p b n -> p (b n)")[:, 0:NT]
            for n in range(NS):
                dve.wait_ge(ib_mm, n + 1)
                for c in range(2):
                    k = 2 * n + c
                    dve.wait_ge(barA_ready, k + 1)
                    if k >= 2:
                        dve.wait_ge(hc_ready, k - 1)
                    nc.vector.tensor_tensor_scan(hs[:, c, :], barA[:, k % BA, :], IB, 0.0, ALU.mult, ALU.add).then_inc(scanned, 1)
                dve.wait_ge(cb_mm, n + 1)
                for c in range(2):
                    k = 2 * n + c
                    dve.wait_ge(scanned, k + 1)
                    if k >= 4:
                        dve.wait_ge(hc_used, k - 3)
                    nc.vector.tensor_tensor(hc[:, k % 4, :], hs[:, c, :], CB, ALU.mult).then_inc(hc_ready, 1)
            dve.wait_ge(yscan_mm, 1)
            for t in range(NTILE):
                step(nc.vector.tensor_tensor(h[0:ROWS[t], t, :], PS[0:ROWS[t], t // 2, (t % 2) * D:(t % 2 + 1) * D],
                                             h[0:ROWS[t], t, :], ALU.add))
            settle()

            layernorm(3)

            def hidden(x):
                for n in range(2):
                    dve.wait_ge(silu_ready, x * 2 + (n + 1))
                    nc.vector.tensor_tensor(hT1[:, n * HALF:(n + 1) * HALF], silu_g[:, n, :], PS[:, 2 * n + 1, 0:HALF],
                                            ALU.mult).then_inc(hT_ready, 1)

            def add_output(x, gate):
                for grp, tiles in enumerate(YG):
                    dve.wait_ge(y1_mm, x * 3 + (grp + 1))
                    dve.wait_ge(y1_taken, x * 3 + (grp + 1))
                    for t in tiles:
                        y = PS[0:ROWS[t], 4 + grp, (t % 2) * D:(t % 2 + 1) * D]
                        if gate is None:
                            last = nc.vector.tensor_tensor(h[0:ROWS[t], t, :], y, h[0:ROWS[t], t, :], ALU.add)
                        else:
                            last = nc.vector.scalar_tensor_tensor(h[0:ROWS[t], t, :], y, gate(t), h[0:ROWS[t], t, :],
                                                                  ALU.mult, ALU.add)
                    last.then_inc(y1_taken, 1)

            for grp in range(3):
                nc.vector.memset(r5[:, grp:grp + 1], 0.0).then_inc(y1_taken, 1)
            dve.wait_ge(y1_taken, 3)
            dve.wait_ge(sig_ready, 1)
            link(nc.vector.tensor_tensor(sfc[:, :, :], scores[:, :, :],
                                         e_bias[:, :].unsqueeze(1).broadcast_to([P, NTILE, NR1]), ALU.add))
            for t in range(NTILE):
                for g in range(NGRP):
                    step(nc.vector.max(top8g[:, t * NGRP + g, :], sfc[:, t, 8 * g:8 * g + 8]))
            hidden(0)
            settle()
            link(nc.vector.tensor_tensor(gscore[:, :, :].rearrange("p t g -> p (t g)"), top8g[:, :, 0], top8g[:, :, 1], ALU.add))
            rank_of(gscore[:, :, :])
            link(nc.vector.tensor_scalar(gscore[:, :, :], rank[:, :, :], float(TOPG), None, ALU.is_lt))
            link(nc.vector.tensor_tensor(tmp[:, :, :].rearrange("p t (g e) -> p (t g) e", g=NGRP),
                                         sfc[:, :, :].rearrange("p t (g e) -> p (t g) e", g=NGRP),
                                         gscore[:, :, :].rearrange("p t g -> p (t g)").unsqueeze(2).broadcast_to([P, NTILE * NGRP, 8]),
                                         ALU.mult))
            for t in range(NTILE):
                step(nc.vector.max(top8[:, t, :], tmp[:, t, :]))
            settle()
            for t in range(NTILE):
                step(nc.vector.match_replace(tmp[:, t, :], top8[:, t, :], tmp[:, t, :], REMOVED))
            settle()
            link(nc.vector.tensor_scalar(chosen[:, :, :], tmp[:, :, :], REMOVED, None, ALU.is_equal))
            nc.vector.tensor_copy(chosenb[:, :, :], chosen[:, :, :]).then_inc(chosen_ready, 1)
            add_output(0, None)
            hidden(1)
            dve.wait_ge(count_mm, 1)
            step(nc.vector.tensor_scalar(active[:, :], PS[0:NR1, 6, 256:257], 0.0, None, ALU.is_gt))
            nc.vector.tensor_scalar(activeb[:, :], PS[0:NR1, 6, 256:257], 0.0, None, ALU.is_gt).then_inc(active_ready, 1)
            dve.wait_ge(place_mm, 1)
            link(nc.vector.tensor_copy(upto_n[:, :], PS[0:NR1, 6, 256:257]))
            nc.vector.tensor_scalar(onehot[:, :], place[:, :], upto_n[:, 0:1], active[:, 0:1], ALU.is_equal,
                                    ALU.mult).then_inc(onehot_ready, 1)
            link(nc.vector.tensor_tensor(scores[:, :, :], scores[:, :, :], chosen[:, :, :], ALU.mult))
            link(nc.vector.tensor_reduce(r5[:, :], scores[:, :, :], AX.X, ALU.add))
            dve.wait_ge(lists_mm, 1)
            step(nc.vector.tensor_copy(lists[:, 0:2 * NI], PS[0:1, 6, 256:256 + 2 * NI]))
            link(nc.vector.tensor_reduce(counts[:, 0:1], PS[0:1, 7, 384:384 + NI].rearrange("p (i s) -> p i s", s=SLOTS1)[:, :, 0],
                                         AX.X, ALU.add))
            nc.vector.tensor_scalar(lists[:, 2 * NI:2 * NI + 1], counts[:, 0:1], 2.0, None, ALU.max).then_inc(lists_ready, 1)
            add_output(1, None)
            link(nc.vector.tensor_scalar(r5[:, :], r5[:, :], 1e-20, None, ALU.add))
            link(nc.vector.reciprocal(r5[:, :], r5[:, :]))
            link(nc.vector.tensor_tensor(scores[:, :, :], scores[:, :, :], over_e(r5, NR1), ALU.mult))
            link(nc.vector.tensor_scalar(scores[:, :, :], scores[:, :, :], SCALE1, None, ALU.mult))
            dve.wait_ge(pos_mm, 1)
            earlier = PS[:, 7, 0:NTILE * NR1].rearrange("p (t e) -> p t e", t=NTILE)
            step(nc.vector.memset(gates1[:, :, 0:1], 0.0))
            link(nc.vector.scalar_tensor_tensor(gates1[:, :, 1:NR1 + 1], earlier, float(CAP), scores[:, :, :],
                                                ALU.is_lt, ALU.mult))
            dve.wait_ge(lists_ready, 1)
            iters = dve.value_load(lists[0:1, 2 * NI:2 * NI + 1], min_val=2, max_val=-(-NR1 // SLOTS1))
            with dve.Fori(0, iters) as i:
                for s in range(SLOTS1):
                    col = dve.value_load(lists[0:1, bass.ds(i * SLOTS1 + (NI + s), 1)], min_val=0, max_val=NR1)
                    hidden(i * SLOTS1 + (2 + s))
                    add_output(i * SLOTS1 + (2 + s), lambda t: gates1[0:ROWS[t], t, :][:, bass.ds(col, 1)])

        @block.tensor
        def _(pe):
            mm = nc.tensor.matmul

            def transpose_xn(l):
                if l == 0:
                    pe.wait_ge(ident_in, 16)
                for t in range(NTILE):
                    pe.wait_ge(xn_ready, NTILE * l + t + 1)
                    for c in range(2):
                        last = nc.tensor.transpose(PS[:, 2 * c + t // 4, (t % 4) * P:(t % 4 + 1) * P],
                                                   xn[:, t, c * P:(c + 1) * P], ident[:, :])
                last.then_inc(xT_mm, 1)
                pe.wait_ge(xT_lo, l + 1)
                pe.wait_ge(xT_hi, l + 1)

            def half(n):
                return slice(n * HALF, (n + 1) * HALF)

            for k in range(KP):
                pe.wait_ge(patch_in[k], 32)
                for t in range(NTILE):
                    mm(PS[0:ROWS[t], t, 0:D], patches[:, k, t * P:t * P + ROWS[t]], wtok[:, k, :], start=(k == 0), stop=False)
            pe.wait_ge(pos_in, 32)
            for t in range(NTILE):
                mm(PS[0:ROWS[t], t, 0:D], rowsel[:, t * P:t * P + ROWS[t]], posb, start=False, stop=True).then_inc(embed_mm, 1)

            transpose_xn(0)
            pe.wait_ge(attn_in, 11 * 16)
            for n in range(2):
                for c in range(2):
                    last = mm(PS[0:R_KV, n, 0:HALF], wkv[:, c, :], xT[:, c, half(n)], start=c == 0, stop=c == 1)
            last.then_inc(kv_mm, 1)
            for n in range(2):
                for c in range(2):
                    last = mm(PS[:, 2 + n, 0:HALF], wq[:, c, :], xT[:, c, half(n)], start=c == 0, stop=c == 1)
            last.then_inc(qc_mm, 1)
            pe.wait_ge(sq_ready, 1)
            for n in range(2):
                last = mm(PS[0:R_KV, 4 + n, 0:HALF], ones64[:, :], sq[:, half(n)], start=True, stop=True)
            last.then_inc(ms_mm, 1)
            pe.wait_ge(qc_ready, 1)
            pe.wait_ge(attn2_in, 4 * 16)
            for idx in range(8):
                which, m, b0 = idx // 4, idx % 4, 4 * (idx % 2)
                if idx == 1:
                    pe.wait_ge(rms_ready, 1)
                if idx >= 2:
                    pe.wait_ge(rope_read, idx - 1)
                if idx == 4:
                    pe.wait_ge(kvn_ready, 1)
                for n in range(2):
                    if which == 0:
                        mm(PS[:, b0 + n, 0:HALF], wqa[:, m, :], qc[:, half(n)], start=True, stop=True)
                        last = mm(PS[:, b0 + 2 + n, 0:HALF], wqb[:, m, :], qc[:, half(n)], start=True, stop=True)
                    else:
                        mm(PS[:, b0 + n, 0:HALF], wkac[:, m, :], kvn[:, half(n)], start=True, stop=False)
                        for c in range(2):
                            mm(PS[:, b0 + n, 0:HALF], wkar[:, c, m, :], xT[:, c, half(n)], start=False, stop=c == 1)
                        for c in range(2):
                            last = mm(PS[:, b0 + 2 + n, 0:HALF], wkbr[:, c, m, :], xT[:, c, half(n)], start=c == 0, stop=c == 1)
                last.then_inc(rope_mm, 1)
            pe.wait_ge(rope_read, 8)
            for g, (c0, rows) in enumerate(GROUPS):
                last = mm(PS[0:rows, 4 + g // 2, (g % 2) * D:(g % 2 + 1) * D], kvn[:, c0:c0 + rows], wvdec[:, :],
                          start=True, stop=True)
                if g % 2:
                    last.then_inc(v_mm, 1)
            pe.wait_ge(rope_done, 8)

            def scores_of(g):
                c0, rows = GROUPS[g]
                if g:
                    pe.wait_ge(s_shift, g)
                for j in range(4):
                    S = PS[0:rows, j, 0:4 * GR].rearrange("p (m n) -> p m n", m=4)
                    for m in range(4):
                        for ab in range(2):
                            mm(S[:, m, 0:rows], qk[32 * j:32 * j + 32, 0, m, ab, c0:c0 + rows],
                               qk[32 * j:32 * j + 32, 1, m, ab, c0:c0 + rows], start=(m == 0 and ab == 0), stop=False,
                               skip_group_check=True)
                    last = mm(S[:, :, 0:rows], identb[0:rows, 0:rows], maskb[0:rows, :, 0:rows], start=False, stop=True,
                              skip_group_check=True)
                last.then_inc(s_mm, 1)

            def take_ticket(key):
                k = ticket[key]
                if k >= 3:
                    pe.wait_ge(pt_ready, k - 2)
                return PS[:, 4 + k % 3, :]

            def transpose_o(g):
                rows = GROUPS[g][1]
                bank = take_ticket(("O", g))
                pe.wait_ge(o_ready, g + 1)
                for c in range(2):
                    last = nc.tensor.transpose(bank[:, c * GR:c * GR + rows], obuf[0:rows, c * P:(c + 1) * P], ident[0:rows, 0:rows])
                last.then_inc(pt_mm, 1)

            scores_of(0)
            pe.wait_ge(v_ready, 3)
            for g in range(NG):
                rows = GROUPS[g][1]
                if g + 1 < NG:
                    scores_of(g + 1)
                if g:
                    transpose_o(g - 1)
                pe.wait_ge(p_ready, g + 1)
                for q in range(4):
                    bank = take_ticket(("P", g, q))
                    for x in range(4):
                        last = nc.tensor.transpose(bank[0:rows, x * GR:x * GR + rows], prob[0:rows, 4 * q + x, 0:rows],
                                                   ident[0:rows, 0:rows])
                    last.then_inc(pt_mm, 1)
                if g:
                    pe.wait_ge(o_ready, g)
                for hh in range(NH):
                    if hh % 4 == 0:
                        pe.wait_ge(pt_ready, ticket[("P", g, hh // 4)] + 1)
                    j, m = hh // 4, hh % 4
                    last = mm(PS[0:rows, 7, hh * (HD + 1):(hh + 1) * (HD + 1)], probT[0:rows, hh, 0:rows],
                              vext[0:rows, g, 4 * m + j, :], start=True, stop=True)
                last.then_inc(pv_mm, 1)
            transpose_o(NG - 1)
            pe.wait_ge(pt_ready, ticket[("O", NG - 1)] + 1)
            for t in range(NTILE):
                for c in range(2):
                    last = mm(PS[0:ROWS[t], t, 0:D], OT[:, c, t * P:t * P + ROWS[t]], wo[:, c, :], start=c == 0, stop=c == 1)
                last.then_inc(wo_mm, 1)

            transpose_xn(1)
            pe.wait_ge(route_in, 10 * 16)
            for t in range(NTILE):
                for c in range(2):
                    last = mm(PS[:, 7, 8 * t:8 * t + 8], xT[:, c, t * P:(t + 1) * P], rw0[:, c, :], start=c == 0, stop=c == 1)
            last.then_inc(r0_mm, 1)
            with pe.Fori(0, E0 // SLOTS0) as i:
                for s in range(SLOTS0):
                    pe.wait_ge(up_in[s], i * 16 + 16)
                    for f in range(FT0):
                        z = f % 2
                        if f >= 2:
                            pe.wait_ge(gelu_done, i * (SLOTS0 * FT0) + (s * FT0 + f - 1))
                        for n in range(2):
                            for c in range(2):
                                last = mm(PS[:, 2 * z + n, 0:HALF], w0up[:, s, c, f * P:(f + 1) * P], xT[:, c, half(n)],
                                          start=c == 0, stop=c == 1)
                        last.then_inc(up_mm, 1)
                    pe.wait_ge(dn_in[s], i * 16 + 16)
                    for grp, tiles in enumerate(YG):
                        pe.wait_ge(y_taken, i * (3 * SLOTS0) + (3 * s + grp + 1))
                        for t in tiles:
                            for f in range(FT0):
                                if t == 0:
                                    pe.wait_ge(gelu_done, i * (SLOTS0 * FT0) + (s * FT0 + f + 1))
                                last = mm(PS[0:ROWS[t], 4 + grp, (t % 2) * D:(t % 2 + 1) * D],
                                          hT0[:, f, t * P:t * P + ROWS[t]], w0dn[:, s, f, :], start=f == 0, stop=f == FT0 - 1)
                        last.then_inc(y_mm, 1)

            transpose_xn(2)
            pe.wait_ge(scan_in, 7 * 16)
            for c in range(2):
                for n in range(2):
                    for k in range(2):
                        last = mm(PS[:, 2 * c + n, 0:HALF], w_in[:, k, c * P:(c + 1) * P], xT[:, k, half(n)], start=k == 0, stop=k == 1)
            last.then_inc(u_mm, 1)
            pe.wait_ge(u_ready, 1)

            def project(bank, rows, w, done):
                for n in range(2):
                    for k in range(2):
                        last = mm(PS[0:rows, bank + n, 0:HALF], w_x[:, k, w:w + rows], u[:, k, half(n)], start=k == 0, stop=k == 1)
                last.then_inc(done, 1)

            project(4, R_DT, 0, dtl_mm)
            project(6, NS, R_DT, b_mm)
            pe.wait_ge(dtl_ready, 1)
            for c in range(2):
                for n in range(2):
                    last = mm(PS[:, 2 * c + n, 0:HALF], w_dt[:, c * P:(c + 1) * P], dtl[:, half(n)], start=True, stop=True)
            last.then_inc(dt_mm, 1)
            project(4, NS, R_DT + NS, c_mm)
            pe.wait_ge(b_ready, 1)
            pe.wait_ge(a_ready, 1)
            pe.wait_ge(dtu_ready, 1)
            for n in range(2):
                for k in range(2):
                    last = mm(PS[0:NS, 6 + n, 0:HALF], a_neg[:, k, :], dtu[:, k, half(n)], start=k == 0, stop=k == 1)
            last.then_inc(g_mm, 1)
            for bank in range(3):
                mm(PS[:, bank, :], zerosb[:, 0:P], zerosb[:, :], start=True, stop=False, skip_group_check=True)
            pe.wait_ge(du_ready, 1)

            def add_to_y(src, c):
                for t in range(NTILE):
                    last = mm(PS[0:ROWS[t], t // 2, (t % 2) * D + c * P:(t % 2) * D + (c + 1) * P],
                              src[:, t * P:t * P + ROWS[t]], ident[:, :], start=False, stop=False, skip_group_check=True)
                return last

            def broadcast(bank, row, n, done):
                mm(PS[:, bank, 0:512], sel[:, n, :], row[:, 0:512], start=True, stop=True)
                mm(PS[:, bank + 1, 0:NT - 512], sel[:, n, :], row[:, 512:NT], start=True, stop=True).then_inc(done, 1)

            for c in range(2):
                add_to_y(du[:, c, :], c)
            pe.wait_ge(c_ready, 1)
            pe.wait_ge(inp_ready, 1)
            for n in range(NS):
                if n:
                    pe.wait_ge(scanned, 2 * n)
                broadcast(3, inpT, n, ib_mm)
                if n:
                    pe.wait_ge(hc_ready, 2 * n)
                broadcast(5, cT, n, cb_mm)
                if n:
                    for c in range(2):
                        add_to_y(hc[:, (2 * (n - 1) + c) % 4, :], c).then_inc(hc_used, 1)
            pe.wait_ge(hc_ready, 2 * NS)
            for c in range(2):
                add_to_y(hc[:, (2 * (NS - 1) + c) % 4, :], c)
            for bank in range(3):
                last = mm(PS[:, bank, :], zerosb[:, 0:P], zerosb[:, :], start=False, stop=True, skip_group_check=True)
            last.then_inc(yscan_mm, 1)

            transpose_xn(3)
            for t in range(NTILE):
                for c in range(2):
                    last = mm(PS[:, 7, NR1 * t:NR1 * (t + 1)], xT[:, c, t * P:(t + 1) * P], gw1[:, c, :], start=c == 0, stop=c == 1)
            last.then_inc(r1_mm, 1)

            def expert_up(s, x):
                for n in range(2):
                    for j in range(2):
                        for c in range(2):
                            w = (2 * j + c) * F1
                            last = mm(PS[:, 2 * n + j, 0:HALF], w1s[:, s, w:w + F1], xT[:, c, half(n)], start=c == 0, stop=c == 1)
                    last.then_inc(gu_mm, 1)

            def expert_down(s, x):
                for grp, tiles in enumerate(YG):
                    pe.wait_ge(hT_ready, x * 2 + (1 if grp == 0 else 2))
                    pe.wait_ge(y1_taken, x * 3 + (grp + 1))
                    for t in tiles:
                        last = mm(PS[0:ROWS[t], 4 + grp, (t % 2) * D:(t % 2 + 1) * D],
                                  hT1[:, t * P:t * P + ROWS[t]], w1s[:, s, 4 * F1:4 * F1 + D], start=True, stop=True)
                    last.then_inc(y1_mm, 1)

            for x in range(2):
                pe.wait_ge(w1_in[x], 16)
                expert_up(x, x)
                expert_down(x, x)
            pe.wait_ge(sig_ready, 1)
            pe.wait_ge(chosen_ready, 1)
            pe.wait_ge(y1_taken, 6)
            for t in range(NTILE):
                last = mm(PS[0:NR1, 6, 256:257], chosenb[:, t, :], validb[:, t:t + 1], start=t == 0, stop=t == NTILE - 1)
            last.then_inc(count_mm, 1)
            for t in range(NTILE):
                for s in range(t):
                    mm(PS[:, 7, NR1 * t:NR1 * (t + 1)], onesb[:, :], chosenb[:, s, :], start=s == 0, stop=False)
                last = mm(PS[:, 7, NR1 * t:NR1 * (t + 1)], upperb[:, :], chosenb[:, t, :], start=t == 0, stop=True)
            last.then_inc(pos_mm, 1)
            pe.wait_ge(active_ready, 1)
            mm(PS[0:NR1, 6, 256:257], upto[:, :], activeb[:, :], start=True, stop=True).then_inc(place_mm, 1)
            pe.wait_ge(onehot_ready, 1)
            for k in range(2):
                mm(PS[0:1, 6, 256 + k * NI:256 + (k + 1) * NI], numbers[:, k:k + 1], onehot[:, :], start=True, stop=True)
            mm(PS[0:1, 7, 384:384 + NI], numbers[:, 2:3], onehot[:, :], start=True, stop=True).then_inc(lists_mm, 1)
            pe.wait_ge(lists_ready, 1)
            iters = pe.value_load(lists[0:1, 2 * NI:2 * NI + 1], min_val=2, max_val=-(-NR1 // SLOTS1))
            with pe.Fori(0, iters) as i:
                for s in range(SLOTS1):
                    pe.wait_ge(w1_in[s], i * 16 + (32 if s < 2 else 16))
                    expert_up(s, None)
                    expert_down(s, i * SLOTS1 + (2 + s))


ticket = {}
for _g in range(NG):
    if _g:
        ticket[("O", _g - 1)] = len(ticket)
    for _q in range(4):
        ticket[("P", _g, _q)] = len(ticket)
ticket[("O", NG - 1)] = len(ticket)


def shape_constants():
    bf = np.dtype("bfloat16")
    f = np.float32
    rowsel = np.zeros((T + 2, NT), f)
    n = np.arange(NT)
    rowsel[n % T, n] = 1
    rowsel[T, n] = n % T == 0
    rowsel[T + 1, n] = n % T != 0
    r = np.arange(GR)
    ok = (r[:, None] // T == r[None, :] // T) & (r[None, :] <= r[:, None])
    inv = (1.0 / 10000.0 ** (np.arange(0, RD, 2, dtype=np.float32) / RD)).astype(f)
    fr = np.outer(np.arange(T, dtype=f), inv).astype(f)
    cosT, sinT = np.ones((P, T), f), np.zeros((P, T), f)
    for j in range(4):
        cosT[32 * j + 16:32 * j + 32] = np.cos(fr).T
        sinT[32 * j + 16:32 * j + 32] = np.sin(fr).T
    sel = np.zeros((NS, NS, P), f)
    sel[np.arange(NS), np.arange(NS)] = 1
    before = np.broadcast_to(np.tril(np.ones((8, 8), f), -1), (P, 8, 8))
    valid = (np.arange(NPAD) < NT).astype(f).reshape(NTILE, P).T
    e = np.arange(NR1, dtype=f)
    return dict(validb=valid.astype(bf), upto=np.triu(np.ones((NR1, NR1), f)).astype(bf),
                place=np.ascontiguousarray(np.broadcast_to(np.arange(1, NI + 1, dtype=f), (NR1, NI))),
                numbers=np.stack([e, e + 1, np.ones(NR1, f)], 1),
                rowsel=rowsel, ident=np.eye(P, dtype=f), identb=np.eye(P, dtype=f).astype(bf),
                onesb=np.ones((P, P), bf), upperb=np.triu(np.ones((P, P), f), 1).astype(bf),
                maskb=np.ascontiguousarray(np.broadcast_to(np.where(ok, 0.0, MASKED).astype(f)[:, None, :], (GR, 4, GR))).astype(bf),
                ones64=np.full((R_KV, R_KV), 1.0 / R_KV, f), cosT=cosT, sinT=sinT, sel=sel,
                before=np.ascontiguousarray(before))


def rows_first(w, k=P):
    return w.reshape(w.shape[0] // k, k, w.shape[1]).transpose(1, 0, 2)


def head_quads(w, width, parts):
    o = np.zeros((w.shape[0], 4, 4, 32), w.dtype)
    w4 = w.reshape(w.shape[0], 4, 4, width)
    for (a, b), at in parts:
        o[:, :, :, at:at + b - a] = w4[:, :, :, a:b]
    return o.reshape(w.shape[0], 4, 128)


def kernel(**inputs):
    import concourse.bacc as bacc
    from concourse.bass_utils import run_bass_kernel_spmd

    I = {k: np.asarray(v) for k, v in inputs.items()}
    a = {}
    x = I["x"].reshape(B, 3, 6, 16, 6, 16).transpose(1, 3, 5, 0, 2, 4).reshape(768, B, 36)
    px = np.zeros((768, B, T), x.dtype)
    px[:, :, 1:] = x
    a["patchesT"] = px.reshape(KP, P, NT)
    a["W_tok"] = I["L0_tok_W"].T.reshape(KP, P, D)
    a["posb"] = np.concatenate([I["L0_tok_pos_embed"][0], I["L0_tok_cls_token"][0], I["L0_tok_b"][None]], 0)
    a["wkv"] = rows_first(I["L0_attn_W_kv"])
    a["wq"] = rows_first(I["L0_attn_W_q"])
    a["g_kv"] = I["L0_attn_g_kv"].reshape(R_KV, 1)
    a["wo"] = rows_first(I["L0_attn_W_o"])
    a["wvdec"] = I["L0_attn_W_vdec"]
    a["wkac"] = head_quads(I["L0_attn_W_kdec"], HD, [((0, 16), 0)])
    kr = I["L0_attn_W_krope"]
    a["wkar"] = head_quads(kr, RD, [((0, 16), 16)]).reshape(2, P, 4, P).transpose(1, 0, 2, 3)
    a["wkbr"] = head_quads(kr, RD, [((16, 32), 16)]).reshape(2, P, 4, P).transpose(1, 0, 2, 3)
    qr = I["L0_attn_W_qrope"]
    wqa = head_quads(I["L0_attn_W_qdec"], HD, [((0, 16), 0)]).reshape(R_Q, 4, 4, 32)
    wqa[..., 16:] = head_quads(qr, RD, [((0, 16), 16)]).reshape(R_Q, 4, 4, 32)[..., 16:]
    a["wqa"] = wqa.reshape(R_Q, 4, P)
    a["wqb"] = head_quads(qr, RD, [((16, 32), 16)])
    a["rw0"] = rows_first(I["L0_ffn_router_w"])
    up = np.concatenate([I["L0_ffn_shared_up"], I["L0_ffn_routed_up"]], 0)
    dn = np.concatenate([I["L0_ffn_shared_down"], I["L0_ffn_routed_down"]], 0)
    a["w0up"] = up.reshape(E0, 2, P, F0).transpose(0, 2, 1, 3)
    a["w0dn"] = dn.reshape(E0, FT0, P, D).transpose(0, 2, 1, 3)
    a["w_in"] = rows_first(I["L1_attn_w_in"])
    a["w_x"] = rows_first(I["L1_attn_w_x"])
    a["w_dt"] = I["L1_attn_w_dt"]
    a["b_dt"] = I["L1_attn_b_dt"].reshape(2, P).T
    a["a_log"] = rows_first(I["L1_attn_A_log"])
    a["d_p"] = I["L1_attn_Dp"].reshape(2, P).T
    a["gw1"] = rows_first(I["L1_ffn_gate_weight"].T)
    a["e_bias"] = np.broadcast_to(I["L1_ffn_e_bias"], (P, NR1))
    sg, su, sd = (I["L1_ffn_shared_" + k] for k in ("gate", "up", "down"))
    w1 = np.concatenate([I["L1_ffn_w1"], sg.reshape(2, F1, D)], 0)
    w3 = np.concatenate([I["L1_ffn_w3"], su.reshape(2, F1, D)], 0)
    w2 = np.concatenate([I["L1_ffn_w2"], sd.reshape(D, 2, F1).transpose(1, 0, 2)], 0)

    def gated(w):
        return w.transpose(0, 2, 1).reshape(E1, 2, P, F1).transpose(0, 2, 1, 3).reshape(E1, P, 2 * F1)
    a["w1"] = np.concatenate([gated(w1), gated(w3), w2.transpose(0, 2, 1)], 2)
    a.update(shape_constants())

    nc = bacc.Bacc("TRN2", target_bir_lowering=False, num_devices=1)
    arrays, aps = {}, {}
    for name, v in a.items():
        v = np.ascontiguousarray(v)
        arrays[f"in_{name}"] = v
        aps[name] = nc.dram_tensor(f"in_{name}", v.shape, mybir.dt.from_np(v.dtype), kind="ExternalInput").ap()
    out = nc.dram_tensor("out_0", (NT, D), F32, kind="ExternalOutput").ap()
    vit_tower(nc, aps, out)
    r = run_bass_kernel_spmd(nc, [arrays], core_ids=[0])
    return np.asarray(r.results[0]["out_0"]).reshape(B, T, D)
```

```python
from contextlib import ExitStack

import numpy as np
import concourse.bass as bass
from concourse import mybir

F32 = mybir.dt.float32
BF16 = mybir.dt.bfloat16
ALU = mybir.AluOpType
ACT = mybir.ActivationFunctionType
AX = mybir.AxisListType

P = 128
B = 16
T = 37
NT = B * T
NTILE = -(-NT // P)
ROWS = [min(P, NT - P * t) for t in range(NTILE)]
NPAD = NTILE * P
HALF = NT // 2
D = 256
KP = 768 // P
LN_EPS = 1e-5
RMS_EPS = 1e-6

NH, HD, RD = 16, 16, 32
R_KV, R_Q = 64, 128
SCALE = float(HD + RD) ** -0.5
IMGS = 3
GR = IMGS * T
GROUPS = [(g * GR, min(GR, NT - g * GR)) for g in range(-(-NT // GR))]
NG = len(GROUPS)
MASKED = -1e30

SCR_ROPE = 16 * NT + NG * NH * 32 + 4 * NT + 2 * NT + 4 * P

E0, F0 = 9, 1024
FT0 = F0 // P
K0 = 2
SLOTS0 = 2
SHARED = SLOTS0
TS = 2 * P
ITEMS0 = (K0 * NT + (E0 - 1) * (TS - 1)) // TS
CHUNKS = -(-NT // TS)

NS = 16
R_DT = 64
DT_MIN, DT_MAX = 0.001, 0.1

E1, F1 = 66, 128
NR1, NGRP, TOPG, TOPK = 64, 8, 4, 8
CAP = 256
SCALE1 = 2.5
SLOTS1 = 3
NI = 72
W1C = 2 * 2 * F1 + D
REMOVED = -3e38


def vit_tower(nc, A, out):
    ctx = ExitStack()
    with ctx:
        def sb(name, shape, dt=F32):
            return ctx.enter_context(nc.sbuf_tensor(name, shape, dt))

        def sem(name):
            return ctx.enter_context(nc.semaphore(name))

        PS = ctx.enter_context(nc.psum_tensor("PS", [P, 8, 512], F32))

        h = sb("h", [P, NTILE, D])
        xn = sb("xn", [P, NTILE, D])
        xT = sb("xT", [P, 2, NPAD])
        stats = sb("stats", [P, NTILE, 6])
        mv = sb("mv", [P, NTILE, 2])
        std = sb("std", [P, NTILE])
        rstd = sb("rstd", [P, NTILE])
        ident = sb("ident", [P, P])
        identb = sb("identb", [P, P], BF16)
        onesb = sb("onesb", [P, P], BF16)
        upperb = sb("upperb", [P, P], BF16)
        maskb = sb("maskb", [GR, 4, GR], BF16)
        ones64 = sb("ones64", [R_KV, R_KV])
        before = sb("before", [P, 8, 8])
        cosT = sb("cosT", [P, T])
        sinT = sb("sinT", [P, T])
        sel = sb("sel", [3 * 32, NS, P], BF16)

        wkv = sb("wkv", [P, 2, R_KV])
        wq = sb("wq", [P, 2, R_Q])
        g_kv = sb("g_kv", [R_KV, 1])
        wo = sb("wo", [P, 4, D])
        wvdec = sb("wvdec", [R_KV, D])
        w_in = sb("w_in", [P, 2, D])
        w_x = sb("w_x", [P, 2, R_DT + 2 * NS])
        w_dt = sb("w_dt", [R_DT, D])
        b_dt = sb("b_dt", [P, 2])
        a_log = sb("a_log", [P, 2, NS])
        d_p = sb("d_p", [P, 2])
        rw0 = sb("rw0", [P, 2, 8])
        gw1 = sb("gw1", [P, 2, NR1])
        e_bias = sb("e_bias", [P, NR1])

        SCR = 22800
        scratch = sb("scratch", [P, SCR])

        def views(*shapes):
            at, out_ = 0, []
            for rows, shape in shapes:
                n = int(np.prod(shape))
                v = scratch[0:rows, at:at + n]
                if len(shape) > 1:
                    names = "abcd"[:len(shape)]
                    v = v.rearrange(f"p ({' '.join(names)}) -> p {' '.join(names)}",
                                    **{c: s for c, s in zip(names[1:], shape[1:])})
                out_.append(v)
                at += n
            assert at <= SCR, at
            return out_

        w0up = sb("w0up", [P, SLOTS0 + 1, 2, F0])
        w0dn = sb("w0dn", [P, SLOTS0 + 1, FT0, D])
        w0flat = w0up[:, :, :, :].rearrange("p s c f -> p (s c f)")
        patches = w0flat[:, 0:KP * NT].rearrange("p (k n) -> p k n", k=KP)
        wtok = w0dn[:, 0, 0:KP, :]
        rowsel = w0dn[0:T + 2, 1, 0:3, :].rearrange("p a b -> p (a b)")[:, 0:NT]
        posb = w0dn[0:T + 2, 2, 0, :]
        (qk, vpad, OT, kvn, qc, wkac, rt) = views(
            (P, (2, 4, 2, NT)), (GR, (NG, NH, 32)), (P, (4, NT)), (R_KV, (NT,)), (P, (NT,)), (R_KV, (4, P)),
            (P, (2, 4, NT)))
        rope_at = SCR_ROPE
        prob = scratch[0:GR, rope_at:rope_at + 3 * 8 * GR].rearrange("p (b h n) -> p b h n", b=3, h=8)
        probT = scratch[0:GR, rope_at + 3 * 8 * GR:rope_at + 5 * 8 * GR].rearrange("p (b h n) -> p b h n", b=2, h=8)
        kv_sb, sq, rms, rrms = (w0flat[0:R_KV, 3072 + k * NT:3072 + (k + 1) * NT] for k in range(4))
        wkar = w0flat[:, 0:1024].rearrange("p (c m n) -> p c m n", c=2, m=4)
        wkbr = w0flat[:, 1024:2048].rearrange("p (c m n) -> p c m n", c=2, m=4)
        wqa = w0flat[:, 2048:2560].rearrange("p (m n) -> p m n", m=4)
        wqb = w0flat[:, 2560:3072].rearrange("p (m n) -> p m n", m=4)
        mx = sb("mx", [GR, NH])
        rsum = sb("rsum", [GR, NH])
        (hT0, xe, xeT, ysb, yg) = views((P, (FT0, NT)), (P, (SLOTS0, 2 * D)), (P, (2, 2, TS)), (P, (2, 2 * D)),
                                        (P, (K0, NTILE, D)))
        by_expert = nc.dram_tensor("by_expert", (ITEMS0 + SLOTS0, 2, P, D), F32, kind="Internal").ap()
        zeros = sb("zeros", [P, D])
        chosen0b = sb("chosen0b", [P, NTILE, 8], BF16)
        nitems = sb("nitems", [P, 8])
        upto_items = sb("upto_items", [P, 8])
        first_slot = sb("first_slot", [P, 8])
        ones8 = sb("ones8", [P, 8])
        slot_of = sb("slot_of", [P, NTILE, 8])
        slots8 = sb("slots8", [P, NTILE, 8])
        slots = sb("slots", [P, K0, NTILE], mybir.dt.uint32)
        gate_k = sb("gate_k", [P, K0, NTILE])
        item_cmp = sb("item_cmp", [1, ITEMS0 + SLOTS0, 8])
        place2 = sb("place2", [1, ITEMS0 // SLOTS0])
        item_e = sb("item_e", [1, ITEMS0 + SLOTS0])
        items = sb("items", [1, ITEMS0 + SLOTS0 + 1], mybir.dt.int32)
        lg0 = sb("lg0", [P, NTILE, 8])
        p0 = sb("p0", [P, NTILE, 8])
        r5 = sb("r5", [P, NTILE])
        cmp_gt = sb("cmp_gt", [P, NTILE, 8, 8])
        cmp_eq = sb("cmp_eq", [P, NTILE, 8, 8])
        rank = sb("rank", [P, NTILE, 8])
        BA = 4
        (u, dt, dtu, spa, spb, bT, cT, dtl, inpT, rest, barA, hs, hc, du) = views(
            (P, (2, NT)), (P, (2, NT)), (P, (2, NT)), (P, (2, NT)), (P, (2, NT)),
            (NS, (NT,)), (NS, (NT,)), (R_DT, (NT,)), (NS, (NT,)), (NS, (2, NT)),
            (P, (BA, NT)), (P, (2, NT)), (P, (4, NT)), (P, (2, NT)))
        inp3 = sb("inp3", [96, NT], BF16)
        c3 = sb("c3", [96, NT], BF16)
        mid_b = sb("mid_b", [NS, NT], BF16)
        a_neg = sb("a_neg", [P, 2, NS])
        zerosb = sb("zerosb", [P, 512], BF16)
        w1s = sb("w1s", [P, SLOTS1, W1C])
        (silu_g, hT1) = views((P, (2, HALF)), (P, (NT,)))
        scores = sb("scores", [P, NTILE, NR1])
        sfc = sb("sfc", [P, NTILE, NR1])
        top8g = sb("top8g", [P, NTILE * NGRP, 8])
        gscore = sb("gscore", [P, NTILE, NGRP])
        tmp = sb("tmp", [P, NTILE, NR1])
        top8 = sb("top8", [P, NTILE, 8])
        chosen = sb("chosen", [P, NTILE, NR1])
        chosenb = sb("chosenb", [P, NTILE, NR1], BF16)
        gates1 = sb("gates1", [P, NTILE, NR1 + 1])
        validb = sb("validb", [P, NTILE], BF16)
        upto = sb("upto", [NR1, NR1], BF16)
        place = sb("place", [NR1, NI])
        numbers = sb("numbers", [NR1, 3])
        active = sb("active", [NR1, 1])
        activeb = sb("activeb", [NR1, 1], BF16)
        upto_n = sb("upto_n", [NR1, 1])
        onehot = sb("onehot", [NR1, NI])
        counts = sb("counts", [1, 1])
        lists = sb("lists", [1, 2 * NI + 1], mybir.dt.int32)

        patch_in = [sem(f"patch_in{k}") for k in range(KP)]
        pos_in = sem("pos_in")
        ident_in = sem("ident_in")
        attn_in = sem("attn_in")
        attn2_in = sem("attn2_in")
        route_in = sem("route_in")
        scan_in = sem("scan_in")
        embed_mm = sem("embed_mm")
        dve_step = sem("dve_step")
        act_step = sem("act_step")
        var_ready = sem("var_ready")
        std_ready = sem("std_ready")
        xn_ready = sem("xn_ready")
        xT_mm = sem("xT_mm")
        xT_lo = sem("xT_lo")
        xT_hi = sem("xT_hi")
        kv_mm, kv_ready, sq_ready, ms_mm, rms_ready, kvn_ready = (
            sem(n) for n in ("kv_mm", "kv_ready", "sq_ready", "ms_mm", "rms_ready", "kvn_ready"))
        qc_mm, qc_ready = sem("qc_mm"), sem("qc_ready")
        rope_mm, rope_read, rope_done = sem("rope_mm"), sem("rope_read"), sem("rope_done")
        v_mm, v_ready, v_ones = sem("v_mm"), sem("v_ready"), sem("v_ones")
        s_mm, s_shift, p_ready = sem("s_mm"), sem("s_shift"), sem("p_ready")
        exp_ready, sums_ready = sem("exp_ready"), sem("sums_ready")
        pt_mm, pt_ready = sem("pt_mm"), sem("pt_ready")
        pv_mm, o_ready, wo_mm = sem("pv_mm"), sem("o_ready"), sem("wo_mm")
        h_attn = sem("h_attn")
        r0_mm, r0_shift, r0_exp = sem("r0_mm"), sem("r0_shift"), sem("r0_exp")
        up_in = [sem(f"up_in{s}") for s in range(SLOTS0 + 1)]
        dn_in = [sem(f"dn_in{s}") for s in range(SLOTS0 + 1)]
        zeros_ready, chosen0_ready, pos0_mm = (
            sem(n) for n in ("zeros_ready", "chosen0_ready", "pos0_mm"))
        items_ready, slots_ready, sorted_out = sem("items_ready"), sem("slots_ready"), sem("sorted_out")
        xe_in = [sem(f"xe_in{s}") for s in range(SLOTS0)]
        y_out = [sem(f"y_out{s}") for s in range(SLOTS0)]
        yg_in = [sem(f"yg_in{t}") for t in range(NTILE)]
        y_all_out = sem("y_all_out")
        xeT_mm, xeT_ready = sem("xeT_mm"), sem("xeT_ready")
        up_mm, gelu_done, y_mm, y_taken = sem("up_mm"), sem("gelu_done"), sem("y_mm"), sem("y_taken")
        u_mm, u_ready, dtl_mm, dtl_ready = sem("u_mm"), sem("u_ready"), sem("dtl_mm"), sem("dtl_ready")
        b_mm, b_ready, c_mm, c_ready = sem("b_mm"), sem("b_ready"), sem("c_mm"), sem("c_ready")
        dt_mm, sp_abs, sp_ln, sp_max = sem("dt_mm"), sem("sp_abs"), sem("sp_ln"), sem("sp_max")
        dt_ready, dtu_ready, a_exp, a_ready = sem("dt_ready"), sem("dtu_ready"), sem("a_exp"), sem("a_ready")
        c3_ready, inp3_ready = sem("c3_ready"), sem("inp3_ready")
        g_mm, inp_ready, ring_ready, du_ready = sem("g_mm"), sem("inp_ready"), sem("ring_ready"), sem("du_ready")
        barA_ready, ib_mm, cb_mm, scanned = sem("barA_ready"), sem("ib_mm"), sem("cb_mm"), sem("scanned")
        hc_ready, hc_used, yscan_mm = sem("hc_ready"), sem("hc_used"), sem("yscan_mm")
        r1_mm, sig_ready, chosen_ready, pos_mm = sem("r1_mm"), sem("sig_ready"), sem("chosen_ready"), sem("pos_mm")
        w1_in = [sem(f"w1_in{s}") for s in range(SLOTS1)]
        count_mm, active_ready, place_mm, onehot_ready, lists_mm, lists_ready = (
            sem(n) for n in ("count_mm", "active_ready", "place_mm", "onehot_ready", "lists_mm", "lists_ready"))
        gu_mm, silu_ready, hT_ready = sem("gu_mm"), sem("silu_ready"), sem("hT_ready")
        y1_mm, y1_taken, out_done = sem("y1_mm"), sem("y1_taken"), sem("out_done")

        block = ctx.enter_context(nc.Block())

        YG = [(0, 1), (2, 3), (4,)]

        @block.sync
        def _(sp):
            for k in range(KP):
                sp.dma_start(patches[:, k, :], A["patchesT"][k]).then_inc(patch_in[k], 16)
                sp.dma_start(wtok[:, k, :], A["W_tok"][k]).then_inc(patch_in[k], 16)
            sp.dma_start(rowsel, A["rowsel"]).then_inc(pos_in, 16)
            sp.dma_start(posb, A["posb"]).then_inc(pos_in, 16)
            sp.dma_start(ident[:, :], A["ident"]).then_inc(ident_in, 16)
            for dst, name in ((wkv[:, :, :], "wkv"), (wq[:, :, :], "wq"), (g_kv[:, :], "g_kv"),
                              (ones64[:, :], "ones64"), (wkac, "wkac"), (cosT[:, :], "cosT"),
                              (sinT[:, :], "sinT"), (wvdec[:, :], "wvdec"), (wo[:, :, :], "wo"),
                              (maskb[:, :, :], "maskb"), (identb[:, :], "identb")):
                sp.dma_start(dst, A[name]).then_inc(attn_in, 16)
            sp.wait_ge(embed_mm, NTILE)
            for dst, name in ((wqa, "wqa"), (wqb, "wqb"), (wkar, "wkar"), (wkbr, "wkbr")):
                sp.dma_start(dst, A[name]).then_inc(attn2_in, 16)
            for dst, name in ((rw0[:, :, :], "rw0"), (gw1[:, :, :], "gw1"), (e_bias[:, :], "e_bias"),
                              (before[:, :, :], "before"), (onesb[:, :], "onesb"), (upperb[:, :], "upperb"),
                              (validb[:, :], "validb"), (upto[:, :], "upto"), (place[:, :], "place"),
                              (numbers[:, :], "numbers")):
                sp.dma_start(dst, A[name]).then_inc(route_in, 16)
            for dst, name in ((w_in[:, :, :], "w_in"), (w_x[:, :, :], "w_x"), (w_dt[:, :], "w_dt"),
                              (b_dt[:, :], "b_dt"), (a_log[:, :, :], "a_log"), (d_p[:, :], "d_p"),
                              (sel[:, :, :], "sel")):
                sp.dma_start(dst, A[name]).then_inc(scan_in, 16)
            sp.dma_start(w0dn[:, SHARED], A["w0dn"][0]).then_inc(dn_in[SHARED], 16)
            sp.wait_ge(rope_mm, 8)
            sp.dma_start(w0up[:, SHARED], A["w0up"][0]).then_inc(up_in[SHARED], 16)
            for s in range(2):
                sp.dma_start(w1s[:, s, :], A["w1"][NR1 + s]).then_inc(w1_in[s], 16)
            sp.wait_ge(items_ready, 1)
            iters0 = sp.value_load(items[0:1, ITEMS0 + SLOTS0:ITEMS0 + SLOTS0 + 1], min_val=2, max_val=ITEMS0 // SLOTS0)
            for s in range(SLOTS0):
                e = sp.value_load(items[0:1, s:s + 1], min_val=1, max_val=E0 - 1)
                sp.dma_start(w0up[:, s], A["w0up"][e]).then_inc(up_in[s], 16)
                sp.dma_start(w0dn[:, s], A["w0dn"][e]).then_inc(dn_in[s], 16)
            with sp.Fori(0, iters0 - 1) as i:
                for s in range(SLOTS0):
                    e = sp.value_load(items[0:1, bass.ds(i * SLOTS0 + (SLOTS0 + s), 1)], min_val=1, max_val=E0 - 1)
                    sp.wait_ge(up_mm, i * (SLOTS0 * 4) + (FT0 + (s + 1) * 4))
                    sp.dma_start(w0up[:, s], A["w0up"][e]).then_inc(up_in[s], 16)
                    sp.wait_ge(y_mm, i * SLOTS0 + (3 + s + 1))
                    sp.dma_start(w0dn[:, s], A["w0dn"][e]).then_inc(dn_in[s], 16)
            sp.wait_ge(lists_ready, 1)
            iters = sp.value_load(lists[0:1, 2 * NI:2 * NI + 1], min_val=2, max_val=-(-NR1 // SLOTS1))
            for s in range(SLOTS1):
                if s < 2:
                    sp.wait_ge(y1_mm, 3 * (s + 1))
                e = sp.value_load(lists[0:1, s:s + 1], min_val=0, max_val=NR1 - 1)
                sp.dma_start(w1s[:, s, :], A["w1"][e]).then_inc(w1_in[s], 16)
            with sp.Fori(0, iters - 1) as i:
                for s in range(SLOTS1):
                    e = sp.value_load(lists[0:1, bass.ds(i * SLOTS1 + (SLOTS1 + s), 1)], min_val=0, max_val=NR1 - 1)
                    sp.wait_ge(y1_mm, i * (SLOTS1 * 3) + (6 + (s + 1) * 3))
                    sp.dma_start(w1s[:, s, :], A["w1"][e]).then_inc(w1_in[s], 16)
            for t in range(NTILE):
                sp.wait_ge(y1_taken, iters * (3 * SLOTS1) + (6 + t // 2 + 1))
                sp.dma_start(out[t * P:t * P + ROWS[t], :], h[0:ROWS[t], t, :]).then_inc(out_done, 16)
            sp.wait_ge(out_done, 16 * NTILE)

        @block.gpsimd
        def _(pool):
            nc.gpsimd.memset(vpad[:, :, :, HD:32], 0.0).then_inc(v_ones, 1)
            nc.gpsimd.memset(zeros[:, :], 0.0).then_inc(zeros_ready, 1)
            for idx in range(8):
                which, m = idx // 4, idx % 4
                pool.wait_ge(rope_read, idx + 1)
                r = rt[:, idx % 2]
                nc.gpsimd.tensor_tensor(qk[:, which, m, 0, :], r[:, 0, :], r[:, 1, :], ALU.subtract)
                nc.gpsimd.tensor_tensor(qk[:, which, m, 1, :], r[:, 2, :], r[:, 3, :], ALU.add).then_inc(rope_done, 1)
            pool.wait_ge(zeros_ready, 1)
            rows_by_expert = by_expert.rearrange("i j p d -> (i j p) d")
            part = (ITEMS0 + SLOTS0) * TS // SLOTS0
            for s in range(SLOTS0):
                pool.dma_start(rows_by_expert[s * part:(s + 1) * part].rearrange("(p r) d -> p r d", p=P),
                               zeros[:, :].unsqueeze(1).broadcast_to([P, part // P, D])).then_inc(y_out[s], 16)
            for u in range(2 * NG):
                rows = GROUPS[u // 2][1]
                x = u % 2
                pool.wait_ge(sums_ready, u + 1)
                nc.gpsimd.tensor_tensor(prob[0:rows, u % 3, :, 0:rows], prob[0:rows, u % 3, :, 0:rows],
                                        rsum[0:rows, 8 * x:8 * x + 8].unsqueeze(2).broadcast_to([rows, 8, rows]),
                                        ALU.mult).then_inc(p_ready, 1)
            pool.wait_ge(items_ready, 1)
            iters0 = pool.value_load(items[0:1, ITEMS0 + SLOTS0:ITEMS0 + SLOTS0 + 1], min_val=2, max_val=ITEMS0 // SLOTS0)
            for s in range(SLOTS0):
                pool.wait_ge(y_out[s], 16)
            pool.wait_ge(slots_ready, 1)
            for t in range(NTILE):
                for k in range(K0):
                    nc.gpsimd.indirect_dma_start(
                        rows_by_expert, bass.IndirectOffsetOnAxis(ap=slots[0:ROWS[t], k, t:t + 1], axis=0),
                        xn[0:ROWS[t], t, :], None).then_inc(sorted_out, 16)
            pool.wait_ge(sorted_out, 16 * NTILE * K0)
            for s in range(SLOTS0):
                pool.dma_start(xe[:, s, :].rearrange("p (j d) -> p j d", j=2),
                               by_expert[s].rearrange("j p d -> p j d")).then_inc(xe_in[s], 16)
            with pool.Fori(0, iters0) as i:
                for s in range(SLOTS0):
                    pool.wait_ge(xeT_mm, i * SLOTS0 + (s + 1))
                    pool.dma_start(xe[:, s, :].rearrange("p (j d) -> p j d", j=2),
                                   by_expert[i * SLOTS0 + (SLOTS0 + s)].rearrange("j p d -> p j d")).then_inc(xe_in[s], 16)
                    pool.wait_ge(y_taken, i * SLOTS0 + (6 + s + 1))
                    pool.dma_start(by_expert[i * SLOTS0 + s].rearrange("j p d -> p j d"),
                                   ysb[:, s, :].rearrange("p (j d) -> p j d", j=2)).then_inc(y_out[s], 16)
            for s in range(SLOTS0):
                pool.wait_ge(xe_in[s], iters0 * 16 + 16)
            for s in range(SLOTS0):
                pool.wait_ge(y_out[s], iters0 * 16 + 16)
            pool.sem_inc(y_all_out, 1)
            pool.wait_ge(y_all_out, 1)
            for t in range(NTILE):
                for k in range(K0):
                    nc.gpsimd.indirect_dma_start(
                        yg[0:ROWS[t], k, t, :], None, rows_by_expert,
                        bass.IndirectOffsetOnAxis(ap=slots[0:ROWS[t], k, t:t + 1], axis=0)).then_inc(yg_in[t], 16)

        @block.scalar
        def _(act):
            steps = [0]

            def link(ins):
                steps[0] += 1
                ins.then_inc(act_step, 1)
                act.wait_ge(act_step, steps[0])

            def layernorm(l):
                act.wait_ge(var_ready, l + 1)
                nc.scalar.activation(std[:, :], mv[:, :, 1], ACT.Sqrt, bias=LN_EPS).then_inc(std_ready, 1)
                act.wait_ge(xT_mm, l + 1)
                nc.scalar.copy(xT[:, 1, :], PS[:, 2:4, :].rearrange("p b n -> p (b n)")[:, 0:NPAD]).then_inc(xT_hi, 1)

            layernorm(0)
            act.wait_ge(qc_mm, 1)
            nc.scalar.copy(qc.rearrange("p (b n) -> p b n", b=2), PS[:, 2:4, 0:HALF]).then_inc(qc_ready, 1)
            act.wait_ge(kv_ready, 1)
            nc.scalar.activation(sq, kv_sb, ACT.Square).then_inc(sq_ready, 1)
            act.wait_ge(ms_mm, 1)
            nc.scalar.activation(rms.rearrange("p (b n) -> p b n", b=2), PS[0:R_KV, 4:6, 0:HALF], ACT.Sqrt,
                                 bias=RMS_EPS).then_inc(rms_ready, 1)
            act.wait_ge(v_ones, 1)
            for i in range(NG // 2):
                act.wait_ge(v_mm, i + 1)
                rows = GR if i < NG // 2 - 1 else None
                if rows:
                    nc.scalar.copy(vpad[:, 2 * i:2 * i + 2, :, 0:HD],
                                   PS[0:GR, 4 + i, :].rearrange("p (g h d) -> p g h d", g=2, h=NH)).then_inc(v_ready, 1)
                else:
                    last = GROUPS[-1][1]
                    nc.scalar.copy(vpad[:, 2 * i, :, 0:HD],
                                   PS[0:GR, 4 + i, 0:D].rearrange("p (h d) -> p h d", h=NH))
                    nc.scalar.copy(vpad[0:last, 2 * i + 1, :, 0:HD],
                                   PS[0:last, 4 + i, D:2 * D].rearrange("p (h d) -> p h d", h=NH)).then_inc(v_ready, 1)

            def exps(u):
                rows = GROUPS[u // 2][1]
                p = prob[0:rows, u % 3, :, 0:rows]
                act.wait_ge(s_shift, u + 1)
                nc.scalar.activation(p, p, ACT.Exp, scale=SCALE).then_inc(exp_ready, 1)

            exps(0)
            exps(1)
            exps(2)
            for kind, unit in SCHEDULE:
                g, x = divmod(unit, 2)
                c0, rows = GROUPS[g]
                if kind == "P":
                    if unit >= 2:
                        act.wait_ge(pv_mm, unit - 1)
                    for q in range(2):
                        k = 2 * unit + q
                        act.wait_ge(pt_mm, k + 1)
                        nc.scalar.copy(probT[0:rows, x, 4 * q:4 * q + 4, 0:rows],
                                       PS[0:rows, 4 + k % 3, 0:4 * GR].rearrange("p (c n) -> p c n", c=4)[:, :, 0:rows]).then_inc(pt_ready, 1)
                elif kind == "S":
                    exps(unit)
                elif kind == "V" and x:
                    act.wait_ge(pv_mm, unit + 1)
                    nc.scalar.copy(OT[:, :, c0:c0 + rows],
                                   PS[:, 7, 0:4 * GR].rearrange("p (m n) -> p m n", m=4)[:, :, 0:rows]).then_inc(o_ready, 1)

            layernorm(1)
            act.wait_ge(r0_shift, 1)
            nc.scalar.activation(lg0[:, :, :], lg0[:, :, :], ACT.Exp).then_inc(r0_exp, 1)
            for f in range(FT0):
                z = f % 2
                act.wait_ge(up_mm, f + 1)
                nc.scalar.activation(hT0[:, f, :].rearrange("p (b n) -> p b n", b=2),
                                     PS[:, 2 * z:2 * z + 2, 0:HALF], ACT.Gelu).then_inc(gelu_done, 1)
            act.wait_ge(items_ready, 1)
            iters0 = act.value_load(items[0:1, ITEMS0 + SLOTS0:ITEMS0 + SLOTS0 + 1], min_val=2, max_val=ITEMS0 // SLOTS0)
            with act.Fori(0, iters0) as i:
                for s in range(SLOTS0):
                    for z in range(4):
                        act.wait_ge(up_mm, i * (SLOTS0 * 4) + (FT0 + s * 4 + z + 1))
                        nc.scalar.activation(hT0[:, 2 * z:2 * z + 2, s * TS:(s + 1) * TS],
                                             PS[:, z, :].rearrange("p (f n) -> p f n", f=2), ACT.Gelu).then_inc(gelu_done, 1)

            layernorm(2)
            act.wait_ge(scan_in, 7 * 16)
            nc.scalar.activation(a_neg[:, :, :], a_log[:, :, :], ACT.Exp).then_inc(a_exp, 1)
            act.wait_ge(u_mm, 1)
            for c in range(2):
                last = nc.scalar.copy(u[:, c, :].rearrange("p (b n) -> p b n", b=2), PS[:, 2 * c:2 * c + 2, 0:HALF])
            last.then_inc(u_ready, 1)
            act.wait_ge(dtl_mm, 1)
            nc.scalar.copy(dtl.rearrange("p (b n) -> p b n", b=2), PS[0:R_DT, 4:6, 0:HALF]).then_inc(dtl_ready, 1)
            act.wait_ge(b_mm, 1)
            nc.scalar.copy(bT.rearrange("p (b n) -> p b n", b=2), PS[0:NS, 6:8, 0:HALF]).then_inc(b_ready, 1)
            act.wait_ge(c_mm, 1)
            nc.scalar.copy(cT.rearrange("p (b n) -> p b n", b=2), PS[0:NS, 4:6, 0:HALF]).then_inc(c_ready, 1)
            act.wait_ge(sp_max, 1)
            link(nc.scalar.activation(spa, spb, ACT.Abs))
            link(nc.scalar.activation(spa, spa, ACT.Exp, scale=-1.0))
            nc.scalar.activation(spa, spa, ACT.Ln, bias=1.0).then_inc(sp_ln, 1)
            act.wait_ge(dt_ready, 1)
            act.wait_ge(a_ready, 1)
            act.wait_ge(ring_ready, 1)
            for n in range(NS):
                for c in range(2):
                    k = 2 * n + c
                    if k >= BA:
                        act.wait_ge(scanned, k - BA + 1)
                    nc.scalar.activation(barA[:, k % BA, :].rearrange("p (b t) -> p b t", b=B)[:, :, 1:T],
                                         dt[:, c, :].rearrange("p (b t) -> p b t", b=B)[:, :, 1:T], ACT.Exp,
                                         scale=a_neg[:, c, n:n + 1]).then_inc(barA_ready, 1)

            layernorm(3)
            act.wait_ge(r1_mm, 1)
            nc.scalar.activation(scores[:, :, :].rearrange("p t e -> p (t e)"), PS[:, 7, 0:NTILE * NR1],
                                 ACT.Sigmoid).then_inc(sig_ready, 1)
            def silu_of(x):
                for n in range(2):
                    act.wait_ge(gu_mm, x * 2 + (n + 1))
                    nc.scalar.activation(silu_g[:, n, :], PS[:, 2 * n, 0:HALF], ACT.Silu).then_inc(silu_ready, 1)

            for x in range(2):
                silu_of(x)
            act.wait_ge(lists_ready, 1)
            iters = act.value_load(lists[0:1, 2 * NI:2 * NI + 1], min_val=2, max_val=-(-NR1 // SLOTS1))
            with act.Fori(0, iters) as i:
                for s in range(SLOTS1):
                    silu_of(i * SLOTS1 + (2 + s))

        @block.vector
        def _(dve):
            steps = [0]

            def step(ins):
                steps[0] += 1
                ins.then_inc(dve_step, 1)

            def settle():
                dve.wait_ge(dve_step, steps[0])

            def link(ins):
                step(ins)
                settle()

            def layernorm(l):
                for t in range(NTILE):
                    step(nc.vector.bn_stats(stats[:, t, :], h[:, t, :]))
                settle()
                for t in range(NTILE):
                    last = nc.vector.bn_aggr(mv[:, t, :], stats[:, t, :])
                last.then_inc(var_ready, 1)
                dve.wait_ge(std_ready, l + 1)
                link(nc.vector.reciprocal(rstd[:, :], std[:, :]))
                for t in range(NTILE):
                    nc.vector.tensor_scalar(xn[:, t, :], h[:, t, :], mv[:, t, 0:1], rstd[:, t:t + 1],
                                            ALU.subtract, ALU.mult).then_inc(xn_ready, 1)
                dve.wait_ge(xT_mm, l + 1)
                nc.vector.tensor_copy(xT[:, 0, :], PS[:, 0:2, :].rearrange("p b n -> p (b n)")[:, 0:NPAD]).then_inc(xT_lo, 1)

            def rank_of(score):
                sj = score.unsqueeze(2).broadcast_to([P, NTILE, 8, 8])
                se = score.unsqueeze(3).broadcast_to([P, NTILE, 8, 8])
                step(nc.vector.tensor_tensor(cmp_gt[:, :, :, :], sj, se, ALU.is_gt))
                link(nc.vector.tensor_tensor(cmp_eq[:, :, :, :], sj, se, ALU.is_equal))
                link(nc.vector.tensor_tensor(cmp_eq[:, :, :, :].rearrange("p t e j -> p t (e j)"),
                                             cmp_eq[:, :, :, :].rearrange("p t e j -> p t (e j)"),
                                             before[:, :, :].rearrange("p e j -> p (e j)").unsqueeze(1).broadcast_to([P, NTILE, 64]),
                                             ALU.mult))
                link(nc.vector.tensor_tensor(cmp_gt[:, :, :, :], cmp_gt[:, :, :, :], cmp_eq[:, :, :, :], ALU.add))
                link(nc.vector.tensor_reduce(rank[:, :, :], cmp_gt[:, :, :, :], AX.X, ALU.add))

            step(nc.vector.memset(inp3[:, :], 0.0))
            step(nc.vector.memset(c3[:, :], 0.0))
            link(nc.vector.memset(h[:, NTILE - 1, :], 0.0))
            step(nc.vector.memset(zerosb[:, :], 0.0))
            for t in range(NTILE):
                dve.wait_ge(embed_mm, t + 1)
                step(nc.vector.tensor_copy(h[0:ROWS[t], t, :], PS[0:ROWS[t], t, 0:D]))
            settle()

            layernorm(0)
            dve.wait_ge(kv_mm, 1)
            link(nc.vector.tensor_copy(kv_sb.rearrange("p (b n) -> p b n", b=2), PS[0:R_KV, 0:2, 0:HALF]))
            step(nc.vector.memset(mx[:, :], 0.0))
            nc.vector.memset(rsum[:, :], 0.0).then_inc(kv_ready, 1)
            dve.wait_ge(rms_ready, 1)
            link(nc.vector.reciprocal(rrms, rms))
            dve.wait_ge(attn_in, 11 * 16)
            nc.vector.scalar_tensor_tensor(kvn, kv_sb, g_kv[:, 0:1], rrms, ALU.mult, ALU.mult).then_inc(kvn_ready, 1)

            def table(tab):
                return tab[:, :].unsqueeze(1).broadcast_to([P, 8, T])

            for idx in range(8):
                b0 = 4 * (idx % 2)
                dve.wait_ge(rope_mm, idx + 1)
                if idx >= 2:
                    dve.wait_ge(rope_done, idx - 1)
                for j, (src, tab) in enumerate(((0, cosT), (2, sinT), (2, cosT), (0, sinT))):
                    for n in range(2):
                        last = nc.vector.tensor_tensor(
                            rt[:, idx % 2, j, n * HALF:(n + 1) * HALF].rearrange("p (b t) -> p b t", t=T),
                            PS[:, b0 + src + n, 0:HALF].rearrange("p (b t) -> p b t", t=T), table(tab), ALU.mult)
                last.then_inc(rope_read, 1)

            def shift_scores(u):
                g, x = divmod(u, 2)
                rows = GROUPS[g][1]
                m8 = mx[0:rows, 8 * x:8 * x + 8].rearrange("p (j m) -> p j m", j=2)
                S = PS[0:rows, 2 * x:2 * x + 2, 0:4 * GR].rearrange("p j (m n) -> p j m n", m=4)[:, :, :, 0:rows]
                dve.wait_ge(s_mm, u + 1)
                link(nc.vector.tensor_reduce(m8, S, AX.X, ALU.max))
                if u >= 3:
                    dve.wait_ge(pt_mm, 2 * (u - 3) + 2)
                nc.vector.tensor_tensor(prob[0:rows, u % 3, :, 0:rows].rearrange("p (j m) n -> p j m n", j=2), S,
                                        m8.unsqueeze(3).broadcast_to([rows, 2, 4, rows]), ALU.subtract).then_inc(s_shift, 1)

            def sums(u):
                rows = GROUPS[u // 2][1]
                rs = rsum[0:rows, 8 * (u % 2):8 * (u % 2) + 8]
                dve.wait_ge(exp_ready, u + 1)
                if u >= 2:
                    dve.wait_ge(p_ready, u - 1)
                link(nc.vector.tensor_reduce(rs, prob[0:rows, u % 3, :, 0:rows], AX.X, ALU.add))
                nc.vector.reciprocal(rs, rs).then_inc(sums_ready, 1)

            shift_scores(0)
            for unit in range(1, 2 * NG):
                shift_scores(unit)
                sums(unit - 1)
            sums(2 * NG - 1)
            for t in range(NTILE):
                dve.wait_ge(wo_mm, t + 1)
                step(nc.vector.tensor_tensor(h[0:ROWS[t], t, :], PS[0:ROWS[t], t, 0:D], h[0:ROWS[t], t, :], ALU.add))
            settle()

            layernorm(1)
            dve.wait_ge(r0_mm, 1)
            logits = PS[:, 7, 0:NTILE * 8].rearrange("p (t e) -> p t e", t=NTILE)

            def over_e(v, n=8):
                return v[:, :].unsqueeze(2).broadcast_to([P, NTILE, n])

            link(nc.vector.tensor_reduce(r5[:, :], logits, AX.X, ALU.max))
            nc.vector.tensor_tensor(lg0[:, :, :], logits, over_e(r5), ALU.subtract).then_inc(r0_shift, 1)
            dve.wait_ge(r0_exp, 1)
            link(nc.vector.tensor_reduce(r5[:, :], lg0[:, :, :], AX.X, ALU.add))
            link(nc.vector.reciprocal(r5[:, :], r5[:, :]))
            link(nc.vector.tensor_tensor(p0[:, :, :], lg0[:, :, :], over_e(r5), ALU.mult))
            dve.wait_ge(route_in, 10 * 16)
            rank_of(p0[:, :, :])
            nc.vector.scalar_tensor_tensor(chosen0b[:, :, :], rank[:, :, :], float(K0), over_e(validb), ALU.is_lt,
                                           ALU.mult).then_inc(chosen0_ready, 1)
            for tiles in YG:
                a, b = tiles[0], tiles[-1] + 1
                nc.vector.tensor_tensor(h[:, a:b, :], h[:, a:b, :], xn[:, a:b, :], ALU.add).then_inc(y_taken, 1)
            step(nc.vector.memset(ones8[:, :], 1.0))
            dve.wait_ge(pos0_mm, 1)
            earlier0 = PS[:, 7, 64:64 + NTILE * 8].rearrange("p (t e) -> p t e", t=NTILE)
            tokens_of = PS[:, 7, 112:120]
            link(nc.vector.tensor_scalar(nitems[:, :], tokens_of, 0.0, None, ALU.is_gt))
            for k in range(1, CHUNKS):
                link(nc.vector.scalar_tensor_tensor(nitems[:, :], tokens_of, float(k * TS), nitems[:, :], ALU.is_gt, ALU.add))
            link(nc.vector.tensor_tensor_scan(upto_items[:, :], ones8[:, :], nitems[:, :], 0.0, ALU.mult, ALU.add))
            step(nc.vector.tensor_tensor(item_cmp[:, :, :],
                                         upto_items[0:1, :].unsqueeze(1).broadcast_to([1, ITEMS0 + SLOTS0, 8]),
                                         place[0:1, 0:ITEMS0 + SLOTS0].unsqueeze(2).broadcast_to([1, ITEMS0 + SLOTS0, 8]),
                                         ALU.is_lt))
            step(nc.vector.tensor_scalar(place2[:, :], place[0:1, 0:ITEMS0].rearrange("p (i s) -> p i s", s=SLOTS0)[:, :, 0],
                                         upto_items[0:1, 7:8], None, ALU.is_le))
            link(nc.vector.tensor_tensor(first_slot[:, :], upto_items[:, :], nitems[:, :], ALU.subtract))
            step(nc.vector.tensor_reduce(item_e[:, :], item_cmp[:, :, :], AX.X, ALU.add))
            step(nc.vector.tensor_scalar(first_slot[:, :], first_slot[:, :], float(TS), 1.0, ALU.mult, ALU.add))
            link(nc.vector.tensor_reduce(counts[:, 0:1], place2[:, :], AX.X, ALU.add))
            link(nc.vector.tensor_scalar(items[:, 0:ITEMS0 + SLOTS0], item_e[:, :], float(E0 - 2), 1.0, ALU.min, ALU.add))
            nc.vector.tensor_scalar(items[:, ITEMS0 + SLOTS0:ITEMS0 + SLOTS0 + 1], counts[:, 0:1], 2.0, None,
                                    ALU.max).then_inc(items_ready, 1)
            link(nc.vector.tensor_tensor(slot_of[:, :, :], earlier0,
                                         first_slot[:, :].unsqueeze(1).broadcast_to([P, NTILE, 8]), ALU.add))
            link(nc.vector.tensor_tensor(slot_of[:, :, :], slot_of[:, :, :], chosen0b[:, :, :], ALU.mult))
            for t in range(NTILE):
                step(nc.vector.max(slots8[:, t, :], slot_of[:, t, :]))
            settle()
            nc.vector.tensor_scalar(slots[:, :, :], slots8[:, :, 0:K0].rearrange("p t k -> p k t"), -1.0, 0.0, ALU.add,
                                    ALU.max).then_inc(slots_ready, 1)
            for k in range(K0):
                link(nc.vector.tensor_tensor(rank[:, :, :], slot_of[:, :, :],
                                             slots8[:, :, k:k + 1].broadcast_to([P, NTILE, 8]), ALU.is_equal))
                link(nc.vector.tensor_tensor(rank[:, :, :], rank[:, :, :], p0[:, :, :], ALU.mult))
                link(nc.vector.tensor_reduce(gate_k[:, k, :], rank[:, :, :], AX.X, ALU.add))
            dve.wait_ge(y_taken, 3)
            for grp, tiles in enumerate(YG):
                dve.wait_ge(y_mm, grp + 1)
                for t in tiles:
                    last = nc.vector.tensor_tensor(h[0:ROWS[t], t, :], PS[0:ROWS[t], 4 + grp, (t % 2) * D:(t % 2 + 1) * D],
                                                   h[0:ROWS[t], t, :], ALU.add)
                last.then_inc(y_taken, 1)
            iters0 = dve.value_load(items[0:1, ITEMS0 + SLOTS0:ITEMS0 + SLOTS0 + 1], min_val=2, max_val=ITEMS0 // SLOTS0)
            dve.wait_ge(xeT_mm, 1)
            nc.vector.tensor_copy(xeT[:, 0].rearrange("p c n -> p (c n)"), PS[:, 7, :]).then_inc(xeT_ready, 1)
            with dve.Fori(0, iters0) as i:
                for s in range(SLOTS0):
                    dve.wait_ge(xeT_mm, i * SLOTS0 + (s + 2))
                    nc.vector.tensor_copy(xeT[:, 1 - s].rearrange("p c n -> p (c n)"), PS[:, 7, :]).then_inc(xeT_ready, 1)
                    dve.wait_ge(y_out[s], i * 16 + 16)
                    dve.wait_ge(y_mm, i * SLOTS0 + (3 + s + 1))
                    nc.vector.tensor_copy(ysb[:, s, :], PS[:, 4 + s, :]).then_inc(y_taken, 1)
            dve.wait_ge(y_taken, 6)
            for t in range(NTILE):
                dve.wait_ge(yg_in[t], 16 * K0)
                for k in range(K0):
                    link(nc.vector.scalar_tensor_tensor(h[0:ROWS[t], t, :], yg[0:ROWS[t], k, t, :],
                                                        gate_k[0:ROWS[t], k, t:t + 1], h[0:ROWS[t], t, :],
                                                        ALU.mult, ALU.add))

            layernorm(2)
            dve.wait_ge(a_exp, 1)
            nc.vector.tensor_scalar(a_neg[:, :, :], a_neg[:, :, :], -1.0, None, ALU.mult).then_inc(a_ready, 1)
            nc.vector.memset(barA.rearrange("p r (b t) -> p r b t", b=B)[:, :, :, 0:1], 0.0).then_inc(ring_ready, 1)
            def split3(parts, x):
                link(nc.vector.tensor_copy(parts[0:NS, :], x))
                link(nc.vector.tensor_tensor(rest[:, 0, :], x, parts[0:NS, :], ALU.subtract))
                link(nc.vector.tensor_copy(parts[32:32 + NS, :], rest[:, 0, :]))
                link(nc.vector.tensor_copy(mid_b[:, :], rest[:, 0, :]))
                link(nc.vector.tensor_tensor(rest[:, 1, :], rest[:, 0, :], mid_b[:, :], ALU.subtract))
                return nc.vector.tensor_copy(parts[64:64 + NS, :], rest[:, 1, :])

            dve.wait_ge(c_ready, 1)
            split3(c3, cT).then_inc(c3_ready, 1)
            dve.wait_ge(dt_mm, 1)
            for c in range(2):
                for n, bank in enumerate((2 * c, 2 * c + 1)):
                    last = nc.vector.tensor_scalar(spb[:, c, n * HALF:(n + 1) * HALF], PS[:, bank, 0:HALF],
                                                   b_dt[:, c:c + 1], None, ALU.add)
            last.then_inc(sp_max, 1)
            dve.wait_ge(sp_max, 1)
            dve.wait_ge(sp_ln, 1)
            link(nc.vector.tensor_scalar(spb, spb, 0.0, None, ALU.max))
            link(nc.vector.tensor_tensor(spa, spa, spb, ALU.add))
            nc.vector.tensor_scalar(dt, spa, DT_MAX - DT_MIN, DT_MIN, ALU.mult, ALU.add).then_inc(dt_ready, 1)
            dve.wait_ge(dt_ready, 1)
            dve.wait_ge(u_ready, 1)
            nc.vector.tensor_tensor(dtu, dt, u, ALU.mult).then_inc(dtu_ready, 1)
            for c in range(2):
                last = nc.vector.tensor_scalar(du[:, c, :], u[:, c, :], d_p[:, c:c + 1], None, ALU.mult)
            last.then_inc(du_ready, 1)
            dve.wait_ge(g_mm, 1)
            dve.wait_ge(b_ready, 1)
            nc.vector.tensor_tensor(inpT.rearrange("p (b n) -> p b n", b=2), PS[0:NS, 6:8, 0:HALF],
                                    bT.rearrange("p (b n) -> p b n", b=2), ALU.mult).then_inc(inp_ready, 1)
            dve.wait_ge(inp_ready, 1)
            split3(inp3, inpT).then_inc(inp3_ready, 1)
            IB = PS[:, 3:5, :].rearrange("p b n -> p (b n)")[:, 0:NT]
            CB = PS[:, 5:7, :].rearrange("p b n -> p (b n)")[:, 0:NT]
            for n in range(NS):
                dve.wait_ge(ib_mm, n + 1)
                for c in range(2):
                    k = 2 * n + c
                    dve.wait_ge(barA_ready, k + 1)
                    if k >= 2:
                        dve.wait_ge(hc_ready, k - 1)
                    nc.vector.tensor_tensor_scan(hs[:, c, :], barA[:, k % BA, :], IB, 0.0, ALU.mult, ALU.add).then_inc(scanned, 1)
                dve.wait_ge(cb_mm, n + 1)
                for c in range(2):
                    k = 2 * n + c
                    dve.wait_ge(scanned, k + 1)
                    if k >= 4:
                        dve.wait_ge(hc_used, k - 3)
                    nc.vector.tensor_tensor(hc[:, k % 4, :], hs[:, c, :], CB, ALU.mult).then_inc(hc_ready, 1)
            dve.wait_ge(yscan_mm, 1)
            for t in range(NTILE):
                step(nc.vector.tensor_tensor(h[0:ROWS[t], t, :], PS[0:ROWS[t], t // 2, (t % 2) * D:(t % 2 + 1) * D],
                                             h[0:ROWS[t], t, :], ALU.add))
            settle()

            layernorm(3)

            def hidden(x):
                for n in range(2):
                    dve.wait_ge(silu_ready, x * 2 + (n + 1))
                    nc.vector.tensor_tensor(hT1[:, n * HALF:(n + 1) * HALF], silu_g[:, n, :], PS[:, 2 * n + 1, 0:HALF],
                                            ALU.mult).then_inc(hT_ready, 1)

            def add_output(x, gate):
                for grp, tiles in enumerate(YG):
                    dve.wait_ge(y1_mm, x * 3 + (grp + 1))
                    dve.wait_ge(y1_taken, x * 3 + (grp + 1))
                    for t in tiles:
                        y = PS[0:ROWS[t], 4 + grp, (t % 2) * D:(t % 2 + 1) * D]
                        if gate is None:
                            last = nc.vector.tensor_tensor(h[0:ROWS[t], t, :], y, h[0:ROWS[t], t, :], ALU.add)
                        else:
                            last = nc.vector.scalar_tensor_tensor(h[0:ROWS[t], t, :], y, gate(t), h[0:ROWS[t], t, :],
                                                                  ALU.mult, ALU.add)
                    last.then_inc(y1_taken, 1)

            for grp in range(3):
                nc.vector.memset(r5[:, grp:grp + 1], 0.0).then_inc(y1_taken, 1)
            dve.wait_ge(y1_taken, 3)
            dve.wait_ge(sig_ready, 1)
            link(nc.vector.tensor_tensor(sfc[:, :, :], scores[:, :, :],
                                         e_bias[:, :].unsqueeze(1).broadcast_to([P, NTILE, NR1]), ALU.add))
            for t in range(NTILE):
                for g in range(NGRP):
                    step(nc.vector.max(top8g[:, t * NGRP + g, :], sfc[:, t, 8 * g:8 * g + 8]))
            hidden(0)
            settle()
            link(nc.vector.tensor_tensor(gscore[:, :, :].rearrange("p t g -> p (t g)"), top8g[:, :, 0], top8g[:, :, 1], ALU.add))
            rank_of(gscore[:, :, :])
            link(nc.vector.tensor_scalar(gscore[:, :, :], rank[:, :, :], float(TOPG), None, ALU.is_lt))
            link(nc.vector.tensor_tensor(tmp[:, :, :].rearrange("p t (g e) -> p (t g) e", g=NGRP),
                                         sfc[:, :, :].rearrange("p t (g e) -> p (t g) e", g=NGRP),
                                         gscore[:, :, :].rearrange("p t g -> p (t g)").unsqueeze(2).broadcast_to([P, NTILE * NGRP, 8]),
                                         ALU.mult))
            for t in range(NTILE):
                step(nc.vector.max(top8[:, t, :], tmp[:, t, :]))
            settle()
            for t in range(NTILE):
                step(nc.vector.match_replace(tmp[:, t, :], top8[:, t, :], tmp[:, t, :], REMOVED))
            settle()
            link(nc.vector.tensor_scalar(chosen[:, :, :], tmp[:, :, :], REMOVED, None, ALU.is_equal))
            nc.vector.tensor_copy(chosenb[:, :, :], chosen[:, :, :]).then_inc(chosen_ready, 1)
            add_output(0, None)
            hidden(1)
            dve.wait_ge(count_mm, 1)
            step(nc.vector.tensor_scalar(active[:, :], PS[0:NR1, 6, 256:257], 0.0, None, ALU.is_gt))
            nc.vector.tensor_scalar(activeb[:, :], PS[0:NR1, 6, 256:257], 0.0, None, ALU.is_gt).then_inc(active_ready, 1)
            dve.wait_ge(place_mm, 1)
            link(nc.vector.tensor_copy(upto_n[:, :], PS[0:NR1, 6, 256:257]))
            nc.vector.tensor_scalar(onehot[:, :], place[:, :], upto_n[:, 0:1], active[:, 0:1], ALU.is_equal,
                                    ALU.mult).then_inc(onehot_ready, 1)
            link(nc.vector.tensor_tensor(scores[:, :, :], scores[:, :, :], chosen[:, :, :], ALU.mult))
            link(nc.vector.tensor_reduce(r5[:, :], scores[:, :, :], AX.X, ALU.add))
            dve.wait_ge(lists_mm, 1)
            step(nc.vector.tensor_copy(lists[:, 0:2 * NI], PS[0:1, 6, 256:256 + 2 * NI]))
            link(nc.vector.tensor_reduce(counts[:, 0:1], PS[0:1, 7, 384:384 + NI].rearrange("p (i s) -> p i s", s=SLOTS1)[:, :, 0],
                                         AX.X, ALU.add))
            nc.vector.tensor_scalar(lists[:, 2 * NI:2 * NI + 1], counts[:, 0:1], 2.0, None, ALU.max).then_inc(lists_ready, 1)
            add_output(1, None)
            link(nc.vector.tensor_scalar(r5[:, :], r5[:, :], 1e-20, None, ALU.add))
            link(nc.vector.reciprocal(r5[:, :], r5[:, :]))
            link(nc.vector.tensor_tensor(scores[:, :, :], scores[:, :, :], over_e(r5, NR1), ALU.mult))
            link(nc.vector.tensor_scalar(scores[:, :, :], scores[:, :, :], SCALE1, None, ALU.mult))
            dve.wait_ge(pos_mm, 1)
            earlier = PS[:, 7, 0:NTILE * NR1].rearrange("p (t e) -> p t e", t=NTILE)
            step(nc.vector.memset(gates1[:, :, 0:1], 0.0))
            link(nc.vector.scalar_tensor_tensor(gates1[:, :, 1:NR1 + 1], earlier, float(CAP), scores[:, :, :],
                                                ALU.is_lt, ALU.mult))
            dve.wait_ge(lists_ready, 1)
            iters = dve.value_load(lists[0:1, 2 * NI:2 * NI + 1], min_val=2, max_val=-(-NR1 // SLOTS1))
            with dve.Fori(0, iters) as i:
                for s in range(SLOTS1):
                    col = dve.value_load(lists[0:1, bass.ds(i * SLOTS1 + (NI + s), 1)], min_val=0, max_val=NR1)
                    hidden(i * SLOTS1 + (2 + s))
                    add_output(i * SLOTS1 + (2 + s), lambda t: gates1[0:ROWS[t], t, :][:, bass.ds(col, 1)])

        @block.tensor
        def _(pe):
            mm = nc.tensor.matmul

            def transpose_xn(l):
                if l == 0:
                    pe.wait_ge(ident_in, 16)
                for t in range(NTILE):
                    pe.wait_ge(xn_ready, NTILE * l + t + 1)
                    for c in range(2):
                        last = nc.tensor.transpose(PS[:, 2 * c + t // 4, (t % 4) * P:(t % 4 + 1) * P],
                                                   xn[:, t, c * P:(c + 1) * P], ident[:, :])
                last.then_inc(xT_mm, 1)
                pe.wait_ge(xT_lo, l + 1)
                pe.wait_ge(xT_hi, l + 1)

            def half(n):
                return slice(n * HALF, (n + 1) * HALF)

            for k in range(KP):
                pe.wait_ge(patch_in[k], 32)
                for t in range(NTILE):
                    mm(PS[0:ROWS[t], t, 0:D], patches[:, k, t * P:t * P + ROWS[t]], wtok[:, k, :], start=(k == 0), stop=False)
            pe.wait_ge(pos_in, 32)
            for t in range(NTILE):
                mm(PS[0:ROWS[t], t, 0:D], rowsel[:, t * P:t * P + ROWS[t]], posb, start=False, stop=True).then_inc(embed_mm, 1)

            transpose_xn(0)
            pe.wait_ge(attn_in, 11 * 16)
            for n in range(2):
                for c in range(2):
                    last = mm(PS[0:R_KV, n, 0:HALF], wkv[:, c, :], xT[:, c, half(n)], start=c == 0, stop=c == 1)
            last.then_inc(kv_mm, 1)
            for n in range(2):
                for c in range(2):
                    last = mm(PS[:, 2 + n, 0:HALF], wq[:, c, :], xT[:, c, half(n)], start=c == 0, stop=c == 1)
            last.then_inc(qc_mm, 1)
            pe.wait_ge(sq_ready, 1)
            for n in range(2):
                last = mm(PS[0:R_KV, 4 + n, 0:HALF], ones64[:, :], sq[:, half(n)], start=True, stop=True)
            last.then_inc(ms_mm, 1)
            pe.wait_ge(qc_ready, 1)
            pe.wait_ge(attn2_in, 4 * 16)
            for idx in range(8):
                which, m, b0 = idx // 4, idx % 4, 4 * (idx % 2)
                if idx == 1:
                    pe.wait_ge(rms_ready, 1)
                if idx >= 2:
                    pe.wait_ge(rope_read, idx - 1)
                if idx == 4:
                    pe.wait_ge(kvn_ready, 1)
                for n in range(2):
                    if which == 0:
                        mm(PS[:, b0 + n, 0:HALF], wqa[:, m, :], qc[:, half(n)], start=True, stop=True)
                        last = mm(PS[:, b0 + 2 + n, 0:HALF], wqb[:, m, :], qc[:, half(n)], start=True, stop=True)
                    else:
                        mm(PS[:, b0 + n, 0:HALF], wkac[:, m, :], kvn[:, half(n)], start=True, stop=False)
                        for c in range(2):
                            mm(PS[:, b0 + n, 0:HALF], wkar[:, c, m, :], xT[:, c, half(n)], start=False, stop=c == 1)
                        for c in range(2):
                            last = mm(PS[:, b0 + 2 + n, 0:HALF], wkbr[:, c, m, :], xT[:, c, half(n)], start=c == 0, stop=c == 1)
                last.then_inc(rope_mm, 1)
            pe.wait_ge(rope_read, 8)
            for g, (c0, rows) in enumerate(GROUPS):
                last = mm(PS[0:rows, 4 + g // 2, (g % 2) * D:(g % 2 + 1) * D], kvn[:, c0:c0 + rows], wvdec[:, :],
                          start=True, stop=True)
                if g % 2:
                    last.then_inc(v_mm, 1)
            pe.wait_ge(rope_done, 8)

            def scores_of(u):
                g, x = divmod(u, 2)
                c0, rows = GROUPS[g]
                if u >= 2:
                    pe.wait_ge(s_shift, u - 1)
                for j in (2 * x, 2 * x + 1):
                    S = PS[0:rows, j, 0:4 * GR].rearrange("p (m n) -> p m n", m=4)
                    for m in range(4):
                        for ab in range(2):
                            mm(S[:, m, 0:rows], qk[32 * j:32 * j + 32, 0, m, ab, c0:c0 + rows],
                               qk[32 * j:32 * j + 32, 1, m, ab, c0:c0 + rows], start=(m == 0 and ab == 0), stop=False,
                               skip_group_check=True)
                    last = mm(S[:, :, 0:rows], identb[0:rows, 0:rows], maskb[0:rows, :, 0:rows], start=False, stop=True,
                              skip_group_check=True)
                last.then_inc(s_mm, 1)

            def transpose_p(u):
                rows = GROUPS[u // 2][1]
                pe.wait_ge(p_ready, u + 1)
                for q in range(2):
                    k = 2 * u + q
                    if k >= 3:
                        pe.wait_ge(pt_ready, k - 2)
                    for y in range(4):
                        last = nc.tensor.transpose(PS[0:rows, 4 + k % 3, y * GR:y * GR + rows], prob[0:rows, u % 3, 4 * q + y, 0:rows],
                                                   ident[0:rows, 0:rows])
                    last.then_inc(pt_mm, 1)

            def times_v(u):
                g, x = divmod(u, 2)
                rows = GROUPS[g][1]
                if x == 0 and g:
                    pe.wait_ge(o_ready, g)
                pe.wait_ge(pt_ready, 2 * u + 2)
                for y in range(8):
                    j, m = 2 * x + y // 4, y % 4
                    last = mm(PS[32 * j:32 * j + 32, 7, m * GR:m * GR + rows], vpad[0:rows, g, 4 * m + j, :],
                              probT[0:rows, x, y, 0:rows], start=True, stop=True)
                last.then_inc(pv_mm, 1)

            scores_of(0)
            scores_of(1)
            scores_of(2)
            pe.wait_ge(v_ready, 3)
            for kind, unit in SCHEDULE:
                {"P": transpose_p, "S": scores_of, "V": times_v}[kind](unit)
            pe.wait_ge(o_ready, NG)
            for t in range(NTILE):
                for m in range(4):
                    last = mm(PS[0:ROWS[t], t, 0:D], OT[:, m, t * P:t * P + ROWS[t]], wo[:, m, :], start=m == 0, stop=m == 3)
                last.then_inc(wo_mm, 1)

            transpose_xn(1)
            pe.wait_ge(route_in, 10 * 16)
            for t in range(NTILE):
                for c in range(2):
                    last = mm(PS[:, 7, 8 * t:8 * t + 8], xT[:, c, t * P:(t + 1) * P], rw0[:, c, :], start=c == 0, stop=c == 1)
            last.then_inc(r0_mm, 1)
            pe.wait_ge(up_in[SHARED], 16)
            for f in range(FT0):
                z = f % 2
                if f >= 2:
                    pe.wait_ge(gelu_done, f - 1)
                for n in range(2):
                    for c in range(2):
                        last = mm(PS[:, 2 * z + n, 0:HALF], w0up[:, SHARED, c, f * P:(f + 1) * P], xT[:, c, half(n)],
                                  start=c == 0, stop=c == 1)
                last.then_inc(up_mm, 1)
                if f == FT0 // 2:
                    pe.wait_ge(chosen0_ready, 1)
                    for t in range(NTILE):
                        for e in range(t):
                            mm(PS[:, 7, 64 + 8 * t:72 + 8 * t], onesb[:, :], chosen0b[:, e, :], start=e == 0, stop=False)
                        mm(PS[:, 7, 64 + 8 * t:72 + 8 * t], upperb[:, :], chosen0b[:, t, :], start=t == 0, stop=True)
                    for t in range(NTILE):
                        last = mm(PS[:, 7, 112:120], onesb[:, :], chosen0b[:, t, :], start=t == 0, stop=t == NTILE - 1)
                    last.then_inc(pos0_mm, 1)
            pe.wait_ge(dn_in[SHARED], 16)
            for grp, tiles in enumerate(YG):
                pe.wait_ge(y_taken, grp + 1)
                for t in tiles:
                    for f in range(FT0):
                        if t == 0:
                            pe.wait_ge(gelu_done, f + 1)
                        last = mm(PS[0:ROWS[t], 4 + grp, (t % 2) * D:(t % 2 + 1) * D],
                                  hT0[:, f, t * P:t * P + ROWS[t]], w0dn[:, SHARED, f, :], start=f == 0, stop=f == FT0 - 1)
                last.then_inc(y_mm, 1)

            def transpose_item(s):
                for j in range(2):
                    for c in range(2):
                        last = nc.tensor.transpose(PS[:, 7, c * TS + j * P:c * TS + (j + 1) * P],
                                                   xe[:, s, j * D + c * P:j * D + (c + 1) * P], ident[:, :])
                last.then_inc(xeT_mm, 1)

            pe.wait_ge(items_ready, 1)
            iters0 = pe.value_load(items[0:1, ITEMS0 + SLOTS0:ITEMS0 + SLOTS0 + 1], min_val=2, max_val=ITEMS0 // SLOTS0)
            pe.wait_ge(xe_in[0], 16)
            transpose_item(0)
            with pe.Fori(0, iters0) as i:
                for s in range(SLOTS0):
                    pe.wait_ge(up_in[s], i * 16 + 16)
                    pe.wait_ge(xeT_ready, i * SLOTS0 + (s + 1))
                    for z in range(4):
                        for f in (2 * z, 2 * z + 1):
                            for c in range(2):
                                last = mm(PS[:, z, (f % 2) * TS:(f % 2 + 1) * TS], w0up[:, s, c, f * P:(f + 1) * P],
                                          xeT[:, s, c, :], start=c == 0, stop=c == 1)
                        last.then_inc(up_mm, 1)
                    pe.wait_ge(xe_in[1 - s], i * 16 + (16 if s == 0 else 32))
                    transpose_item(1 - s)
                    pe.wait_ge(dn_in[s], i * 16 + 16)
                    pe.wait_ge(y_taken, i * SLOTS0 + (5 + s))
                    for j in range(2):
                        for f in range(FT0):
                            if j == 0 and f % 2 == 0:
                                pe.wait_ge(gelu_done, i * (SLOTS0 * 4) + (FT0 + s * 4 + f // 2 + 1))
                            last = mm(PS[:, 4 + s, j * D:(j + 1) * D], hT0[:, f, s * TS + j * P:s * TS + (j + 1) * P],
                                      w0dn[:, s, f, :], start=f == 0, stop=f == FT0 - 1)
                    last.then_inc(y_mm, 1)

            transpose_xn(2)
            pe.wait_ge(scan_in, 7 * 16)
            for c in range(2):
                for n in range(2):
                    for k in range(2):
                        last = mm(PS[:, 2 * c + n, 0:HALF], w_in[:, k, c * P:(c + 1) * P], xT[:, k, half(n)], start=k == 0, stop=k == 1)
            last.then_inc(u_mm, 1)
            pe.wait_ge(u_ready, 1)

            def project(bank, rows, w, done):
                for n in range(2):
                    for k in range(2):
                        last = mm(PS[0:rows, bank + n, 0:HALF], w_x[:, k, w:w + rows], u[:, k, half(n)], start=k == 0, stop=k == 1)
                last.then_inc(done, 1)

            project(4, R_DT, 0, dtl_mm)
            project(6, NS, R_DT, b_mm)
            pe.wait_ge(dtl_ready, 1)
            for c in range(2):
                for n in range(2):
                    last = mm(PS[:, 2 * c + n, 0:HALF], w_dt[:, c * P:(c + 1) * P], dtl[:, half(n)], start=True, stop=True)
            last.then_inc(dt_mm, 1)
            project(4, NS, R_DT + NS, c_mm)
            pe.wait_ge(b_ready, 1)
            pe.wait_ge(a_ready, 1)
            pe.wait_ge(dtu_ready, 1)
            for n in range(2):
                for k in range(2):
                    last = mm(PS[0:NS, 6 + n, 0:HALF], a_neg[:, k, :], dtu[:, k, half(n)], start=k == 0, stop=k == 1)
            last.then_inc(g_mm, 1)
            for bank in range(3):
                mm(PS[:, bank, :], zerosb[:, 0:P], zerosb[:, :], start=True, stop=False, skip_group_check=True)
            pe.wait_ge(du_ready, 1)

            def add_to_y(src, c):
                for t in range(NTILE):
                    last = mm(PS[0:ROWS[t], t // 2, (t % 2) * D + c * P:(t % 2) * D + (c + 1) * P],
                              src[:, t * P:t * P + ROWS[t]], ident[:, :], start=False, stop=False, skip_group_check=True)
                return last

            def broadcast(bank, row, n, done):
                mm(PS[:, bank, 0:512], sel[:, n, :], row[:, 0:512], start=True, stop=True)
                mm(PS[:, bank + 1, 0:NT - 512], sel[:, n, :], row[:, 512:NT], start=True, stop=True).then_inc(done, 1)

            for c in range(2):
                add_to_y(du[:, c, :], c)
            pe.wait_ge(c3_ready, 1)
            pe.wait_ge(inp3_ready, 1)
            for n in range(NS):
                if n:
                    pe.wait_ge(scanned, 2 * n)
                broadcast(3, inp3, n, ib_mm)
                if n:
                    pe.wait_ge(hc_ready, 2 * n)
                broadcast(5, c3, n, cb_mm)
                if n:
                    for c in range(2):
                        add_to_y(hc[:, (2 * (n - 1) + c) % 4, :], c).then_inc(hc_used, 1)
            pe.wait_ge(hc_ready, 2 * NS)
            for c in range(2):
                add_to_y(hc[:, (2 * (NS - 1) + c) % 4, :], c)
            for bank in range(3):
                last = mm(PS[:, bank, :], zerosb[:, 0:P], zerosb[:, :], start=False, stop=True, skip_group_check=True)
            last.then_inc(yscan_mm, 1)

            transpose_xn(3)
            for t in range(NTILE):
                for c in range(2):
                    last = mm(PS[:, 7, NR1 * t:NR1 * (t + 1)], xT[:, c, t * P:(t + 1) * P], gw1[:, c, :], start=c == 0, stop=c == 1)
            last.then_inc(r1_mm, 1)

            def expert_up(s, x):
                for n in range(2):
                    for j in range(2):
                        for c in range(2):
                            w = (2 * j + c) * F1
                            last = mm(PS[:, 2 * n + j, 0:HALF], w1s[:, s, w:w + F1], xT[:, c, half(n)], start=c == 0, stop=c == 1)
                    last.then_inc(gu_mm, 1)

            def expert_down(s, x):
                for grp, tiles in enumerate(YG):
                    pe.wait_ge(hT_ready, x * 2 + (1 if grp == 0 else 2))
                    pe.wait_ge(y1_taken, x * 3 + (grp + 1))
                    for t in tiles:
                        last = mm(PS[0:ROWS[t], 4 + grp, (t % 2) * D:(t % 2 + 1) * D],
                                  hT1[:, t * P:t * P + ROWS[t]], w1s[:, s, 4 * F1:4 * F1 + D], start=True, stop=True)
                    last.then_inc(y1_mm, 1)

            for x in range(2):
                pe.wait_ge(w1_in[x], 16)
                expert_up(x, x)
                expert_down(x, x)
            pe.wait_ge(sig_ready, 1)
            pe.wait_ge(chosen_ready, 1)
            pe.wait_ge(y1_taken, 6)
            for t in range(NTILE):
                last = mm(PS[0:NR1, 6, 256:257], chosenb[:, t, :], validb[:, t:t + 1], start=t == 0, stop=t == NTILE - 1)
            last.then_inc(count_mm, 1)
            for t in range(NTILE):
                for s in range(t):
                    mm(PS[:, 7, NR1 * t:NR1 * (t + 1)], onesb[:, :], chosenb[:, s, :], start=s == 0, stop=False)
                last = mm(PS[:, 7, NR1 * t:NR1 * (t + 1)], upperb[:, :], chosenb[:, t, :], start=t == 0, stop=True)
            last.then_inc(pos_mm, 1)
            pe.wait_ge(active_ready, 1)
            mm(PS[0:NR1, 6, 256:257], upto[:, :], activeb[:, :], start=True, stop=True).then_inc(place_mm, 1)
            pe.wait_ge(onehot_ready, 1)
            for k in range(2):
                mm(PS[0:1, 6, 256 + k * NI:256 + (k + 1) * NI], numbers[:, k:k + 1], onehot[:, :], start=True, stop=True)
            mm(PS[0:1, 7, 384:384 + NI], numbers[:, 2:3], onehot[:, :], start=True, stop=True).then_inc(lists_mm, 1)
            pe.wait_ge(lists_ready, 1)
            iters = pe.value_load(lists[0:1, 2 * NI:2 * NI + 1], min_val=2, max_val=-(-NR1 // SLOTS1))
            with pe.Fori(0, iters) as i:
                for s in range(SLOTS1):
                    pe.wait_ge(w1_in[s], i * 16 + (32 if s < 2 else 16))
                    expert_up(s, None)
                    expert_down(s, i * SLOTS1 + (2 + s))


SCHEDULE = []
for _u in range(2 * NG):
    SCHEDULE.append(("P", _u))
    if _u + 3 < 2 * NG:
        SCHEDULE.append(("S", _u + 3))
    SCHEDULE.append(("V", _u))


def shape_constants():
    bf = np.dtype("bfloat16")
    f = np.float32
    rowsel = np.zeros((T + 2, NT), f)
    n = np.arange(NT)
    rowsel[n % T, n] = 1
    rowsel[T, n] = n % T == 0
    rowsel[T + 1, n] = n % T != 0
    r = np.arange(GR)
    ok = (r[:, None] // T == r[None, :] // T) & (r[None, :] <= r[:, None])
    inv = (1.0 / 10000.0 ** (np.arange(0, RD, 2, dtype=np.float32) / RD)).astype(f)
    fr = np.outer(np.arange(T, dtype=f), inv).astype(f)
    cosT, sinT = np.ones((P, T), f), np.zeros((P, T), f)
    for j in range(4):
        cosT[32 * j + 16:32 * j + 32] = np.cos(fr).T
        sinT[32 * j + 16:32 * j + 32] = np.sin(fr).T
    sel = np.zeros((3, 32, NS, P), bf)
    sel[:, np.arange(NS), np.arange(NS)] = 1
    sel = sel.reshape(96, NS, P)
    before = np.broadcast_to(np.tril(np.ones((8, 8), f), -1), (P, 8, 8))
    valid = (np.arange(NPAD) < NT).astype(f).reshape(NTILE, P).T
    e = np.arange(NR1, dtype=f)
    return dict(validb=valid.astype(bf), upto=np.triu(np.ones((NR1, NR1), f)).astype(bf),
                place=np.ascontiguousarray(np.broadcast_to(np.arange(1, NI + 1, dtype=f), (NR1, NI))),
                numbers=np.stack([e, e + 1, np.ones(NR1, f)], 1),
                rowsel=rowsel, ident=np.eye(P, dtype=f), identb=np.eye(P, dtype=f).astype(bf),
                onesb=np.ones((P, P), bf), upperb=np.triu(np.ones((P, P), f), 1).astype(bf),
                maskb=np.ascontiguousarray(np.broadcast_to(np.where(ok, 0.0, MASKED).astype(f)[:, None, :], (GR, 4, GR))).astype(bf),
                ones64=np.full((R_KV, R_KV), 1.0 / R_KV, f), cosT=cosT, sinT=sinT, sel=sel,
                before=np.ascontiguousarray(before))


def rows_first(w, k=P):
    return w.reshape(w.shape[0] // k, k, w.shape[1]).transpose(1, 0, 2)


def head_quads(w, width, parts):
    o = np.zeros((w.shape[0], 4, 4, 32), w.dtype)
    w4 = w.reshape(w.shape[0], 4, 4, width)
    for (a, b), at in parts:
        o[:, :, :, at:at + b - a] = w4[:, :, :, a:b]
    return o.reshape(w.shape[0], 4, 128)


def kernel(**inputs):
    import concourse.bacc as bacc
    from concourse.bass_utils import run_bass_kernel_spmd

    I = {k: np.asarray(v) for k, v in inputs.items()}
    a = {}
    x = I["x"].reshape(B, 3, 6, 16, 6, 16).transpose(1, 3, 5, 0, 2, 4).reshape(768, B, 36)
    px = np.zeros((768, B, T), x.dtype)
    px[:, :, 1:] = x
    a["patchesT"] = px.reshape(KP, P, NT)
    a["W_tok"] = I["L0_tok_W"].T.reshape(KP, P, D)
    a["posb"] = np.concatenate([I["L0_tok_pos_embed"][0], I["L0_tok_cls_token"][0], I["L0_tok_b"][None]], 0)
    a["wkv"] = rows_first(I["L0_attn_W_kv"])
    a["wq"] = rows_first(I["L0_attn_W_q"])
    a["g_kv"] = I["L0_attn_g_kv"].reshape(R_KV, 1)
    wo = np.zeros((4, 32, 4, D), I["L0_attn_W_o"].dtype)
    wo[:, :HD] = I["L0_attn_W_o"].reshape(4, 4, HD, D).transpose(1, 2, 0, 3)
    a["wo"] = wo.reshape(P, 4, D)
    a["wvdec"] = I["L0_attn_W_vdec"]
    a["wkac"] = head_quads(I["L0_attn_W_kdec"], HD, [((0, 16), 0)])
    kr = I["L0_attn_W_krope"]
    a["wkar"] = head_quads(kr, RD, [((0, 16), 16)]).reshape(2, P, 4, P).transpose(1, 0, 2, 3)
    a["wkbr"] = head_quads(kr, RD, [((16, 32), 16)]).reshape(2, P, 4, P).transpose(1, 0, 2, 3)
    qr = I["L0_attn_W_qrope"]
    wqa = head_quads(I["L0_attn_W_qdec"], HD, [((0, 16), 0)]).reshape(R_Q, 4, 4, 32)
    wqa[..., 16:] = head_quads(qr, RD, [((0, 16), 16)]).reshape(R_Q, 4, 4, 32)[..., 16:]
    a["wqa"] = wqa.reshape(R_Q, 4, P)
    a["wqb"] = head_quads(qr, RD, [((16, 32), 16)])
    a["rw0"] = rows_first(I["L0_ffn_router_w"])
    up = np.concatenate([I["L0_ffn_shared_up"], I["L0_ffn_routed_up"]], 0)
    dn = np.concatenate([I["L0_ffn_shared_down"], I["L0_ffn_routed_down"]], 0)
    a["w0up"] = up.reshape(E0, 2, P, F0).transpose(0, 2, 1, 3)
    a["w0dn"] = dn.reshape(E0, FT0, P, D).transpose(0, 2, 1, 3)
    a["w_in"] = rows_first(I["L1_attn_w_in"])
    a["w_x"] = rows_first(I["L1_attn_w_x"])
    a["w_dt"] = I["L1_attn_w_dt"]
    a["b_dt"] = I["L1_attn_b_dt"].reshape(2, P).T
    a["a_log"] = rows_first(I["L1_attn_A_log"])
    a["d_p"] = I["L1_attn_Dp"].reshape(2, P).T
    a["gw1"] = rows_first(I["L1_ffn_gate_weight"].T)
    a["e_bias"] = np.broadcast_to(I["L1_ffn_e_bias"], (P, NR1))
    sg, su, sd = (I["L1_ffn_shared_" + k] for k in ("gate", "up", "down"))
    w1 = np.concatenate([I["L1_ffn_w1"], sg.reshape(2, F1, D)], 0)
    w3 = np.concatenate([I["L1_ffn_w3"], su.reshape(2, F1, D)], 0)
    w2 = np.concatenate([I["L1_ffn_w2"], sd.reshape(D, 2, F1).transpose(1, 0, 2)], 0)

    def gated(w):
        return w.transpose(0, 2, 1).reshape(E1, 2, P, F1).transpose(0, 2, 1, 3).reshape(E1, P, 2 * F1)
    a["w1"] = np.concatenate([gated(w1), gated(w3), w2.transpose(0, 2, 1)], 2)
    a.update(shape_constants())

    nc = bacc.Bacc("TRN2", target_bir_lowering=False, num_devices=1)
    arrays, aps = {}, {}
    for name, v in a.items():
        v = np.ascontiguousarray(v)
        arrays[f"in_{name}"] = v
        aps[name] = nc.dram_tensor(f"in_{name}", v.shape, mybir.dt.from_np(v.dtype), kind="ExternalInput").ap()
    out = nc.dram_tensor("out_0", (NT, D), F32, kind="ExternalOutput").ap()
    vit_tower(nc, aps, out)
    r = run_bass_kernel_spmd(nc, [arrays], core_ids=[0])
    return np.asarray(r.results[0]["out_0"]).reshape(B, T, D)
```

```python
from contextlib import ExitStack

import numpy as np
import concourse.bass as bass
from concourse import mybir

F32 = mybir.dt.float32
BF16 = mybir.dt.bfloat16
ALU = mybir.AluOpType
ACT = mybir.ActivationFunctionType
AX = mybir.AxisListType

P = 128
B = 16
T = 37
NT = B * T
NTILE = -(-NT // P)
ROWS = [min(P, NT - P * t) for t in range(NTILE)]
NPAD = NTILE * P
HALF = NT // 2
D = 256
KP = 768 // P
LN_EPS = 1e-5
RMS_EPS = 1e-6

NH, HD, RD = 16, 16, 32
R_KV, R_Q = 64, 128
SCALE = float(HD + RD) ** -0.5
IMGS = 3
GR = IMGS * T
GROUPS = [(g * GR, min(GR, NT - g * GR)) for g in range(-(-NT // GR))]
NG = len(GROUPS)
MASKED = -1e30

SCR_ROPE = 16 * NT + NG * NH * 32 + 4 * NT + 2 * NT + 4 * P

SCR_CB = (10 + 1 + 1 + 1 + 1 + 1 + 4 + 4 + 6 + 2) * NT

E0, F0 = 9, 1024
FT0 = F0 // P
K0 = 2
SLOTS0 = 2
SHARED = SLOTS0
TS = 192
HS = TS // 2
ITEMS0 = (K0 * NT + (E0 - 1) * (TS - 1)) // TS
CHUNKS = -(-NT // TS)
assert ITEMS0 % SLOTS0 == 0

NS = 16
R_DT = 64
DT_MIN, DT_MAX = 0.001, 0.1

E1, F1 = 66, 128
NR1, NGRP, TOPG, TOPK = 64, 8, 4, 8
CAP = 256
SCALE1 = 2.5
SLOTS1 = 2
NI = 72
W1U = 2 * 2 * F1
W1C = W1U + D
REMOVED = -3e38


def vit_tower(nc, A, out):
    ctx = ExitStack()
    with ctx:
        def sb(name, shape, dt=F32):
            return ctx.enter_context(nc.sbuf_tensor(name, shape, dt))

        def sem(name):
            return ctx.enter_context(nc.semaphore(name))

        PS = ctx.enter_context(nc.psum_tensor("PS", [P, 8, 512], F32))

        h = sb("h", [P, NTILE, D])
        xn = sb("xn", [P, NTILE, D])
        xT = sb("xT", [P, 2, NPAD])
        stats = sb("stats", [P, NTILE, 6])
        mv = sb("mv", [P, NTILE, 2])
        std = sb("std", [P, NTILE])
        rstd = sb("rstd", [P, NTILE])
        ident = sb("ident", [P, P])
        identb = sb("identb", [P, P], BF16)
        onesb = sb("onesb", [P, P], BF16)
        upperb = sb("upperb", [P, P], BF16)
        maskb = sb("maskb", [GR, 4, GR], BF16)
        ones64 = sb("ones64", [R_KV, R_KV])
        before = sb("before", [P, 8, 8])
        cosT = sb("cosT", [P, T])
        sinT = sb("sinT", [P, T])
        sel = sb("sel", [3 * 32, NS, P], BF16)

        wkv = sb("wkv", [P, 2, R_KV])
        wq = sb("wq", [P, 2, R_Q])
        g_kv = sb("g_kv", [R_KV, 1])
        wo = sb("wo", [P, 4, D])
        wvdec = sb("wvdec", [R_KV, D])
        w_in = sb("w_in", [P, 2, D])
        w_x = sb("w_x", [P, 2, R_DT + 2 * NS])
        w_dt = sb("w_dt", [R_DT, D])
        b_dt = sb("b_dt", [P, 2])
        a_log = sb("a_log", [P, 2, NS])
        d_p = sb("d_p", [P, 2])
        rw0 = sb("rw0", [P, 2, 8])
        gw1 = sb("gw1", [P, 2, NR1])
        e_bias = sb("e_bias", [P, NR1])

        SCR = 22800
        scratch = sb("scratch", [P, SCR])

        def views(*shapes):
            at, out_ = 0, []
            for rows, shape in shapes:
                n = int(np.prod(shape))
                v = scratch[0:rows, at:at + n]
                if len(shape) > 1:
                    names = "abcd"[:len(shape)]
                    v = v.rearrange(f"p ({' '.join(names)}) -> p {' '.join(names)}",
                                    **{c: s for c, s in zip(names[1:], shape[1:])})
                out_.append(v)
                at += n
            assert at <= SCR, at
            return out_

        w0up = sb("w0up", [P, SLOTS0 + 1, 2, F0])
        w0dn = sb("w0dn", [P, SLOTS0 + 1, FT0, D])
        w0flat = w0up[:, :, :, :].rearrange("p s c f -> p (s c f)")
        patches = w0flat[:, 0:KP * NT].rearrange("p (k n) -> p k n", k=KP)
        wtok = w0dn[:, 0, 0:KP, :]
        rowsel = w0dn[0:T + 2, 1, 0:3, :].rearrange("p a b -> p (a b)")[:, 0:NT]
        posb = w0dn[0:T + 2, 2, 0, :]
        (qk, vpad, OT, kvn, qc, wkac, rt) = views(
            (P, (2, 4, 2, NT)), (GR, (NG, NH, 32)), (P, (4, NT)), (R_KV, (NT,)), (P, (NT,)), (R_KV, (4, P)),
            (P, (2, 4, NT)))
        rope_at = SCR_ROPE
        prob = scratch[0:GR, rope_at:rope_at + 3 * 8 * GR].rearrange("p (b h n) -> p b h n", b=3, h=8)
        probT = scratch[0:GR, rope_at + 3 * 8 * GR:rope_at + 5 * 8 * GR].rearrange("p (b h n) -> p b h n", b=2, h=8)
        keys = [v[:, 0:8 * 4 * GR].rearrange("p (m j n) -> p m j n", m=8, j=4)
                for v in (w0dn[:, 0:2].rearrange("p s f d -> p (s f d)"), w0flat)]
        kv_sb, sq, rms, rrms = (w0flat[0:R_KV, 3072 + k * NT:3072 + (k + 1) * NT] for k in range(4))
        wkar = w0flat[:, 0:1024].rearrange("p (c m n) -> p c m n", c=2, m=4)
        wkbr = w0flat[:, 1024:2048].rearrange("p (c m n) -> p c m n", c=2, m=4)
        wqa = w0flat[:, 2048:2560].rearrange("p (m n) -> p m n", m=4)
        wqb = w0flat[:, 2560:3072].rearrange("p (m n) -> p m n", m=4)
        mx = sb("mx", [GR, NH])
        rsum = sb("rsum", [GR, NH])
        (hT0, xe, xeT, yT, ysb, yg) = views((P, (FT0, NT)), (HS, (SLOTS0, 2 * D)), (P, (SLOTS0, 2, TS)), (P, (2, TS)),
                                            (HS, (SLOTS0, 2 * D)), (P, (K0, NTILE, D)))
        by_expert = nc.dram_tensor("by_expert", (ITEMS0 + SLOTS0, 2, HS, D), F32, kind="Internal").ap()
        rows_by_expert = by_expert.rearrange("i j p d -> (i j p) d")
        zeros = sb("zeros", [P, D])
        chosen0b = sb("chosen0b", [P, NTILE, 8], BF16)
        nitems = sb("nitems", [P, 8])
        upto_items = sb("upto_items", [P, 8])
        first_slot = sb("first_slot", [P, 8])
        ones8 = sb("ones8", [P, 8])
        slot_of = sb("slot_of", [P, NTILE, 8])
        slots8 = sb("slots8", [P, NTILE, 8])
        slots = sb("slots", [P, K0, NTILE], mybir.dt.uint32)
        gate_k = sb("gate_k", [P, K0, NTILE])
        item_cmp = sb("item_cmp", [1, ITEMS0 + SLOTS0, 8])
        place2 = sb("place2", [1, ITEMS0 // SLOTS0])
        item_e = sb("item_e", [1, ITEMS0 + SLOTS0])
        items = sb("items", [1, ITEMS0 + SLOTS0 + 1 + SLOTS0], mybir.dt.int32)
        BEFORE_LAST = ITEMS0 + SLOTS0 + 1
        last_first = sb("last_first", [1, 8])
        cmp_items = sb("cmp_items", [1, SLOTS0, ITEMS0 // SLOTS0])
        before_last_f = sb("before_last_f", [1, SLOTS0])
        lg0 = sb("lg0", [P, NTILE, 8])
        p0 = sb("p0", [P, NTILE, 8])
        r5 = sb("r5", [P, NTILE])
        cmp_gt = sb("cmp_gt", [P, NTILE, 8, 8])
        cmp_eq = sb("cmp_eq", [P, NTILE, 8, 8])
        rank = sb("rank", [P, NTILE, 8])
        BA = 4
        RING = 6
        (u, dt, dtu, spa, spb, bT, cT, dtl, inpT, rest, barA, hs, hc, du) = views(
            (P, (2, NT)), (P, (2, NT)), (P, (2, NT)), (P, (2, NT)), (P, (2, NT)),
            (NS, (NT,)), (NS, (NT,)), (R_DT, (NT,)), (NS, (NT,)), (96, (NT,)),
            (P, (BA, NT)), (P, (2, 2, NT)), (P, (RING, NT)), (P, (2, NT)))
        cb_sb = scratch[:, SCR_CB:SCR_CB + 2 * NT].rearrange("p (b n) -> p b n", b=2)
        inp3 = sb("inp3", [96, NT], BF16)
        c3 = sb("c3", [96, NT], BF16)
        a_neg = sb("a_neg", [P, 2, NS])
        zerosb = sb("zerosb", [P, 512], BF16)
        w1s = sb("w1s", [P, SLOTS1, W1C])
        (silu_g, hT1) = views((P, (2, HALF)), (P, (SLOTS1, NT)))
        scores = sb("scores", [P, NTILE, NR1])
        sfc = sb("sfc", [P, NTILE, NR1])
        top8g = sb("top8g", [P, NTILE * NGRP, 8])
        gscore = sb("gscore", [P, NTILE, NGRP])
        tmp = sb("tmp", [P, NTILE, NR1])
        top8 = sb("top8", [P, NTILE, 8])
        chosen = sb("chosen", [P, NTILE, NR1])
        chosenb = sb("chosenb", [P, NTILE, NR1], BF16)
        gates1 = sb("gates1", [P, NTILE, NR1 + 2])
        validb = sb("validb", [P, NTILE], BF16)
        upto = sb("upto", [NR1, NR1], BF16)
        place = sb("place", [NR1, NI])
        numbers = sb("numbers", [NR1, 3])
        active = sb("active", [NR1, 1])
        activeb = sb("activeb", [NR1, 1], BF16)
        upto_n = sb("upto_n", [NR1, 1])
        onehot = sb("onehot", [NR1, NI])
        counts = sb("counts", [1, 1])
        lists = sb("lists", [1, 2 * NI + 2], mybir.dt.int32)
        ITERS, COLS = NI, NI + 2

        patch_in = [sem(f"patch_in{k}") for k in range(KP)]
        pos_in = sem("pos_in")
        ident_in = sem("ident_in")
        attn_in = sem("attn_in")
        attn2_in = sem("attn2_in")
        route_in = sem("route_in")
        scan_in = sem("scan_in")
        embed_mm = sem("embed_mm")
        dve_step = sem("dve_step")
        act_step = sem("act_step")
        var_ready = sem("var_ready")
        std_ready = sem("std_ready")
        xn_ready = sem("xn_ready")
        xT_mm = sem("xT_mm")
        xT_lo = sem("xT_lo")
        xT_hi = sem("xT_hi")
        kv_mm, kv_ready, sq_ready, ms_mm, rms_ready, kvn_ready = (
            sem(n) for n in ("kv_mm", "kv_ready", "sq_ready", "ms_mm", "rms_ready", "kvn_ready"))
        qc_mm, qc_ready = sem("qc_mm"), sem("qc_ready")
        rope_mm, rope_read, rope_done = sem("rope_mm"), sem("rope_read"), sem("rope_done")
        v_mm, v_ready, v_ones = sem("v_mm"), sem("v_ready"), sem("v_ones")
        s_mm, s_shift, p_ready = sem("s_mm"), sem("s_shift"), sem("p_ready")
        exp_ready, sums_ready = sem("exp_ready"), sem("sums_ready")
        pt_mm, pt_ready = sem("pt_mm"), sem("pt_ready")
        pv_mm, o_ready, wo_mm = sem("pv_mm"), sem("o_ready"), sem("wo_mm")
        h_attn = sem("h_attn")
        r0_mm, r0_shift, r0_exp = sem("r0_mm"), sem("r0_shift"), sem("r0_exp")
        up_in = [sem(f"up_in{s}") for s in range(SLOTS0 + 1)]
        dn_in = [sem(f"dn_in{s}") for s in range(SLOTS0 + 1)]
        zerosb_ready = sem("zerosb_ready")
        tail_ready = sem("tail_ready")
        keys_zero, keys_act, keys_dve = sem("keys_zero"), sem("keys_act"), sem("keys_dve")
        zeros_ready, chosen0_ready, pos0_mm = (
            sem(n) for n in ("zeros_ready", "chosen0_ready", "pos0_mm"))
        items_ready, slots_ready, sorted_out = sem("items_ready"), sem("slots_ready"), sem("sorted_out")
        xe_in = [sem(f"xe_in{s}") for s in range(SLOTS0)]
        y_out = [sem(f"y_out{s}") for s in range(SLOTS0)]
        yg_in = [[sem(f"yg_in{k}_{t}") for t in range(NTILE)] for k in range(K0)]
        y_some_out, y_all_out = sem("y_some_out"), sem("y_all_out")
        xeT_mm, xeT_ready = sem("xeT_mm"), sem("xeT_ready")
        yT_ready, yback_mm = sem("yT_ready"), sem("yback_mm")
        up_mm, gelu_done, y_mm, y_taken = sem("up_mm"), sem("gelu_done"), sem("y_mm"), sem("y_taken")
        u_mm, u_ready, dtl_mm, dtl_ready = sem("u_mm"), sem("u_ready"), sem("dtl_mm"), sem("dtl_ready")
        b_mm, b_ready, c_mm, c_ready = sem("b_mm"), sem("b_ready"), sem("c_mm"), sem("c_ready")
        dt_mm, sp_abs, sp_ln, sp_max = sem("dt_mm"), sem("sp_abs"), sem("sp_ln"), sem("sp_max")
        spexp_ready = sem("spexp_ready")
        dt_ready, dtu_ready, a_exp, a_ready = sem("dt_ready"), sem("dtu_ready"), sem("a_exp"), sem("a_ready")
        c3_ready, inp3_ready = sem("c3_ready"), sem("inp3_ready")
        g_mm, inp_ready, ring_ready, du_ready = sem("g_mm"), sem("inp_ready"), sem("ring_ready"), sem("du_ready")
        barA_ready, ib_mm, cb_mm, scanned = sem("barA_ready"), sem("ib_mm"), sem("cb_mm"), sem("scanned")
        cb_ready, hcp_ready, pair_ready, pair_used = (sem(n) for n in ("cb_ready", "hcp_ready", "pair_ready", "pair_used"))
        hc_ready, hc_used, yscan_mm = sem("hc_ready"), sem("hc_used"), sem("yscan_mm")
        r1_mm, sig_ready, chosen_ready, pos_mm = sem("r1_mm"), sem("sig_ready"), sem("chosen_ready"), sem("pos_mm")
        w1up_in = [sem(f"w1up_in{s}") for s in range(SLOTS1)]
        w1dn_in = [sem(f"w1dn_in{s}") for s in range(SLOTS1)]
        count_mm, active_ready, place_mm, onehot_ready, lists_mm, lists_ready = (
            sem(n) for n in ("count_mm", "active_ready", "place_mm", "onehot_ready", "lists_mm", "lists_ready"))
        gu_mm, silu_ready, hT_ready = sem("gu_mm"), sem("silu_ready"), sem("hT_ready")
        y1_mm, y1_taken, out_done = sem("y1_mm"), sem("y1_taken"), sem("out_done")

        block = ctx.enter_context(nc.Block())

        YG = [(0, 1), (2, 3), (4,)]

        def spread_keys(copy, g, j):
            c0, rows = GROUPS[g]
            r = slice(32 * j, 32 * j + 32)
            return copy(keys[g % 2][r, :, j, 0:rows], qk[r, 1, :, :, c0:c0 + rows].rearrange("p m a n -> p (m a) n"))

        @block.sync
        def _(sp):
            for k in range(KP):
                sp.dma_start(patches[:, k, :], A["patchesT"][k]).then_inc(patch_in[k], 16)
                sp.dma_start(wtok[:, k, :], A["W_tok"][k]).then_inc(patch_in[k], 16)
            sp.dma_start(rowsel, A["rowsel"]).then_inc(pos_in, 16)
            sp.dma_start(posb, A["posb"]).then_inc(pos_in, 16)
            sp.dma_start(ident[:, :], A["ident"]).then_inc(ident_in, 16)
            for dst, name in ((wkv[:, :, :], "wkv"), (wq[:, :, :], "wq"), (g_kv[:, :], "g_kv"),
                              (ones64[:, :], "ones64"), (wkac, "wkac"), (cosT[:, :], "cosT"),
                              (sinT[:, :], "sinT"), (wvdec[:, :], "wvdec"), (wo[:, :, :], "wo"),
                              (maskb[:, :, :], "maskb"), (identb[:, :], "identb")):
                sp.dma_start(dst, A[name]).then_inc(attn_in, 16)
            sp.wait_ge(embed_mm, NTILE)
            for dst, name in ((wqa, "wqa"), (wqb, "wqb"), (wkar, "wkar"), (wkbr, "wkbr")):
                sp.dma_start(dst, A[name]).then_inc(attn2_in, 16)
            for dst, name in ((rw0[:, :, :], "rw0"), (gw1[:, :, :], "gw1"), (e_bias[:, :], "e_bias"),
                              (before[:, :, :], "before"), (onesb[:, :], "onesb"), (upperb[:, :], "upperb"),
                              (validb[:, :], "validb"), (upto[:, :], "upto"), (place[:, :], "place"),
                              (numbers[:, :], "numbers")):
                sp.dma_start(dst, A[name]).then_inc(route_in, 16)
            for dst, name in ((w_in[:, :, :], "w_in"), (w_x[:, :, :], "w_x"), (w_dt[:, :], "w_dt"),
                              (b_dt[:, :], "b_dt"), (a_log[:, :, :], "a_log"), (d_p[:, :], "d_p"),
                              (sel[:, :, :], "sel")):
                sp.dma_start(dst, A[name]).then_inc(scan_in, 16)
            sp.dma_start(w0dn[:, SHARED], A["w0dn"][0]).then_inc(dn_in[SHARED], 16)
            sp.wait_ge(rope_mm, 16)
            sp.dma_start(w0up[:, SHARED], A["w0up"][0]).then_inc(up_in[SHARED], 16)
            sp.wait_ge(zeros_ready, 1)
            part = (ITEMS0 + SLOTS0) * TS // SLOTS0
            for s in range(SLOTS0):
                sp.dma_start(rows_by_expert[s * part:(s + 1) * part].rearrange("(p r) d -> p r d", p=P),
                             zeros[:, :].unsqueeze(1).broadcast_to([P, part // P, D])).then_inc(y_out[s], 16)
            for s in range(2):
                sp.dma_start(w1s[:, s, 0:W1U], A["w1"][NR1 + s, :, 0:W1U]).then_inc(w1up_in[s], 16)
                sp.dma_start(w1s[:, s, W1U:W1C], A["w1"][NR1 + s, :, W1U:W1C]).then_inc(w1dn_in[s], 16)
            sp.wait_ge(items_ready, 1)
            iters0 = sp.value_load(items[0:1, ITEMS0 + SLOTS0:ITEMS0 + SLOTS0 + 1], min_val=2, max_val=ITEMS0 // SLOTS0)
            for s in range(SLOTS0):
                e = sp.value_load(items[0:1, s:s + 1], min_val=1, max_val=E0 - 1)
                sp.dma_start(w0up[:, s], A["w0up"][e]).then_inc(up_in[s], 16)
                sp.dma_start(w0dn[:, s], A["w0dn"][e]).then_inc(dn_in[s], 16)

            def store_item(k, s):
                sp.wait_ge(y_taken, k + (6 + 1))
                sp.dma_start(by_expert[k].rearrange("j p d -> p j d"),
                             ysb[:, s, :].rearrange("p (j d) -> p j d", j=2)).then_inc(y_out[s], 16)

            with sp.Fori(0, iters0 - 1) as i:
                for s in range(SLOTS0):
                    e = sp.value_load(items[0:1, bass.ds(i * SLOTS0 + (SLOTS0 + s), 1)], min_val=1, max_val=E0 - 1)
                    sp.wait_ge(up_mm, i * (SLOTS0 * 4) + (FT0 + (s + 1) * 4))
                    sp.dma_start(w0up[:, s], A["w0up"][e]).then_inc(up_in[s], 16)
                    sp.wait_ge(y_mm, i * (SLOTS0 * 2) + (3 + 2 * (s + 1)))
                    sp.dma_start(w0dn[:, s], A["w0dn"][e]).then_inc(dn_in[s], 16)
                    store_item(i * SLOTS0 + s, s)
            for s in range(SLOTS0):
                store_item((iters0 - 1) * SLOTS0 + s, s)
            sp.wait_ge(lists_ready, 1)
            iters = sp.value_load(lists[0:1, ITERS:ITERS + 1], min_val=2, max_val=-(-NR1 // SLOTS1))
            for s in range(SLOTS1):
                e = sp.value_load(lists[0:1, s:s + 1], min_val=0, max_val=NR1 - 1)
                sp.wait_ge(gu_mm, 2 * (s + 1))
                sp.dma_start(w1s[:, s, 0:W1U], A["w1"][e, :, 0:W1U]).then_inc(w1up_in[s], 16)
            for s in range(SLOTS1):
                e = sp.value_load(lists[0:1, s:s + 1], min_val=0, max_val=NR1 - 1)
                sp.wait_ge(y1_mm, 3 * (s + 1))
                sp.dma_start(w1s[:, s, W1U:W1C], A["w1"][e, :, W1U:W1C]).then_inc(w1dn_in[s], 16)
            with sp.Fori(0, iters - 1) as i:
                for s in range(SLOTS1):
                    e = sp.value_load(lists[0:1, bass.ds(i * SLOTS1 + (SLOTS1 + s), 1)], min_val=0, max_val=NR1 - 1)
                    sp.wait_ge(gu_mm, i * (SLOTS1 * 2) + 2 * (2 + s + 1))
                    sp.dma_start(w1s[:, s, 0:W1U], A["w1"][e, :, 0:W1U]).then_inc(w1up_in[s], 16)
                    sp.wait_ge(y1_mm, i * (SLOTS1 * 3) + 3 * (2 + s + 1))
                    sp.dma_start(w1s[:, s, W1U:W1C], A["w1"][e, :, W1U:W1C]).then_inc(w1dn_in[s], 16)
            for t in range(NTILE):
                sp.wait_ge(y1_taken, iters * (3 * SLOTS1) + (6 + t // 2 + 1))
                sp.dma_start(out[t * P:t * P + ROWS[t], :], h[0:ROWS[t], t, :]).then_inc(out_done, 16)
            sp.wait_ge(out_done, 16 * NTILE)

        @block.gpsimd
        def _(pool):
            nc.gpsimd.memset(vpad[:, :, :, HD:32], 0.0).then_inc(v_ones, 1)
            nc.gpsimd.memset(zeros[:, :], 0.0).then_inc(zeros_ready, 1)
            pool.wait_ge(embed_mm, NTILE)
            nc.gpsimd.memset(keys[0], 0.0).then_inc(keys_zero, 1)
            for idx, (which, m) in enumerate(ROPE_ORDER):
                pool.wait_ge(rope_read, 2 * idx + 2)
                r = rt[:, idx % 2]
                nc.gpsimd.tensor_tensor(qk[:, which, m, 0, :], r[:, 0, :], r[:, 1, :], ALU.subtract)
                nc.gpsimd.tensor_tensor(qk[:, which, m, 1, :], r[:, 2, :], r[:, 3, :], ALU.add).then_inc(rope_done, 1)
            for u in range(2 * NG):
                rows = GROUPS[u // 2][1]
                x = u % 2
                pool.wait_ge(sums_ready, u + 1)
                nc.gpsimd.tensor_tensor(prob[0:rows, u % 3, :, 0:rows], prob[0:rows, u % 3, :, 0:rows],
                                        rsum[0:rows, 8 * x:8 * x + 8].unsqueeze(2).broadcast_to([rows, 8, rows]),
                                        ALU.mult).then_inc(p_ready, 1)
            pool.wait_ge(items_ready, 1)
            iters0 = pool.value_load(items[0:1, ITEMS0 + SLOTS0:ITEMS0 + SLOTS0 + 1], min_val=2, max_val=ITEMS0 // SLOTS0)
            for s in range(SLOTS0):
                pool.wait_ge(y_out[s], 16)
            pool.wait_ge(slots_ready, 1)
            for t in range(NTILE):
                for k in range(K0):
                    nc.gpsimd.indirect_dma_start(
                        rows_by_expert, bass.IndirectOffsetOnAxis(ap=slots[0:ROWS[t], k, t:t + 1], axis=0),
                        xn[0:ROWS[t], t, :], None).then_inc(sorted_out, 16)
            pool.wait_ge(sorted_out, 16 * NTILE * K0)
            for s in range(SLOTS0):
                pool.dma_start(xe[:, s, :].rearrange("p (j d) -> p j d", j=2),
                               by_expert[s].rearrange("j p d -> p j d")).then_inc(xe_in[s], 16)
            pool.wait_ge(tail_ready, 1)
            before_last = [pool.value_load(items[0:1, BEFORE_LAST + s:BEFORE_LAST + s + 1], min_val=0,
                                           max_val=ITEMS0 // SLOTS0) for s in range(SLOTS0)]
            with pool.Fori(0, iters0) as i:
                for s in range(SLOTS0):
                    pool.wait_ge(xeT_mm, i * SLOTS0 + (s + 1))
                    pool.dma_start(xe[:, s, :].rearrange("p (j d) -> p j d", j=2),
                                   by_expert[i * SLOTS0 + (SLOTS0 + s)].rearrange("j p d -> p j d")).then_inc(xe_in[s], 16)
            for s in range(SLOTS0):
                pool.wait_ge(xe_in[s], iters0 * 16 + 16)

            def fetch(k):
                for t in range(NTILE):
                    nc.gpsimd.indirect_dma_start(
                        yg[0:ROWS[t], k, t, :], None, rows_by_expert,
                        bass.IndirectOffsetOnAxis(ap=slots[0:ROWS[t], k, t:t + 1], axis=0)).then_inc(yg_in[k][t], 16)

            for s in range(SLOTS0):
                pool.wait_ge(y_out[s], before_last[s] * 16 + 16)
            pool.sem_inc(y_some_out, 1)
            pool.wait_ge(y_some_out, 1)
            fetch(1)
            for s in range(SLOTS0):
                pool.wait_ge(y_out[s], iters0 * 16 + 16)
            pool.sem_inc(y_all_out, 1)
            pool.wait_ge(y_all_out, 1)
            fetch(0)

            for n in range(NS):
                pool.wait_ge(cb_ready, n + 1)
                pool.wait_ge(scanned, 2 * n + 2)
                if n >= 3:
                    if n % 2:
                        pool.wait_ge(pair_ready, (n - 1) // 2)
                    else:
                        pool.wait_ge(pair_used, (n - 2) // 2)
                nc.gpsimd.tensor_tensor(hc[:, 3 + n % 3, :], hs[:, n % 2, 1, :], cb_sb[:, n % 2, :],
                                        ALU.mult).then_inc(hcp_ready, 1)
                if n % 2:
                    pool.wait_ge(hcp_ready, n + 1)
                    nc.gpsimd.tensor_tensor(hc[:, 3 + n % 3, :], hc[:, 3 + n % 3, :], hc[:, 3 + (n - 1) % 3, :],
                                            ALU.add).then_inc(pair_ready, 1)

        @block.scalar
        def _(act):
            steps = [0]

            def link(ins):
                steps[0] += 1
                ins.then_inc(act_step, 1)
                act.wait_ge(act_step, steps[0])

            def layernorm(l):
                act.wait_ge(var_ready, l + 1)
                nc.scalar.activation(std[:, :], mv[:, :, 1], ACT.Sqrt, bias=LN_EPS).then_inc(std_ready, 1)
                act.wait_ge(xT_mm, l + 1)
                nc.scalar.copy(xT[:, 1, :], PS[:, 2:4, :].rearrange("p b n -> p (b n)")[:, 0:NPAD]).then_inc(xT_hi, 1)

            layernorm(0)
            act.wait_ge(qc_mm, 1)
            nc.scalar.copy(qc.rearrange("p (b n) -> p b n", b=2), PS[:, 2:4, 0:HALF]).then_inc(qc_ready, 1)
            act.wait_ge(kv_ready, 1)
            nc.scalar.activation(sq, kv_sb, ACT.Square).then_inc(sq_ready, 1)
            act.wait_ge(ms_mm, 1)
            nc.scalar.activation(rms.rearrange("p (b n) -> p b n", b=2), PS[0:R_KV, 4:6, 0:HALF], ACT.Sqrt,
                                 bias=RMS_EPS).then_inc(rms_ready, 1)
            def keys_of(g):
                if g >= 2:
                    act.wait_ge(s_mm, 2 * g - 2)
                spread_keys(nc.scalar.copy, g, 0)
                spread_keys(nc.scalar.copy, g, 1).then_inc(keys_act, 1)

            act.wait_ge(rope_done, 8)
            act.wait_ge(keys_zero, 1)
            keys_of(0)
            act.wait_ge(v_ones, 1)
            for i in range(NG // 2):
                act.wait_ge(v_mm, i + 1)
                rows = GR if i < NG // 2 - 1 else None
                if rows:
                    nc.scalar.copy(vpad[:, 2 * i:2 * i + 2, :, 0:HD],
                                   PS[0:GR, 4 + i, :].rearrange("p (g h d) -> p g h d", g=2, h=NH)).then_inc(v_ready, 1)
                else:
                    last = GROUPS[-1][1]
                    nc.scalar.copy(vpad[:, 2 * i, :, 0:HD],
                                   PS[0:GR, 4 + i, 0:D].rearrange("p (h d) -> p h d", h=NH))
                    nc.scalar.copy(vpad[0:last, 2 * i + 1, :, 0:HD],
                                   PS[0:last, 4 + i, D:2 * D].rearrange("p (h d) -> p h d", h=NH)).then_inc(v_ready, 1)

            def exps(u):
                rows = GROUPS[u // 2][1]
                p = prob[0:rows, u % 3, :, 0:rows]
                act.wait_ge(s_shift, u + 1)
                nc.scalar.activation(p, p, ACT.Exp, scale=SCALE).then_inc(exp_ready, 1)
                if u % 2 and u // 2 + 2 < NG:
                    keys_of(u // 2 + 2)

            act.wait_ge(keys_zero, 2)
            keys_of(1)
            exps(0)
            exps(1)
            exps(2)
            for kind, unit in SCHEDULE:
                g, x = divmod(unit, 2)
                c0, rows = GROUPS[g]
                if kind == "P":
                    if unit >= 2:
                        act.wait_ge(pv_mm, unit - 1)
                    for q in range(2):
                        k = 2 * unit + q
                        act.wait_ge(pt_mm, k + 1)
                        nc.scalar.copy(probT[0:rows, x, 4 * q:4 * q + 4, 0:rows],
                                       PS[0:rows, 4 + k % 2, 0:4 * GR].rearrange("p (c n) -> p c n", c=4)[:, :, 0:rows]).then_inc(pt_ready, 1)
                elif kind == "S":
                    exps(unit)
                elif kind == "V" and x:
                    act.wait_ge(pv_mm, unit + 1)
                    nc.scalar.copy(OT[:, :, c0:c0 + rows],
                                   PS[:, 7, 0:4 * GR].rearrange("p (m n) -> p m n", m=4)[:, :, 0:rows]).then_inc(o_ready, 1)

            layernorm(1)
            act.wait_ge(r0_shift, 1)
            nc.scalar.activation(lg0[:, :, :], lg0[:, :, :], ACT.Exp).then_inc(r0_exp, 1)
            for f in range(FT0):
                z = f % 2
                act.wait_ge(up_mm, f + 1)
                nc.scalar.activation(hT0[:, f, :].rearrange("p (b n) -> p b n", b=2),
                                     PS[:, 2 * z:2 * z + 2, 0:HALF], ACT.Gelu).then_inc(gelu_done, 1)
            act.wait_ge(items_ready, 1)
            iters0 = act.value_load(items[0:1, ITEMS0 + SLOTS0:ITEMS0 + SLOTS0 + 1], min_val=2, max_val=ITEMS0 // SLOTS0)
            with act.Fori(0, iters0) as i:
                for s in range(SLOTS0):
                    for z in range(4):
                        act.wait_ge(up_mm, i * (SLOTS0 * 4) + (FT0 + s * 4 + z + 1))
                        nc.scalar.activation(hT0[:, 2 * z:2 * z + 2, s * TS:(s + 1) * TS],
                                             PS[:, z, 0:2 * TS].rearrange("p (f n) -> p f n", f=2), ACT.Gelu).then_inc(gelu_done, 1)

            layernorm(2)
            act.wait_ge(scan_in, 7 * 16)
            nc.scalar.activation(a_neg[:, :, :], a_log[:, :, :], ACT.Exp).then_inc(a_exp, 1)
            act.wait_ge(u_mm, 2)
            nc.scalar.copy(u[:, 1, :].rearrange("p (b n) -> p b n", b=2), PS[:, 2:4, 0:HALF]).then_inc(u_ready, 1)
            act.wait_ge(dtl_mm, 1)
            nc.scalar.copy(dtl.rearrange("p (b n) -> p b n", b=2), PS[0:R_DT, 4:6, 0:HALF]).then_inc(dtl_ready, 1)
            for c in range(2):
                act.wait_ge(dt_mm, c + 1)
                nc.scalar.activation(spa[:, c, :].rearrange("p (b n) -> p b n", b=2), PS[:, 2 * c:2 * c + 2, 0:HALF], ACT.Abs,
                                     bias=b_dt[:, c:c + 1]).then_inc(sp_abs, 1)
            for c in range(2):
                act.wait_ge(sp_abs, c + 1)
                nc.scalar.activation(spa[:, c, :], spa[:, c, :], ACT.Exp, scale=-1.0).then_inc(spexp_ready, 1)
            act.wait_ge(spexp_ready, 2)
            for c in range(2):
                nc.scalar.activation(spa[:, c, :], spa[:, c, :], ACT.Ln, bias=1.0).then_inc(sp_ln, 1)
            act.wait_ge(b_mm, 1)
            nc.scalar.copy(bT.rearrange("p (b n) -> p b n", b=2), PS[0:NS, 6:8, 0:HALF]).then_inc(b_ready, 1)
            act.wait_ge(c_mm, 1)
            nc.scalar.copy(cT.rearrange("p (b n) -> p b n", b=2), PS[0:NS, 4:6, 0:HALF]).then_inc(c_ready, 1)
            act.wait_ge(a_ready, 1)
            act.wait_ge(ring_ready, 1)
            for n in range(NS):
                for c in range(2):
                    k = 2 * n + c
                    if k >= BA:
                        act.wait_ge(scanned, k - BA + 1)
                    if n == 0:
                        act.wait_ge(dt_ready, c + 1)
                    nc.scalar.activation(barA[:, k % BA, :].rearrange("p (b t) -> p b t", b=B)[:, :, 1:T],
                                         dt[:, c, :].rearrange("p (b t) -> p b t", b=B)[:, :, 1:T], ACT.Exp,
                                         scale=a_neg[:, c, n:n + 1]).then_inc(barA_ready, 1)
                act.wait_ge(cb_mm, n + 1)
                if n >= 2:
                    act.wait_ge(hc_ready, n - 1)
                    act.wait_ge(hcp_ready, n - 1)
                nc.scalar.copy(cb_sb[:, n % 2, :], PS[:, 5:7, :].rearrange("p b n -> p (b n)")[:, 0:NT]).then_inc(cb_ready, 1)

            layernorm(3)
            act.wait_ge(r1_mm, 1)
            nc.scalar.activation(scores[:, :, :].rearrange("p t e -> p (t e)"), PS[:, 7, 0:NTILE * NR1],
                                 ACT.Sigmoid).then_inc(sig_ready, 1)
            def silu_of(x):
                for n in range(2):
                    act.wait_ge(gu_mm, x * 2 + (n + 1))
                    nc.scalar.activation(silu_g[:, n, :], PS[:, 2 * n, 0:HALF], ACT.Silu).then_inc(silu_ready, 1)

            for x in range(2):
                silu_of(x)
            act.wait_ge(lists_ready, 1)
            iters = act.value_load(lists[0:1, ITERS:ITERS + 1], min_val=2, max_val=-(-NR1 // SLOTS1))
            with act.Fori(0, iters) as i:
                for s in range(SLOTS1):
                    silu_of(i * SLOTS1 + (2 + s))

        @block.vector
        def _(dve):
            steps = [0]

            def step(ins):
                steps[0] += 1
                ins.then_inc(dve_step, 1)

            def settle():
                dve.wait_ge(dve_step, steps[0])

            def link(ins):
                step(ins)
                settle()

            def layernorm(l, with_stats=False):
                for t in range(0 if with_stats else NTILE):
                    step(nc.vector.bn_stats(stats[:, t, :], h[:, t, :]))
                settle()
                for t in range(NTILE):
                    last = nc.vector.bn_aggr(mv[:, t, :], stats[:, t, :])
                last.then_inc(var_ready, 1)
                dve.wait_ge(std_ready, l + 1)
                link(nc.vector.reciprocal(rstd[:, :], std[:, :]))
                for t in range(NTILE):
                    nc.vector.tensor_scalar(xn[:, t, :], h[:, t, :], mv[:, t, 0:1], rstd[:, t:t + 1],
                                            ALU.subtract, ALU.mult).then_inc(xn_ready, 1)
                dve.wait_ge(xT_mm, l + 1)
                nc.vector.tensor_copy(xT[:, 0, :], PS[:, 0:2, :].rearrange("p b n -> p (b n)")[:, 0:NPAD]).then_inc(xT_lo, 1)

            def rank_of(score):
                sj = score.unsqueeze(2).broadcast_to([P, NTILE, 8, 8])
                se = score.unsqueeze(3).broadcast_to([P, NTILE, 8, 8])
                step(nc.vector.tensor_tensor(cmp_gt[:, :, :, :], sj, se, ALU.is_gt))
                link(nc.vector.tensor_tensor(cmp_eq[:, :, :, :], sj, se, ALU.is_equal))
                link(nc.vector.tensor_tensor(cmp_eq[:, :, :, :].rearrange("p t e j -> p t (e j)"),
                                             cmp_eq[:, :, :, :].rearrange("p t e j -> p t (e j)"),
                                             before[:, :, :].rearrange("p e j -> p (e j)").unsqueeze(1).broadcast_to([P, NTILE, 64]),
                                             ALU.mult))
                link(nc.vector.tensor_tensor(cmp_gt[:, :, :, :], cmp_gt[:, :, :, :], cmp_eq[:, :, :, :], ALU.add))
                link(nc.vector.tensor_reduce(rank[:, :, :], cmp_gt[:, :, :, :], AX.X, ALU.add))

            nc.vector.memset(zerosb[:, :], 0.0).then_inc(zerosb_ready, 1)
            step(nc.vector.memset(inp3[:, :], 0.0))
            step(nc.vector.memset(c3[:, :], 0.0))
            link(nc.vector.memset(h[:, NTILE - 1, :], 0.0))
            for t in range(NTILE):
                dve.wait_ge(embed_mm, t + 1)
                step(nc.vector.tensor_copy(h[0:ROWS[t], t, :], PS[0:ROWS[t], t, 0:D]))
            settle()

            layernorm(0)
            dve.wait_ge(kv_mm, 1)
            link(nc.vector.tensor_copy(kv_sb.rearrange("p (b n) -> p b n", b=2), PS[0:R_KV, 0:2, 0:HALF]))
            step(nc.vector.memset(mx[:, :], 0.0))
            nc.vector.memset(rsum[:, :], 0.0).then_inc(kv_ready, 1)
            dve.wait_ge(attn_in, 11 * 16)

            dve.wait_ge(rms_ready, 1)
            link(nc.vector.reciprocal(rrms, rms))
            nc.vector.scalar_tensor_tensor(kvn, kv_sb, g_kv[:, 0:1], rrms, ALU.mult, ALU.mult).then_inc(kvn_ready, 1)

            def table(tab):
                return tab[:, :].unsqueeze(1).broadcast_to([P, 8, T])

            for idx in range(8):
                b0 = 4 * (idx % 2)
                if idx >= 2:
                    dve.wait_ge(rope_done, idx - 1)
                for n in range(2):
                    dve.wait_ge(rope_mm, 2 * idx + n + 1)
                    for j, (src, tab) in enumerate(((0, cosT), (2, sinT), (2, cosT), (0, sinT))):
                        last = nc.vector.tensor_tensor(
                            rt[:, idx % 2, j, n * HALF:(n + 1) * HALF].rearrange("p (b t) -> p b t", t=T),
                            PS[:, b0 + src + n, 0:HALF].rearrange("p (b t) -> p b t", t=T), table(tab), ALU.mult)
                    last.then_inc(rope_read, 1)

            def keys_of(g):
                if g >= 2:
                    dve.wait_ge(s_mm, 2 * g - 2)
                spread_keys(nc.vector.tensor_copy, g, 2)
                spread_keys(nc.vector.tensor_copy, g, 3).then_inc(keys_dve, 1)

            nc.vector.memset(keys[1], 0.0).then_inc(keys_zero, 1)
            dve.wait_ge(rope_done, 8)
            keys_of(0)
            dve.wait_ge(keys_zero, 2)
            keys_of(1)

            def shift_scores(u):
                g, x = divmod(u, 2)
                rows = GROUPS[g][1]
                m8 = mx[0:rows, 8 * x:8 * x + 8].rearrange("p (j m) -> p j m", j=2)
                S = PS[0:rows, 2 * x:2 * x + 2, 0:4 * GR].rearrange("p j (m n) -> p j m n", m=4)[:, :, :, 0:rows]
                dve.wait_ge(s_mm, u + 1)
                link(nc.vector.tensor_reduce(m8, S, AX.X, ALU.max))
                if u >= 3:
                    dve.wait_ge(pt_mm, 2 * (u - 3) + 2)
                nc.vector.tensor_tensor(prob[0:rows, u % 3, :, 0:rows].rearrange("p (j m) n -> p j m n", j=2), S,
                                        m8.unsqueeze(3).broadcast_to([rows, 2, 4, rows]), ALU.subtract).then_inc(s_shift, 1)
                if u % 2 and u // 2 + 2 < NG:
                    keys_of(u // 2 + 2)

            def sums(u):
                rows = GROUPS[u // 2][1]
                rs = rsum[0:rows, 8 * (u % 2):8 * (u % 2) + 8]
                dve.wait_ge(exp_ready, u + 1)
                if u >= 2:
                    dve.wait_ge(p_ready, u - 1)
                link(nc.vector.tensor_reduce(rs, prob[0:rows, u % 3, :, 0:rows], AX.X, ALU.add))
                nc.vector.reciprocal(rs, rs).then_inc(sums_ready, 1)

            def add_attention(t):
                dve.wait_ge(wo_mm, t + 1)
                nc.vector.tensor_tensor(h[0:ROWS[t], t, :], PS[0:ROWS[t], 6, 0:D], h[0:ROWS[t], t, :],
                                        ALU.add).then_inc(h_attn, 1)
                dve.wait_ge(h_attn, t + 1)
                step(nc.vector.bn_stats(stats[:, t, :], h[:, t, :]))

            shift_scores(0)
            for unit in range(1, 2 * NG):
                shift_scores(unit)
                sums(unit - 1)
                if unit >= 7 and unit % 2:
                    add_attention((unit - 7) // 2)
            sums(2 * NG - 1)
            for t in range(NG - 3, NTILE):
                add_attention(t)

            layernorm(1, with_stats=True)
            dve.wait_ge(r0_mm, 1)
            logits = PS[:, 7, 0:NTILE * 8].rearrange("p (t e) -> p t e", t=NTILE)

            def over_e(v, n=8):
                return v[:, :].unsqueeze(2).broadcast_to([P, NTILE, n])

            link(nc.vector.tensor_reduce(r5[:, :], logits, AX.X, ALU.max))
            nc.vector.tensor_tensor(lg0[:, :, :], logits, over_e(r5), ALU.subtract).then_inc(r0_shift, 1)
            dve.wait_ge(r0_exp, 1)
            link(nc.vector.tensor_reduce(r5[:, :], lg0[:, :, :], AX.X, ALU.add))
            link(nc.vector.reciprocal(r5[:, :], r5[:, :]))
            link(nc.vector.tensor_tensor(p0[:, :, :], lg0[:, :, :], over_e(r5), ALU.mult))
            dve.wait_ge(route_in, 10 * 16)
            rank_of(p0[:, :, :])
            nc.vector.scalar_tensor_tensor(chosen0b[:, :, :], rank[:, :, :], float(K0), over_e(validb), ALU.is_lt,
                                           ALU.mult).then_inc(chosen0_ready, 1)
            for tiles in YG:
                a, b = tiles[0], tiles[-1] + 1
                nc.vector.tensor_tensor(h[:, a:b, :], h[:, a:b, :], xn[:, a:b, :], ALU.add).then_inc(y_taken, 1)
            step(nc.vector.memset(ones8[:, :], 1.0))
            dve.wait_ge(pos0_mm, 1)
            earlier0 = PS[:, 7, 64:64 + NTILE * 8].rearrange("p (t e) -> p t e", t=NTILE)
            tokens_of = PS[:, 7, 112:120]
            link(nc.vector.tensor_scalar(nitems[:, :], tokens_of, 0.0, None, ALU.is_gt))
            for k in range(1, CHUNKS):
                link(nc.vector.scalar_tensor_tensor(nitems[:, :], tokens_of, float(k * TS), nitems[:, :], ALU.is_gt, ALU.add))
            link(nc.vector.tensor_tensor_scan(upto_items[:, :], ones8[:, :], nitems[:, :], 0.0, ALU.mult, ALU.add))
            step(nc.vector.tensor_tensor(item_cmp[:, :, :],
                                         upto_items[0:1, :].unsqueeze(1).broadcast_to([1, ITEMS0 + SLOTS0, 8]),
                                         place[0:1, 0:ITEMS0 + SLOTS0].unsqueeze(2).broadcast_to([1, ITEMS0 + SLOTS0, 8]),
                                         ALU.is_lt))
            step(nc.vector.tensor_scalar(place2[:, :], place[0:1, 0:ITEMS0].rearrange("p (i s) -> p i s", s=SLOTS0)[:, :, 0],
                                         upto_items[0:1, 7:8], None, ALU.is_le))
            link(nc.vector.tensor_tensor(first_slot[:, :], upto_items[:, :], nitems[:, :], ALU.subtract))
            step(nc.vector.tensor_reduce(item_e[:, :], item_cmp[:, :, :], AX.X, ALU.add))
            step(nc.vector.tensor_scalar(first_slot[:, :], first_slot[:, :], float(TS), 1.0, ALU.mult, ALU.add))
            link(nc.vector.tensor_reduce(counts[:, 0:1], place2[:, :], AX.X, ALU.add))
            link(nc.vector.tensor_scalar(items[:, 0:ITEMS0 + SLOTS0], item_e[:, :], float(E0 - 2), 1.0, ALU.min, ALU.add))
            nc.vector.tensor_scalar(items[:, ITEMS0 + SLOTS0:ITEMS0 + SLOTS0 + 1], counts[:, 0:1], 2.0, None,
                                    ALU.max).then_inc(items_ready, 1)
            link(nc.vector.tensor_tensor(slot_of[:, :, :], earlier0,
                                         first_slot[:, :].unsqueeze(1).broadcast_to([P, NTILE, 8]), ALU.add))
            link(nc.vector.tensor_tensor(slot_of[:, :, :], slot_of[:, :, :], chosen0b[:, :, :], ALU.mult))
            for t in range(NTILE):
                step(nc.vector.max(slots8[:, t, :], slot_of[:, t, :]))
            settle()
            nc.vector.tensor_scalar(slots[:, :, :], slots8[:, :, 0:K0].rearrange("p t k -> p k t"), -1.0, 0.0, ALU.add,
                                    ALU.max).then_inc(slots_ready, 1)
            link(nc.vector.tensor_tensor(last_first[:, :], upto_items[0:1, :], nitems[0:1, :], ALU.subtract))
            link(nc.vector.scalar_tensor_tensor(last_first[:, :], nitems[0:1, :], 0.0, last_first[:, :], ALU.is_gt, ALU.mult))
            link(nc.vector.tensor_reduce(counts[:, 0:1], last_first[:, :], AX.X, ALU.max))
            link(nc.vector.tensor_scalar(cmp_items[:, :, :], place[0:1, 0:ITEMS0].rearrange("p (i s) -> p s i", s=SLOTS0),
                                         counts[:, 0:1], None, ALU.is_le))
            link(nc.vector.tensor_reduce(before_last_f[:, :], cmp_items[:, :, :], AX.X, ALU.add))
            nc.vector.tensor_copy(items[:, BEFORE_LAST:BEFORE_LAST + SLOTS0], before_last_f[:, :]).then_inc(tail_ready, 1)
            for k in range(K0):
                link(nc.vector.tensor_tensor(rank[:, :, :], slot_of[:, :, :],
                                             slots8[:, :, k:k + 1].broadcast_to([P, NTILE, 8]), ALU.is_equal))
                link(nc.vector.tensor_tensor(rank[:, :, :], rank[:, :, :], p0[:, :, :], ALU.mult))
                link(nc.vector.tensor_reduce(gate_k[:, k, :], rank[:, :, :], AX.X, ALU.add))
            dve.wait_ge(y_taken, 3)
            for grp, tiles in enumerate(YG):
                dve.wait_ge(y_mm, grp + 1)
                for t in tiles:
                    last = nc.vector.tensor_tensor(h[0:ROWS[t], t, :], PS[0:ROWS[t], 4 + grp, (t % 2) * D:(t % 2 + 1) * D],
                                                   h[0:ROWS[t], t, :], ALU.add)
                last.then_inc(y_taken, 1)
            iters0 = dve.value_load(items[0:1, ITEMS0 + SLOTS0:ITEMS0 + SLOTS0 + 1], min_val=2, max_val=ITEMS0 // SLOTS0)
            dve.wait_ge(xeT_mm, 1)
            nc.vector.tensor_copy(xeT[:, 0].rearrange("p c n -> p (c n)"), PS[:, 7, 0:2 * TS]).then_inc(xeT_ready, 1)
            with dve.Fori(0, iters0) as i:
                for s in range(SLOTS0):
                    for c in range(2):
                        dve.wait_ge(y_mm, i * (SLOTS0 * 2) + (3 + 2 * s + c + 1))
                        nc.vector.tensor_copy(yT[:, c, :], PS[:, 4 + c, 0:TS]).then_inc(yT_ready, 1)
                    dve.wait_ge(xeT_mm, i * SLOTS0 + (s + 2))
                    nc.vector.tensor_copy(xeT[:, 1 - s].rearrange("p c n -> p (c n)"), PS[:, 7, 0:2 * TS]).then_inc(xeT_ready, 1)
                    dve.wait_ge(y_out[s], i * 16 + 16)
                    dve.wait_ge(yback_mm, i * SLOTS0 + (s + 1))
                    nc.vector.tensor_copy(ysb[:, s, :], PS[0:HS, 6, :]).then_inc(y_taken, 1)
            dve.wait_ge(y_taken, 6)
            for k in (1, 0):
                for t in range(NTILE):
                    dve.wait_ge(yg_in[k][t], 16)
                    step(nc.vector.scalar_tensor_tensor(h[0:ROWS[t], t, :], yg[0:ROWS[t], k, t, :],
                                                        gate_k[0:ROWS[t], k, t:t + 1], h[0:ROWS[t], t, :],
                                                        ALU.mult, ALU.add))
                    settle()
                    if k == 0:
                        step(nc.vector.bn_stats(stats[:, t, :], h[:, t, :]))

            layernorm(2, with_stats=True)
            dve.wait_ge(a_exp, 1)
            nc.vector.tensor_scalar(a_neg[:, :, :], a_neg[:, :, :], -1.0, None, ALU.mult).then_inc(a_ready, 1)
            nc.vector.memset(barA.rearrange("p r (b t) -> p r b t", b=B)[:, :, :, 0:1], 0.0).then_inc(ring_ready, 1)
            dve.wait_ge(u_mm, 1)
            nc.vector.tensor_copy(u[:, 0, :].rearrange("p (b n) -> p b n", b=2), PS[:, 0:2, 0:HALF]).then_inc(u_ready, 1)

            def split3(parts, x):
                link(nc.vector.tensor_copy(parts[0:NS, :], x))
                link(nc.vector.tensor_tensor(rest[32:32 + NS, :], x, parts[0:NS, :], ALU.subtract))
                link(nc.vector.tensor_copy(parts[32:32 + NS, :], rest[32:32 + NS, :]))
                link(nc.vector.tensor_tensor(rest[64:64 + NS, :], rest[32:32 + NS, :], parts[32:32 + NS, :], ALU.subtract))
                return nc.vector.tensor_copy(parts[64:64 + NS, :], rest[64:64 + NS, :])

            for c in range(2):
                dve.wait_ge(sp_abs, c + 1)
                step(nc.vector.tensor_scalar(spb[:, c, :].rearrange("p (b n) -> p b n", b=2), PS[:, 2 * c:2 * c + 2, 0:HALF],
                                             b_dt[:, c:c + 1], 0.0, ALU.add, ALU.max))
            settle()
            nc.vector.tensor_scalar(spb, spb, DT_MAX - DT_MIN, DT_MIN, ALU.mult, ALU.add).then_inc(sp_max, 1)
            dve.wait_ge(u_ready, 2)
            for c in range(2):
                last = nc.vector.tensor_scalar(du[:, c, :], u[:, c, :], d_p[:, c:c + 1], None, ALU.mult)
            last.then_inc(du_ready, 1)
            dve.wait_ge(sp_max, 1)
            for c in range(2):
                dve.wait_ge(sp_ln, c + 1)
                nc.vector.scalar_tensor_tensor(dt[:, c, :], spa[:, c, :], DT_MAX - DT_MIN, spb[:, c, :], ALU.mult,
                                               ALU.add).then_inc(dt_ready, 1)
                dve.wait_ge(dt_ready, c + 1)
                nc.vector.tensor_tensor(dtu[:, c, :], dt[:, c, :], u[:, c, :], ALU.mult).then_inc(dtu_ready, 1)
            dve.wait_ge(c_ready, 1)
            split3(c3, cT).then_inc(c3_ready, 1)
            dve.wait_ge(g_mm, 1)
            dve.wait_ge(b_ready, 1)
            nc.vector.tensor_tensor(inpT.rearrange("p (b n) -> p b n", b=2), PS[0:NS, 6:8, 0:HALF],
                                    bT.rearrange("p (b n) -> p b n", b=2), ALU.mult).then_inc(inp_ready, 1)
            dve.wait_ge(inp_ready, 1)
            split3(inp3, inpT).then_inc(inp3_ready, 1)
            IB = PS[:, 3:5, :].rearrange("p b n -> p (b n)")[:, 0:NT]
            for n in range(NS):
                dve.wait_ge(ib_mm, n + 1)
                for c in range(2):
                    k = 2 * n + c
                    dve.wait_ge(barA_ready, k + 1)
                    if n >= 2:
                        dve.wait_ge((hc_ready, hcp_ready)[c], n - 1)
                    nc.vector.tensor_tensor_scan(hs[:, n % 2, c, :], barA[:, k % BA, :], IB, 0.0, ALU.mult, ALU.add).then_inc(scanned, 1)
                dve.wait_ge(cb_ready, n + 1)
                dve.wait_ge(scanned, 2 * n + 1)
                if n >= 3:
                    dve.wait_ge(hc_used, n - 2)
                nc.vector.tensor_tensor(hc[:, n % 3, :], hs[:, n % 2, 0, :], cb_sb[:, n % 2, :], ALU.mult).then_inc(hc_ready, 1)
            dve.wait_ge(yscan_mm, 1)
            for t in range(NTILE):
                step(nc.vector.tensor_tensor(h[0:ROWS[t], t, :], PS[0:ROWS[t], t // 2, (t % 2) * D:(t % 2 + 1) * D],
                                             h[0:ROWS[t], t, :], ALU.add))
            settle()

            layernorm(3)

            def hidden(x, slot, halves=(0, 1)):
                for n in halves:
                    dve.wait_ge(silu_ready, x * 2 + (n + 1))
                    nc.vector.tensor_tensor(hT1[:, slot, n * HALF:(n + 1) * HALF], silu_g[:, n, :], PS[:, 2 * n + 1, 0:HALF],
                                            ALU.mult).then_inc(hT_ready, 1)

            def add_output(x, gate, grps=(0, 1, 2)):
                for grp in grps:
                    tiles = YG[grp]
                    dve.wait_ge(y1_mm, x * 3 + (grp + 1))
                    dve.wait_ge(y1_taken, x * 3 + (grp + 1))
                    for t in tiles:
                        y = PS[0:ROWS[t], 4 + grp, (t % 2) * D:(t % 2 + 1) * D]
                        if gate is None:
                            last = nc.vector.tensor_tensor(h[0:ROWS[t], t, :], y, h[0:ROWS[t], t, :], ALU.add)
                        else:
                            last = nc.vector.scalar_tensor_tensor(h[0:ROWS[t], t, :], y, gate(t), h[0:ROWS[t], t, :],
                                                                  ALU.mult, ALU.add)
                    last.then_inc(y1_taken, 1)

            for grp in range(3):
                nc.vector.memset(r5[:, grp:grp + 1], 0.0).then_inc(y1_taken, 1)
            dve.wait_ge(y1_taken, 3)
            dve.wait_ge(sig_ready, 1)
            link(nc.vector.tensor_tensor(sfc[:, :, :], scores[:, :, :],
                                         e_bias[:, :].unsqueeze(1).broadcast_to([P, NTILE, NR1]), ALU.add))
            for t in range(NTILE):
                for g in range(NGRP):
                    step(nc.vector.max(top8g[:, t * NGRP + g, :], sfc[:, t, 8 * g:8 * g + 8]))
            settle()
            link(nc.vector.tensor_tensor(gscore[:, :, :].rearrange("p t g -> p (t g)"), top8g[:, :, 0], top8g[:, :, 1], ALU.add))
            rank_of(gscore[:, :, :])
            hidden(0, 0)
            link(nc.vector.tensor_scalar(gscore[:, :, :], rank[:, :, :], float(TOPG), None, ALU.is_lt))
            link(nc.vector.tensor_tensor(tmp[:, :, :].rearrange("p t (g e) -> p (t g) e", g=NGRP),
                                         sfc[:, :, :].rearrange("p t (g e) -> p (t g) e", g=NGRP),
                                         gscore[:, :, :].rearrange("p t g -> p (t g)").unsqueeze(2).broadcast_to([P, NTILE * NGRP, 8]),
                                         ALU.mult))
            for t in range(NTILE):
                step(nc.vector.max(top8[:, t, :], tmp[:, t, :]))
            settle()
            for t in range(NTILE):
                step(nc.vector.match_replace(tmp[:, t, :], top8[:, t, :], tmp[:, t, :], REMOVED))
            settle()
            link(nc.vector.tensor_scalar(chosen[:, :, :], tmp[:, :, :], REMOVED, None, ALU.is_equal))
            nc.vector.tensor_copy(chosenb[:, :, :], chosen[:, :, :]).then_inc(chosen_ready, 1)
            step(nc.vector.tensor_tensor(scores[:, :, :], scores[:, :, :], chosen[:, :, :], ALU.mult))
            dve.wait_ge(count_mm, 1)
            step(nc.vector.tensor_scalar(active[:, :], PS[0:NR1, 7, 320:321], 0.0, None, ALU.is_gt))
            nc.vector.tensor_scalar(activeb[:, :], PS[0:NR1, 7, 320:321], 0.0, None, ALU.is_gt).then_inc(active_ready, 1)
            dve.wait_ge(place_mm, 1)
            link(nc.vector.tensor_copy(upto_n[:, :], PS[0:NR1, 7, 321:322]))
            nc.vector.tensor_scalar(onehot[:, :], place[:, :], upto_n[:, 0:1], active[:, 0:1], ALU.is_equal,
                                    ALU.mult).then_inc(onehot_ready, 1)
            dve.wait_ge(lists_mm, 1)
            step(nc.vector.memset(lists[:, COLS - 1:COLS], NR1 + 1))
            step(nc.vector.tensor_copy(lists[:, 0:NI], PS[0:1, 7, 322:322 + NI]))
            step(nc.vector.tensor_copy(lists[:, COLS:COLS + NI], PS[0:1, 7, 322 + NI:322 + 2 * NI]))
            link(nc.vector.tensor_reduce(counts[:, 0:1], PS[0:1, 7, 466:466 + NI // SLOTS1], AX.X, ALU.add))
            nc.vector.tensor_scalar(lists[:, ITERS:ITERS + 1], counts[:, 0:1], 2.0, None, ALU.max).then_inc(lists_ready, 1)
            add_output(0, None)
            hidden(1, 1)
            link(nc.vector.tensor_reduce(r5[:, :], scores[:, :, :], AX.X, ALU.add))
            add_output(1, None, (0,))
            link(nc.vector.tensor_scalar(r5[:, :], r5[:, :], 1e-20, None, ALU.add))
            link(nc.vector.reciprocal(r5[:, :], r5[:, :]))
            link(nc.vector.tensor_tensor(scores[:, :, :], scores[:, :, :], over_e(r5, NR1), ALU.mult))
            link(nc.vector.tensor_scalar(scores[:, :, :], scores[:, :, :], SCALE1, None, ALU.mult))
            dve.wait_ge(pos_mm, 1)
            earlier = PS[:, 7, 0:NTILE * NR1].rearrange("p (t e) -> p t e", t=NTILE)
            step(nc.vector.memset(gates1[:, :, 0:1], 0.0))
            step(nc.vector.memset(gates1[:, :, NR1 + 1:NR1 + 2], 1.0))
            link(nc.vector.scalar_tensor_tensor(gates1[:, :, 1:NR1 + 1], earlier, float(CAP), scores[:, :, :],
                                                ALU.is_lt, ALU.mult))
            dve.wait_ge(lists_ready, 1)
            iters = dve.value_load(lists[0:1, ITERS:ITERS + 1], min_val=2, max_val=-(-NR1 // SLOTS1))
            with dve.Fori(0, iters) as i:
                for s in range(SLOTS1):
                    before_it = dve.value_load(lists[0:1, bass.ds(i * SLOTS1 + (COLS - 1 + s), 1)], min_val=0, max_val=NR1 + 1)
                    col = dve.value_load(lists[0:1, bass.ds(i * SLOTS1 + (COLS + s), 1)], min_val=0, max_val=NR1 + 1)
                    x = i * SLOTS1 + (2 + s)
                    hidden(x, s, (0,))
                    add_output(i * SLOTS1 + (1 + s), lambda t: gates1[0:ROWS[t], t, :][:, bass.ds(before_it, 1)], (1, 2))
                    hidden(x, s, (1,))
                    add_output(x, lambda t: gates1[0:ROWS[t], t, :][:, bass.ds(col, 1)], (0,))
            col = dve.value_load(lists[0:1, bass.ds(iters * SLOTS1 + (COLS - 1), 1)], min_val=0, max_val=NR1 + 1)
            add_output(iters * SLOTS1 + 1, lambda t: gates1[0:ROWS[t], t, :][:, bass.ds(col, 1)], (1, 2))

        @block.tensor
        def _(pe):
            mm = nc.tensor.matmul

            def keep_busy(bank, n):
                for _ in range(n):
                    mm(PS[:, bank, :], zerosb[:, 0:P], zerosb[:, :], start=True, stop=True)

            def transpose_xn(l):
                if l == 0:
                    pe.wait_ge(ident_in, 16)
                for t in range(NTILE):
                    pe.wait_ge(xn_ready, NTILE * l + t + 1)
                    for c in range(2):
                        last = nc.tensor.transpose(PS[:, 2 * c + t // 4, (t % 4) * P:(t % 4 + 1) * P],
                                                   xn[:, t, c * P:(c + 1) * P], ident[:, :])
                last.then_inc(xT_mm, 1)
                pe.wait_ge(xT_lo, l + 1)
                pe.wait_ge(xT_hi, l + 1)

            def half(n):
                return slice(n * HALF, (n + 1) * HALF)

            pe.wait_ge(zerosb_ready, 1)
            keep_busy(7, 7)
            for k in range(KP):
                pe.wait_ge(patch_in[k], 32)
                for t in range(NTILE):
                    mm(PS[0:ROWS[t], t, 0:D], patches[:, k, t * P:t * P + ROWS[t]], wtok[:, k, :], start=(k == 0), stop=False)
            pe.wait_ge(pos_in, 32)
            for t in range(NTILE):
                mm(PS[0:ROWS[t], t, 0:D], rowsel[:, t * P:t * P + ROWS[t]], posb, start=False, stop=True).then_inc(embed_mm, 1)

            keep_busy(7, 14)
            transpose_xn(0)
            pe.wait_ge(attn_in, 11 * 16)
            for n in range(2):
                for c in range(2):
                    last = mm(PS[0:R_KV, n, 0:HALF], wkv[:, c, :], xT[:, c, half(n)], start=c == 0, stop=c == 1)
            last.then_inc(kv_mm, 1)
            for n in range(2):
                for c in range(2):
                    last = mm(PS[:, 2 + n, 0:HALF], wq[:, c, :], xT[:, c, half(n)], start=c == 0, stop=c == 1)
            last.then_inc(qc_mm, 1)
            keep_busy(7, 6)
            pe.wait_ge(sq_ready, 1)
            for n in range(2):
                last = mm(PS[0:R_KV, 4 + n, 0:HALF], ones64[:, :], sq[:, half(n)], start=True, stop=True)
            last.then_inc(ms_mm, 1)
            pe.wait_ge(qc_ready, 1)
            pe.wait_ge(attn2_in, 4 * 16)
            for idx, (which, m) in enumerate(ROPE_ORDER):
                b0 = 4 * (idx % 2)
                if idx == 1:
                    pe.wait_ge(rms_ready, 1)
                for n in range(2):
                    if idx >= 2:
                        pe.wait_ge(rope_read, 2 * (idx - 2) + n + 1)
                    if which == 0:
                        mm(PS[:, b0 + n, 0:HALF], wqa[:, m, :], qc[:, half(n)], start=True, stop=True)
                        last = mm(PS[:, b0 + 2 + n, 0:HALF], wqb[:, m, :], qc[:, half(n)], start=True, stop=True)
                    else:
                        for c in range(2):
                            mm(PS[:, b0 + n, 0:HALF], wkar[:, c, m, :], xT[:, c, half(n)], start=c == 0, stop=False)
                        for c in range(2):
                            mm(PS[:, b0 + 2 + n, 0:HALF], wkbr[:, c, m, :], xT[:, c, half(n)], start=c == 0, stop=c == 1)
                        if m == 0 and n == 0:
                            pe.wait_ge(kvn_ready, 1)
                        last = mm(PS[:, b0 + n, 0:HALF], wkac[:, m, :], kvn[:, half(n)], start=False, stop=True)
                    last.then_inc(rope_mm, 1)
            pe.wait_ge(rope_read, 16)
            for g, (c0, rows) in enumerate(GROUPS):
                last = mm(PS[0:rows, 4 + g // 2, (g % 2) * D:(g % 2 + 1) * D], kvn[:, c0:c0 + rows], wvdec[:, :],
                          start=True, stop=True)
                if g % 2:
                    last.then_inc(v_mm, 1)
            pe.wait_ge(rope_done, 8)

            def scores_of(u):
                g, x = divmod(u, 2)
                c0, rows = GROUPS[g]
                if u >= 2:
                    pe.wait_ge(s_shift, u - 1)
                if x == 0:
                    pe.wait_ge(keys_act, g + 1)
                    pe.wait_ge(keys_dve, g + 1)
                for m in (2 * x, 2 * x + 1):
                    S = PS[0:rows, m, 0:4 * GR].rearrange("p (j n) -> p j n", j=4)[:, :, 0:rows]
                    for ab in range(2):
                        mm(S, qk[:, 0, m, ab, c0:c0 + rows], keys[g % 2][:, 2 * m + ab, :, 0:rows], start=ab == 0, stop=False)
                    last = mm(S, identb[0:rows, 0:rows], maskb[0:rows, :, 0:rows], start=False, stop=True)
                last.then_inc(s_mm, 1)

            def transpose_p(u):
                rows = GROUPS[u // 2][1]
                pe.wait_ge(p_ready, u + 1)
                for q in range(2):
                    k = 2 * u + q
                    if k >= 2:
                        pe.wait_ge(pt_ready, k - 1)
                    for y in range(4):
                        last = nc.tensor.transpose(PS[0:rows, 4 + k % 2, y * GR:y * GR + rows], prob[0:rows, u % 3, 4 * q + y, 0:rows],
                                                   ident[0:rows, 0:rows])
                    last.then_inc(pt_mm, 1)

            def times_v(u):
                g, x = divmod(u, 2)
                rows = GROUPS[g][1]
                if x == 0 and g:
                    pe.wait_ge(o_ready, g)
                pe.wait_ge(pt_ready, 2 * u + 2)
                for y in range(8):
                    m, j = 2 * x + y // 4, y % 4
                    last = mm(PS[32 * j:32 * j + 32, 7, m * GR:m * GR + rows], vpad[0:rows, g, 8 * x + y, :],
                              probT[0:rows, x, y, 0:rows], start=True, stop=True)
                last.then_inc(pv_mm, 1)

            def wait_busily(u):
                pe.wait_ge(s_shift, u + 2)
                keep_busy(0, 7)

            def project_out(t):
                pe.wait_ge(o_ready, t + 2)
                if t:
                    pe.wait_ge(h_attn, t)
                for m in range(4):
                    last = mm(PS[0:ROWS[t], 6, 0:D], OT[:, m, t * P:t * P + ROWS[t]], wo[:, m, :], start=m == 0, stop=m == 3)
                last.then_inc(wo_mm, 1)

            scores_of(0)
            scores_of(1)
            scores_of(2)
            pe.wait_ge(v_ready, 3)
            for kind, unit in SCHEDULE:
                {"P": transpose_p, "S": scores_of, "V": times_v, "O": project_out, "B": wait_busily}[kind](unit)

            keep_busy(7, 14)
            transpose_xn(1)
            pe.wait_ge(route_in, 10 * 16)
            for t in range(NTILE):
                for c in range(2):
                    last = mm(PS[:, 7, 8 * t:8 * t + 8], xT[:, c, t * P:(t + 1) * P], rw0[:, c, :], start=c == 0, stop=c == 1)
            last.then_inc(r0_mm, 1)
            pe.wait_ge(up_in[SHARED], 16)
            for f in range(FT0):
                z = f % 2
                if f >= 2:
                    pe.wait_ge(gelu_done, f - 1)
                for n in range(2):
                    for c in range(2):
                        last = mm(PS[:, 2 * z + n, 0:HALF], w0up[:, SHARED, c, f * P:(f + 1) * P], xT[:, c, half(n)],
                                  start=c == 0, stop=c == 1)
                last.then_inc(up_mm, 1)
                if f == FT0 // 2:
                    pe.wait_ge(chosen0_ready, 1)
                    for t in range(NTILE):
                        for e in range(t):
                            mm(PS[:, 7, 64 + 8 * t:72 + 8 * t], onesb[:, :], chosen0b[:, e, :], start=e == 0, stop=False)
                        mm(PS[:, 7, 64 + 8 * t:72 + 8 * t], upperb[:, :], chosen0b[:, t, :], start=t == 0, stop=True)
                    for t in range(NTILE):
                        last = mm(PS[:, 7, 112:120], onesb[:, :], chosen0b[:, t, :], start=t == 0, stop=t == NTILE - 1)
                    last.then_inc(pos0_mm, 1)
            pe.wait_ge(dn_in[SHARED], 16)
            for grp, tiles in enumerate(YG):
                pe.wait_ge(y_taken, grp + 1)
                for t in tiles:
                    for f in range(FT0):
                        if t == 0:
                            pe.wait_ge(gelu_done, f + 1)
                        last = mm(PS[0:ROWS[t], 4 + grp, (t % 2) * D:(t % 2 + 1) * D],
                                  hT0[:, f, t * P:t * P + ROWS[t]], w0dn[:, SHARED, f, :], start=f == 0, stop=f == FT0 - 1)
                last.then_inc(y_mm, 1)

            def transpose_item(s):
                for j in range(2):
                    for c in range(2):
                        last = nc.tensor.transpose(PS[:, 7, c * TS + j * HS:c * TS + (j + 1) * HS],
                                                   xe[:, s, j * D + c * P:j * D + (c + 1) * P], ident[0:HS, 0:HS])
                last.then_inc(xeT_mm, 1)

            pe.wait_ge(items_ready, 1)
            iters0 = pe.value_load(items[0:1, ITEMS0 + SLOTS0:ITEMS0 + SLOTS0 + 1], min_val=2, max_val=ITEMS0 // SLOTS0)
            pe.wait_ge(xe_in[0], 16)
            transpose_item(0)
            with pe.Fori(0, iters0) as i:
                for s in range(SLOTS0):
                    pe.wait_ge(up_in[s], i * 16 + 16)
                    pe.wait_ge(xeT_ready, i * SLOTS0 + (s + 1))
                    for z in range(4):
                        for f in (2 * z, 2 * z + 1):
                            for c in range(2):
                                last = mm(PS[:, z, (f % 2) * TS:(f % 2 + 1) * TS], w0up[:, s, c, f * P:(f + 1) * P],
                                          xeT[:, s, c, :], start=c == 0, stop=c == 1)
                        last.then_inc(up_mm, 1)
                    pe.wait_ge(dn_in[s], i * 16 + 16)
                    pe.wait_ge(y_taken, i * SLOTS0 + (6 + s))
                    for c in range(2):
                        for f in range(FT0):
                            if c == 0 and f % 2 == 0:
                                pe.wait_ge(gelu_done, i * (SLOTS0 * 4) + (FT0 + s * 4 + f // 2 + 1))
                            last = mm(PS[:, 4 + c, 0:TS], w0dn[:, s, f, c * P:(c + 1) * P], hT0[:, f, s * TS:(s + 1) * TS],
                                      start=f == 0, stop=f == FT0 - 1)
                        last.then_inc(y_mm, 1)
                    pe.wait_ge(xe_in[1 - s], i * 16 + (16 if s == 0 else 32))
                    transpose_item(1 - s)
                    for c in range(2):
                        pe.wait_ge(yT_ready, i * (SLOTS0 * 2) + (2 * s + c + 1))
                        for j in range(2):
                            last = nc.tensor.transpose(PS[0:HS, 6, j * D + c * P:j * D + (c + 1) * P],
                                                       yT[:, c, j * HS:(j + 1) * HS], ident[:, :])
                    last.then_inc(yback_mm, 1)

            pe.wait_ge(yg_in[0][0], 16)
            keep_busy(7, 14)
            transpose_xn(2)
            pe.wait_ge(scan_in, 7 * 16)
            for c in range(2):
                for n in range(2):
                    for k in range(2):
                        last = mm(PS[:, 2 * c + n, 0:HALF], w_in[:, k, c * P:(c + 1) * P], xT[:, k, half(n)], start=k == 0, stop=k == 1)
                last.then_inc(u_mm, 1)
            keep_busy(7, 4)
            pe.wait_ge(u_ready, 2)

            def project(bank, rows, w, done):
                for n in range(2):
                    for k in range(2):
                        last = mm(PS[0:rows, bank + n, 0:HALF], w_x[:, k, w:w + rows], u[:, k, half(n)], start=k == 0, stop=k == 1)
                last.then_inc(done, 1)

            project(4, R_DT, 0, dtl_mm)
            keep_busy(7, 3)
            pe.wait_ge(dtl_ready, 1)
            for c in range(2):
                for n in range(2):
                    last = mm(PS[:, 2 * c + n, 0:HALF], w_dt[:, c * P:(c + 1) * P], dtl[:, half(n)], start=True, stop=True)
                last.then_inc(dt_mm, 1)
            project(6, NS, R_DT, b_mm)
            project(4, NS, R_DT + NS, c_mm)
            pe.wait_ge(b_ready, 1)
            pe.wait_ge(a_ready, 1)
            for k in range(2):
                pe.wait_ge(dtu_ready, k + 1)
                for n in range(2):
                    last = mm(PS[0:NS, 6 + n, 0:HALF], a_neg[:, k, :], dtu[:, k, half(n)], start=k == 0, stop=k == 1)
            last.then_inc(g_mm, 1)
            for bank in range(3):
                mm(PS[:, bank, :], zerosb[:, 0:P], zerosb[:, :], start=True, stop=False, skip_group_check=True)
            pe.wait_ge(du_ready, 1)

            def add_to_y(src, c):
                for t in range(NTILE):
                    last = mm(PS[0:ROWS[t], t // 2, (t % 2) * D + c * P:(t % 2) * D + (c + 1) * P],
                              src[:, t * P:t * P + ROWS[t]], ident[:, :], start=False, stop=False, skip_group_check=True)
                return last

            def broadcast(bank, row, n, done):
                mm(PS[:, bank, 0:512], sel[:, n, :], row[:, 0:512], start=True, stop=True)
                mm(PS[:, bank + 1, 0:NT - 512], sel[:, n, :], row[:, 512:NT], start=True, stop=True).then_inc(done, 1)

            def add_products(n):
                pe.wait_ge(hc_ready, n + 1)
                add_to_y(hc[:, n % 3, :], 0).then_inc(hc_used, 1)
                if n % 2:
                    pe.wait_ge(pair_ready, (n + 1) // 2)
                    add_to_y(hc[:, 3 + n % 3, :], 1).then_inc(pair_used, 1)

            for c in range(2):
                add_to_y(du[:, c, :], c)
            pe.wait_ge(c3_ready, 1)
            pe.wait_ge(inp3_ready, 1)
            for n in range(NS):
                if n:
                    pe.wait_ge(scanned, 2 * n)
                broadcast(3, inp3, n, ib_mm)
                if n:
                    pe.wait_ge(cb_ready, n)
                broadcast(5, c3, n, cb_mm)
                if n >= 2:
                    add_products(n - 2)
            add_products(NS - 2)
            add_products(NS - 1)
            for bank in range(3):
                last = mm(PS[:, bank, :], zerosb[:, 0:P], zerosb[:, :], start=False, stop=True, skip_group_check=True)
            last.then_inc(yscan_mm, 1)

            keep_busy(7, 16)
            transpose_xn(3)
            for t in range(NTILE):
                for c in range(2):
                    last = mm(PS[:, 7, NR1 * t:NR1 * (t + 1)], xT[:, c, t * P:(t + 1) * P], gw1[:, c, :], start=c == 0, stop=c == 1)
            last.then_inc(r1_mm, 1)

            def expert_up(s, halves=(0, 1)):
                for n in halves:
                    for j in range(2):
                        for c in range(2):
                            w = (2 * j + c) * F1
                            last = mm(PS[:, 2 * n + j, 0:HALF], w1s[:, s, w:w + F1], xT[:, c, half(n)], start=c == 0, stop=c == 1)
                    last.then_inc(gu_mm, 1)

            def expert_down(s, x, grps=(0, 1, 2)):
                for grp in grps:
                    tiles = YG[grp]
                    pe.wait_ge(hT_ready, x * 2 + (1 if grp == 0 else 2))
                    pe.wait_ge(y1_taken, x * 3 + (grp + 1))
                    for t in tiles:
                        last = mm(PS[0:ROWS[t], 4 + grp, (t % 2) * D:(t % 2 + 1) * D],
                                  hT1[:, s, t * P:t * P + ROWS[t]], w1s[:, s, 4 * F1:4 * F1 + D], start=True, stop=True)
                    last.then_inc(y1_mm, 1)

            for x in range(2):
                pe.wait_ge(w1up_in[x], 16)
                pe.wait_ge(w1dn_in[x], 16)
                if x == 0:
                    expert_up(x)
                    expert_down(x, x)
                else:
                    expert_up(x, (0,))
            pe.wait_ge(chosen_ready, 1)
            for t in range(NTILE):
                last = mm(PS[0:NR1, 7, 320:321], chosenb[:, t, :], validb[:, t:t + 1], start=t == 0, stop=t == NTILE - 1)
            last.then_inc(count_mm, 1)
            pe.wait_ge(active_ready, 1)
            mm(PS[0:NR1, 7, 321:322], upto[:, :], activeb[:, :], start=True, stop=True).then_inc(place_mm, 1)
            pe.wait_ge(onehot_ready, 1)
            for k in range(2):
                mm(PS[0:1, 7, 322 + k * NI:322 + (k + 1) * NI], numbers[:, k:k + 1], onehot[:, :], start=True, stop=True)
            mm(PS[0:1, 7, 466:466 + NI // SLOTS1], numbers[:, 2:3],
               onehot[:, :].rearrange("p (i s) -> p i s", s=SLOTS1)[:, :, 0], start=True, stop=True).then_inc(lists_mm, 1)
            expert_up(1, (1,))
            expert_down(1, 1, (0,))
            pe.wait_ge(lists_ready, 1)
            for t in range(NTILE):
                for s in range(t):
                    mm(PS[:, 7, NR1 * t:NR1 * (t + 1)], onesb[:, :], chosenb[:, s, :], start=s == 0, stop=False)
                last = mm(PS[:, 7, NR1 * t:NR1 * (t + 1)], upperb[:, :], chosenb[:, t, :], start=t == 0, stop=True)
            last.then_inc(pos_mm, 1)
            iters = pe.value_load(lists[0:1, ITERS:ITERS + 1], min_val=2, max_val=-(-NR1 // SLOTS1))
            with pe.Fori(0, iters) as i:
                for s in range(SLOTS1):
                    pe.wait_ge(w1up_in[s], i * 16 + 32)
                    expert_up(s, (0,))
                    expert_down(1 - s, i * SLOTS1 + (1 + s), (1, 2))
                    expert_up(s, (1,))
                    pe.wait_ge(w1dn_in[s], i * 16 + 32)
                    expert_down(s, i * SLOTS1 + (2 + s), (0,))
            expert_down(SLOTS1 - 1, iters * SLOTS1 + 1, (1, 2))


SCHEDULE = []
for _u in range(2 * NG):
    SCHEDULE.append(("P", _u))
    if _u == 2 * NG - 3:
        SCHEDULE.append(("B", _u))
    if _u == 2 * NG - 1:
        SCHEDULE.append(("O", NTILE - 2))
    if _u + 3 < 2 * NG:
        SCHEDULE.append(("S", _u + 3))
    SCHEDULE.append(("V", _u))
    if 4 <= _u < 2 * NG - 2 and _u % 2 == 0:
        SCHEDULE.append(("O", _u // 2 - 2))
SCHEDULE.append(("O", NTILE - 1))


ROPE_ORDER = [(w, m) for m in range(4) for w in range(2)]


def shape_constants():
    bf = np.dtype("bfloat16")
    f = np.float32
    rowsel = np.zeros((T + 2, NT), f)
    n = np.arange(NT)
    rowsel[n % T, n] = 1
    rowsel[T, n] = n % T == 0
    rowsel[T + 1, n] = n % T != 0
    r = np.arange(GR)
    ok = (r[:, None] // T == r[None, :] // T) & (r[None, :] <= r[:, None])
    inv = (1.0 / 10000.0 ** (np.arange(0, RD, 2, dtype=np.float32) / RD)).astype(f)
    fr = np.outer(np.arange(T, dtype=f), inv).astype(f)
    cosT, sinT = np.ones((P, T), f), np.zeros((P, T), f)
    for j in range(4):
        cosT[32 * j + 16:32 * j + 32] = np.cos(fr).T
        sinT[32 * j + 16:32 * j + 32] = np.sin(fr).T
    sel = np.zeros((3, 32, NS, P), bf)
    sel[:, np.arange(NS), np.arange(NS)] = 1
    sel = sel.reshape(96, NS, P)
    before = np.broadcast_to(np.tril(np.ones((8, 8), f), -1), (P, 8, 8))
    valid = (np.arange(NPAD) < NT).astype(f).reshape(NTILE, P).T
    e = np.arange(NR1, dtype=f)
    return dict(validb=valid.astype(bf), upto=np.triu(np.ones((NR1, NR1), f)).astype(bf),
                place=np.ascontiguousarray(np.broadcast_to(np.arange(1, NI + 1, dtype=f), (NR1, NI))),
                numbers=np.stack([e, e + 1, np.ones(NR1, f)], 1),
                rowsel=rowsel, ident=np.eye(P, dtype=f), identb=np.eye(P, dtype=f).astype(bf),
                onesb=np.ones((P, P), bf), upperb=np.triu(np.ones((P, P), f), 1).astype(bf),
                maskb=np.ascontiguousarray(np.broadcast_to(np.where(ok, 0.0, MASKED).astype(f)[:, None, :], (GR, 4, GR))).astype(bf),
                ones64=np.full((R_KV, R_KV), 1.0 / R_KV, f), cosT=cosT, sinT=sinT, sel=sel,
                before=np.ascontiguousarray(before))


def rows_first(w, k=P):
    return w.reshape(w.shape[0] // k, k, w.shape[1]).transpose(1, 0, 2)


def head_quads(w, width, parts):
    o = np.zeros((w.shape[0], 4, 4, 32), w.dtype)
    w4 = w.reshape(w.shape[0], 4, 4, width)
    for (a, b), at in parts:
        o[:, :, :, at:at + b - a] = w4[:, :, :, a:b]
    return o.reshape(w.shape[0], 4, 128)


def kernel(**inputs):
    import concourse.bacc as bacc
    from concourse.bass_utils import run_bass_kernel_spmd

    I = {k: np.asarray(v) for k, v in inputs.items()}
    a = {}
    x = I["x"].reshape(B, 3, 6, 16, 6, 16).transpose(1, 3, 5, 0, 2, 4).reshape(768, B, 36)
    px = np.zeros((768, B, T), x.dtype)
    px[:, :, 1:] = x
    a["patchesT"] = px.reshape(KP, P, NT)
    a["W_tok"] = I["L0_tok_W"].T.reshape(KP, P, D)
    a["posb"] = np.concatenate([I["L0_tok_pos_embed"][0], I["L0_tok_cls_token"][0], I["L0_tok_b"][None]], 0)
    a["wkv"] = rows_first(I["L0_attn_W_kv"])
    a["wq"] = rows_first(I["L0_attn_W_q"])
    a["g_kv"] = I["L0_attn_g_kv"].reshape(R_KV, 1)
    wo = np.zeros((4, 32, 4, D), I["L0_attn_W_o"].dtype)
    wo[:, :HD] = I["L0_attn_W_o"].reshape(4, 4, HD, D).transpose(1, 2, 0, 3)
    a["wo"] = wo.reshape(P, 4, D)
    a["wvdec"] = I["L0_attn_W_vdec"]
    a["wkac"] = head_quads(I["L0_attn_W_kdec"], HD, [((0, 16), 0)])
    kr = I["L0_attn_W_krope"]
    a["wkar"] = head_quads(kr, RD, [((0, 16), 16)]).reshape(2, P, 4, P).transpose(1, 0, 2, 3)
    a["wkbr"] = head_quads(kr, RD, [((16, 32), 16)]).reshape(2, P, 4, P).transpose(1, 0, 2, 3)
    qr = I["L0_attn_W_qrope"]
    wqa = head_quads(I["L0_attn_W_qdec"], HD, [((0, 16), 0)]).reshape(R_Q, 4, 4, 32)
    wqa[..., 16:] = head_quads(qr, RD, [((0, 16), 16)]).reshape(R_Q, 4, 4, 32)[..., 16:]
    a["wqa"] = wqa.reshape(R_Q, 4, P)
    a["wqb"] = head_quads(qr, RD, [((16, 32), 16)])
    a["rw0"] = rows_first(I["L0_ffn_router_w"])
    up = np.concatenate([I["L0_ffn_shared_up"], I["L0_ffn_routed_up"]], 0)
    dn = np.concatenate([I["L0_ffn_shared_down"], I["L0_ffn_routed_down"]], 0)
    a["w0up"] = up.reshape(E0, 2, P, F0).transpose(0, 2, 1, 3)
    a["w0dn"] = dn.reshape(E0, FT0, P, D).transpose(0, 2, 1, 3)
    a["w_in"] = rows_first(I["L1_attn_w_in"])
    a["w_x"] = rows_first(I["L1_attn_w_x"])
    a["w_dt"] = I["L1_attn_w_dt"]
    a["b_dt"] = I["L1_attn_b_dt"].reshape(2, P).T
    a["a_log"] = rows_first(I["L1_attn_A_log"])
    a["d_p"] = I["L1_attn_Dp"].reshape(2, P).T
    a["gw1"] = rows_first(I["L1_ffn_gate_weight"].T)
    a["e_bias"] = np.broadcast_to(I["L1_ffn_e_bias"], (P, NR1))
    sg, su, sd = (I["L1_ffn_shared_" + k] for k in ("gate", "up", "down"))
    w1 = np.concatenate([I["L1_ffn_w1"], sg.reshape(2, F1, D)], 0)
    w3 = np.concatenate([I["L1_ffn_w3"], su.reshape(2, F1, D)], 0)
    w2 = np.concatenate([I["L1_ffn_w2"], sd.reshape(D, 2, F1).transpose(1, 0, 2)], 0)

    def gated(w):
        return w.transpose(0, 2, 1).reshape(E1, 2, P, F1).transpose(0, 2, 1, 3).reshape(E1, P, 2 * F1)
    a["w1"] = np.concatenate([gated(w1), gated(w3), w2.transpose(0, 2, 1)], 2)
    a.update(shape_constants())

    nc = bacc.Bacc("TRN2", target_bir_lowering=False, num_devices=1)
    arrays, aps = {}, {}
    for name, v in a.items():
        v = np.ascontiguousarray(v)
        arrays[f"in_{name}"] = v
        aps[name] = nc.dram_tensor(f"in_{name}", v.shape, mybir.dt.from_np(v.dtype), kind="ExternalInput").ap()
    out = nc.dram_tensor("out_0", (NT, D), F32, kind="ExternalOutput").ap()
    vit_tower(nc, aps, out)
    r = run_bass_kernel_spmd(nc, [arrays], core_ids=[0])
    return np.asarray(r.results[0]["out_0"]).reshape(B, T, D)
```
